# Optimizing a Trainium2 kernel written in Bass

```python
import numpy as np
import jax
import jax.numpy as jnp

def _softmax(x, axis=-1):
    return jax.nn.softmax(x, axis=axis)

def _gelu(x):
    return jax.nn.gelu(x, approximate=True)

def _silu(x):
    return jax.nn.silu(x)

def _sigmoid(x):
    return jax.nn.sigmoid(x)

def _layernorm(x, axis=-1, eps=1e-05):
    m = jnp.mean(x, axis=axis, keepdims=True)
    v = jnp.var(x, axis=axis, keepdims=True)
    return (x - m) / jnp.sqrt(v + eps)

def _scatter_add(tgt, idx, src, axis=0):
    return tgt.at[idx].add(src)

def _segment_sum(src, seg, n):
    return jax.ops.segment_sum(src, seg, n)
kernel_name = 'mk_adaln_d1_jaxref_r8_79fd5a'

def setup_inputs(seed: int=0):
    np.random.seed(seed)
    _w = jnp.asarray

    def _L0_attn_setup():
        import jax, jax.numpy as jnp
        import numpy as np
        B, S, E = (2, 256, 128)
        H, W_SIZE = (16, 128)
        D = E // H
        key = jax.random.key(seed)
        ks = jax.random.split(key, 7)
        std = 1.0 / np.sqrt(E)
        return {'x': jax.random.normal(ks[0], (B, S, E), dtype=jnp.float32), 'Wq': jax.random.normal(ks[1], (E, E), dtype=jnp.float32) * std, 'bq': jax.random.normal(ks[2], (E,), dtype=jnp.float32) * std, 'Wk': jax.random.normal(ks[3], (E, E), dtype=jnp.float32) * std, 'bk': jax.random.normal(ks[4], (E,), dtype=jnp.float32) * std, 'Wv': jax.random.normal(ks[5], (E, E), dtype=jnp.float32) * std, 'bv': jax.random.normal(ks[6], (E,), dtype=jnp.float32) * std}
    _L0_attn_in = _L0_attn_setup()

    def _L0_ffn_setup():
        import jax, jax.numpy as jnp
        import numpy as np
        D_MODEL = 128
        N_EXPERTS = 8
        TOP_K = 2
        FFN_HIDDEN = 4 * D_MODEL
        key = jax.random.key(seed)
        ks = jax.random.split(key, 6)

        def xavier(k, shape):
            fan_in, fan_out = (shape[-2], shape[-1])
            lim = jnp.sqrt(6.0 / (fan_in + fan_out))
            return jax.random.uniform(k, shape, jnp.float32, -lim, lim)
        x = jax.random.normal(ks[0], (4, 256, D_MODEL), jnp.float32)
        w_gate = xavier(ks[1], (N_EXPERTS, D_MODEL))
        W1 = xavier(ks[2], (N_EXPERTS, D_MODEL, FFN_HIDDEN))
        b1 = jnp.zeros((N_EXPERTS, FFN_HIDDEN), jnp.float32)
        W2 = xavier(ks[3], (N_EXPERTS, FFN_HIDDEN, D_MODEL))
        b2 = jnp.zeros((N_EXPERTS, D_MODEL), jnp.float32)
        return {'x': x, 'w_gate': w_gate, 'W1': W1, 'b1': b1, 'W2': W2, 'b2': b2}
    _L0_ffn_in = _L0_ffn_setup()
    _L0_c = _w((lambda *s: np.random.randn(*s).astype(np.float32) * 0.05)(32, 128))
    _L0_wmod = _w((lambda *s: np.random.randn(*s).astype(np.float32) * 0.05)(128, 6 * 128) * 128 ** (-0.5))
    _d = {'L0_attn_x': _L0_attn_in['x'], 'L0_attn_Wq': _L0_attn_in['Wq'], 'L0_attn_bq': _L0_attn_in['bq'], 'L0_attn_Wk': _L0_attn_in['Wk'], 'L0_attn_bk': _L0_attn_in['bk'], 'L0_attn_Wv': _L0_attn_in['Wv'], 'L0_attn_bv': _L0_attn_in['bv'], 'L0_ffn_w_gate': _L0_ffn_in['w_gate'], 'L0_ffn_W1': _L0_ffn_in['W1'], 'L0_ffn_b1': _L0_ffn_in['b1'], 'L0_ffn_W2': _L0_ffn_in['W2'], 'L0_ffn_b2': _L0_ffn_in['b2'], 'L0_c': _L0_c, 'L0_wmod': _L0_wmod}
    _x0 = _d['L0_attn_x']
    _d['L0_attn_x'] = jax.random.normal(jax.random.fold_in(jax.random.key(seed), 1), (32, 256, 128), dtype=_x0.dtype)
    del _x0
    return _d

def reference(L0_attn_x, L0_attn_Wq, L0_attn_bq, L0_attn_Wk, L0_attn_bk, L0_attn_Wv, L0_attn_bv, L0_ffn_w_gate, L0_ffn_W1, L0_ffn_b1, L0_ffn_W2, L0_ffn_b2, L0_c, L0_wmod):

    def _L0_attn_ref(x, Wq, bq, Wk, bk, Wv, bv):
        import jax, jax.numpy as jnp
        import numpy as np
        B, S, E = (2, 256, 128)
        H, W_SIZE = (16, 128)
        D = E // H
        b, s, e = x.shape
        scale = jnp.float32(D) ** (-0.5)
        q = (x @ Wq.T + bq).reshape(b, H, s, D)
        k = (x @ Wk.T + bk).reshape(b, H, s, D)
        v = (x @ Wv.T + bv).reshape(b, H, s, D)
        i = jnp.arange(s)[:, None]
        j = jnp.arange(s)[None, :]
        mask = (j >= i - W_SIZE) & (j < i + W_SIZE)
        qk = jnp.einsum('bhid,bhjd->bhij', q, k)
        scores = jnp.where(mask, qk, 0.0) * scale
        probs = jax.nn.softmax(scores, axis=-1)
        out = jnp.einsum('bhij,bhjd->bhid', probs, v)
        out = out.transpose(0, 2, 1, 3).reshape(b, s, e)
        return out

    def _L0_ffn_ref(x, w_gate, W1, b1, W2, b2):
        import jax, jax.numpy as jnp
        import numpy as np
        D_MODEL = 128
        N_EXPERTS = 8
        TOP_K = 2
        FFN_HIDDEN = 4 * D_MODEL
        B, S, D = x.shape
        flat_x = x.reshape(-1, D)
        gate = jax.nn.softmax(flat_x @ w_gate.T, axis=-1)
        topk_scores, topk_idx = jax.lax.top_k(gate, TOP_K)
        cw = (jax.nn.one_hot(topk_idx, N_EXPERTS, dtype=flat_x.dtype) * topk_scores[..., None]).sum(axis=1)
        h = jax.nn.gelu(jnp.einsum('td,edh->teh', flat_x, W1) + b1, approximate=False)
        y = jnp.einsum('teh,ehd->ted', h, W2) + b2
        out = jnp.einsum('ted,te->td', y, cw)
        return out.reshape(B, S, D)
    x = L0_attn_x
    mod = (_silu(L0_c) @ L0_wmod).reshape(L0_c.shape[0], 6, 1, -1)
    sa, ca, ga, sb, cb, gb = (mod[:, 0], mod[:, 1], mod[:, 2], mod[:, 3], mod[:, 4], mod[:, 5])
    ga = (2 * (ga >= 0) - 1) * jnp.maximum(jnp.abs(ga), 0.25)
    gb = (2 * (gb >= 0) - 1) * jnp.maximum(jnp.abs(gb), 0.25)
    h = _layernorm(x, axis=-1) * (1 + ca) + sa
    x = x + ga * _L0_attn_ref(h, L0_attn_Wq, L0_attn_bq, L0_attn_Wk, L0_attn_bk, L0_attn_Wv, L0_attn_bv)
    h = _layernorm(x, axis=-1) * (1 + cb) + sb
    x = x + gb * _L0_ffn_ref(h, L0_ffn_w_gate, L0_ffn_W1, L0_ffn_b1, L0_ffn_W2, L0_ffn_b2)
    return x

_drawn_inputs = setup_inputs


def setup_inputs(seed=0):
    import zlib

    import numpy as np

    out = dict(_drawn_inputs(seed))
    spreads = {'L0_ffn_b1': (0.0, 0.764), 'L0_ffn_b2': (0.0, 0.611)}
    factors = {'L0_attn_bq': 8.0, 'L0_attn_bk': 8.0, 'L0_attn_bv': 8.0}
    for name, (base, spread) in spreads.items():
        noise = np.random.default_rng([zlib.crc32(name.encode()), seed]).standard_normal(out[name].shape)
        drawn = base * np.exp(spread * noise) if base else spread * noise
        out[name] = jnp.asarray(drawn.astype(out[name].dtype))
    for name, factor in factors.items():
        out[name] = (out[name] * factor).astype(out[name].dtype)
    return out
```

```python
from contextlib import ExitStack

import concourse.bass as bass
from concourse import mybir

P = 128
F32 = mybir.dt.float32
F32R = mybir.dt.float32r
BF16 = mybir.dt.bfloat16
I32 = mybir.dt.int32
ALU = mybir.AluOpType
ACT = mybir.ActivationFunctionType
AX_X = mybir.AxisListType.X

NB, S, E = 32, 256, 128
H, D = 16, 8
TOK = NB * S
WINDOW = 128
NBLK = S // WINDOW
HG = 4
GB = H // HG
CB = 2
CG = CB * GB
CT = CB * S
NT = CT // P
CHUNKS = NB // CB
GROUPS = CHUNKS * CG
R = S // H
C = S // R
CQ = C // 4
BODY = 2 * CG
BODIES = GROUPS // BODY
LAG = 10
SLOT = 32
SHIFT = 3 * D
NV = D + 1
EPS = 1e-5
MASKED = -1.0e30
U32 = mybir.dt.uint32
NE, TOPK = 8, 2
HID = 512
HC = HID // P
EXP = 2 * HID + HC + E
ROW = E + 2
TR = 256
REGION = TOK + TR
STEPS = -(-(TOPK * TOK + NE * (TR - 1)) // (4 * TR)) * 4
SU = 4
TAB_STEPS = 18
DVE_BIAS, DVE_SILU, DVE_WEIGHTS, DVE_MOD = 9, 21, 31, 51


def after(eng, sem, count):
    if not isinstance(count, int) or count > 0:
        eng.wait_ge(sem, count)


def live(i, n):
    return not isinstance(i, int) or 0 <= i < n


def over_groups(eng, slot):
    for g in range(BODY):
        slot(0, g)
    with eng.Fori(1, BODIES - 1) as it:
        for g in range(BODY):
            slot(it, g)
    for g in range(BODY):
        slot(BODIES - 1, g)
    for g in range(LAG):
        slot(BODIES, g)


NEWTON = 4
RSTD_STEPS = 3 + 3 * NEWTON


def rsqrt(dve, sem, done, out, var, half, tmp):
    dve.tensor_scalar(half, var, EPS, None, ALU.add).then_inc(sem, 1)
    dve.wait_ge(sem, done + 1)
    dve.tensor_scalar(out.bitcast(I32), half.bitcast(I32), 1, None, ALU.logical_shift_right).then_inc(sem, 1)
    dve.wait_ge(sem, done + 2)
    dve.tensor_scalar(out.bitcast(I32), out.bitcast(I32), -1.0, float(0x5F3759DF), ALU.mult, ALU.add).then_inc(sem, 1)
    for n in range(3, RSTD_STEPS, 3):
        dve.wait_ge(sem, done + n)
        dve.tensor_tensor(tmp, out, out, ALU.mult).then_inc(sem, 1)
        dve.wait_ge(sem, done + n + 1)
        dve.scalar_tensor_tensor(out=tmp, in0=tmp, scalar=0.5, in1=half, op0=ALU.mult, op1=ALU.mult).then_inc(sem, 1)
        dve.wait_ge(sem, done + n + 2)
        dve.scalar_tensor_tensor(out=out, in0=tmp, scalar=-1.5, in1=out, op0=ALU.add, op1=ALU.mult).then_inc(sem, 1)


def over_steps(eng, step):
    bodies = STEPS // SU
    for u in range(SU):
        step(0, u)
    with eng.Fori(1, bodies - 1) as it:
        for u in range(SU):
            step(it, u)
    for u in range(SU):
        step(bodies - 1, u)
    step(bodies, 0)


def build(nc, x, wq, bq, wk, bk, wv, bv, w_gate, w1, b1, w2, b2, cond, wmod, out):
    with ExitStack() as ctx:
        def sb(name, shape, dt=F32):
            return ctx.enter_context(nc.sbuf_tensor(name, shape, dt))

        def passing(scope, name, shape, dt=F32):
            return scope.enter_context(nc.sbuf_tensor(name, shape, dt))

        def psum(name):
            return ctx.enter_context(nc.psum_tensor(name, [P, 512], F32))

        def sem(name):
            return ctx.enter_context(nc.semaphore(name))

        def dram(name, shape):
            return nc.dram_tensor(name, shape, F32, kind="Internal").ap()

        mod_rows = dram("mod_rows", [NB, 6, E])
        v_rows = dram("v_rows", [CHUNKS, CT, E])
        x_mid = dram("x_mid", [NB, S, E])

        x_expert = dram("x_expert", [NE * REGION, ROW])
        y_token = dram("y_token", [TOPK * TOK + TR, E])

        pS1 = [psum("pS1a"), psum("pS1b")]
        pS2 = [psum("pS2a"), psum("pS2b")]
        pO = psum("pO")
        pP = [psum("pPa"), psum("pPb")]
        pB = psum("pB")

        ident = sb("ident", [P, P])
        identb = sb("identb", [P, P], BF16)
        neg = sb("neg", [P, NBLK, P], BF16)
        tri = sb("tri", [P, NBLK, P])
        nfloor = sb("nfloor", [P, NBLK])
        row_id = sb("row_id", [P, 1], I32)
        row_bits = sb("row_bits", [P, 1], I32)
        low_mask = sb("low_mask", [P, 2])
        quad = sb("quad", [P, 1])
        bias_ind = sb("bias_ind", [P, 4, P], BF16)

        w_slot = sb("w_slot", [P, 2, C, SLOT])
        wvT = sb("wvT", [P, E])
        experts = sb("experts", [P, NE, EXP])
        bias_rep = experts[0:1, :, :].rearrange("o x n -> o (x n)")[:, 0:24 * 256].bitcast(BF16).rearrange(
            "o (r m) -> o r m", m=512)
        bias_lhs = sb("bias_lhs", [P, 2, CQ, P], BF16)
        bv_all = sb("bv_all", [P, E])
        scaleT = sb("scaleT", [P, 2, NB])
        shiftT = sb("shiftT", [P, 2, NB])

        x_in = sb("x_in", [P, 2, NT, E])
        stats = sb("stats", [P, NT, 6])
        mean_var = sb("mean_var", [P, NT, 2])
        rstd = sb("rstd", [P, NT])
        half_var = sb("half_var", [P, NT])
        r_tmp = sb("r_tmp", [P, NT])
        xn = sb("xn", [P, NT, E])
        hT = sb("hT", [P, CT])
        rounded = sb("rounded", [P, 2, 4, P], F32R)
        q_pack = sb("q_pack", [P, CG, S], F32R)
        k_pack = sb("k_pack", [P, 2, CG, S], F32R)
        v_tok = sb("v_tok", [P, NT, E])
        v_slot = sb("v_slot", [P, 2, NBLK, CG, HG, SLOT])
        row_max = sb("row_max", [P, 2, HG, NBLK])
        nshift = sb("nshift", [P, 4, GB, HG, NBLK], F32R)
        nshiftT = sb("nshiftT", [HG * NBLK, 2, P], F32R)
        with ExitStack() as setup:
            w_nat = passing(setup, "w_nat", [P, 3, E])
            bias_row = passing(setup, "bias_row", [1, 2, E])
            bias_rest = passing(setup, "bias_rest", [1, 2, E])
            bias_part = passing(setup, "bias_part", [1, 3, 2, E], BF16)
            c_in = passing(setup, "c_in", [P, E])
            c_exp = passing(setup, "c_exp", [P, E])
            siluT = passing(setup, "siluT", [P, NB])
            wmod_sb = passing(setup, "wmod_sb", [P, 6, E])
            mod_sb = passing(setup, "mod_sb", [NB, 6, E])
            gate_sign = passing(setup, "gate_sign", [NB, 2, E])
        probs = sb("probs", [P, 2, HG, NBLK * S])
        oT = sb("oT", [P, 2, S])
        o_rows = sb("o_rows", [P, 2, NBLK, H, NV])
        o_mask = sb("o_mask", [P, 2, NBLK, H, NV])
        o_tmp = sb("o_tmp", [P, NBLK, H, NV])
        e_arg = sb("e_arg", [P, 2, H * NBLK])
        e_shift = sb("e_shift", [P, 2, H * NBLK])
        rden = sb("rden", [P, 2, NBLK, H])
        x_res = sb("x_res", [P, 2, NBLK, E])
        ga_all = sb("ga_all", [P, 2, E])
        o_att = sb("o_att", [P, NBLK, E])
        x_new = sb("x_new", [P, 2, NBLK, E])

        cs_all = sb("cs_all", [P, 2, E])
        stats2 = sb("stats2", [P, NBLK, 6])
        mean_var2 = sb("mean_var2", [P, NBLK, 2])
        rstd2 = sb("rstd2", [P, NBLK])
        half_var2 = sb("half_var2", [P, NBLK])
        r_tmp2 = sb("r_tmp2", [P, NBLK])
        h2f = sb("h2f", [P, NBLK, E])
        h2_rows = sb("h2_rows", [P, TOPK, NBLK, ROW])
        token_id = sb("token_id", [P, TOPK, NBLK])
        h2T = sb("h2T", [P, S])
        wgT = sb("wgT", [P, NE])
        logits = sb("logits", [P, NBLK, NE])
        top = sb("top", [P, NBLK, NE])
        top_at = sb("top_at", [P, NBLK, NE], U32)
        top_atf = sb("top_atf", [P, NBLK, TOPK])
        top_arg = sb("top_arg", [P, NBLK, NE])
        top_exp = sb("top_exp", [P, NBLK, NE])
        chosen = sb("chosen", [P, NBLK, TOPK, NE])
        chosen_b = sb("chosen_b", [P, NBLK, NE], BF16)
        expert_id = sb("expert_id", [P, NE])
        expert_idi = sb("expert_idi", [P, NE], I32)
        next_row = sb("next_row", [P, NE])
        place = sb("place", [P, NBLK, NE])
        place_of = sb("place_of", [P, NBLK, TOPK, NE])
        row_f = sb("row_f", [P, NBLK, TOPK])
        row_i = sb("row_i", [P, NBLK, TOPK], I32)
        gate_sum = sb("gate_sum", [P, NBLK])
        gate_inv = sb("gate_inv", [P, NBLK])
        before_b = sb("before_b", [P, P], BF16)
        ones_b = sb("ones_b", [P, P], BF16)
        pad_rows = sb("pad_rows", [P, NBLK, ROW])
        pad_idi = sb("pad_idi", [P, NBLK], I32)
        pad_id = sb("pad_id", [P, NBLK])
        ones_row = sb("ones_row", [1, NE])
        step_idi = sb("step_idi", [1, STEPS], I32)
        step_id = sb("step_id", [1, STEPS])
        b1_rows = sb("b1_rows", [NE * HC, P])
        wg_rows = sb("wg_rows", [NE, E])

        with ExitStack() as attention:
            q_diag = passing(attention, "q_diag", [P, 2, CG, HG, S], F32R)
        pad_f = sb("pad_f", [P, NE, NBLK])
        pad_i = sb("pad_i", [P, NE, NBLK], I32)
        count_f = sb("count_f", [1, NE])
        tiles_i = sb("tiles_i", [1, NE], I32)
        tiles = sb("tiles", [1, NE])
        tiles_sum = sb("tiles_sum", [1, NE])
        past = sb("past", [1, STEPS, NE - 1])
        past_n = sb("past_n", [1, STEPS, NE - 1])
        step_expert = sb("step_expert", [1, STEPS])
        step_base = sb("step_base", [1, STEPS])
        step_lim = sb("step_lim", [1, STEPS])
        last_tile = sb("last_tile", [1, 1])
        step_row = sb("step_row", [1, STEPS])
        table = sb("table", [1, 2, STEPS], I32)
        w_ring = sb("w_ring", [P, SU, EXP])
        xs = sb("xs", [P, SU, NBLK, ROW])
        hidT = sb("hidT", [P, 2, HC, TR])
        xsT = sb("xsT", [P, 2, TR])
        dest = sb("dest", [P, SU, NBLK], I32)
        y_sum = sb("y_sum", [P, 2, NBLK, E])
        y_out = sb("y_out", [P, 2, NBLK, E])
        fin_y = sb("fin_y", [P, 2, TOPK, NT, E])
        fin_x = sb("fin_x", [P, 2, NT, E])
        fin_gb = sb("fin_gb", [P, 2, CB, E])

        s_ld = sem("s_ld")
        s_pool0 = sem("s_pool0")
        s_dve0 = sem("s_dve0")
        s_act0 = sem("s_act0")
        s_pe0 = sem("s_pe0")
        s_biasl = sem("s_biasl")
        s_mod = sem("s_mod")
        s_x = [sem("s_x0"), sem("s_x1")]
        s_stats = sem("s_stats")
        s_aggr = sem("s_aggr")
        s_rstd = sem("s_rstd")
        s_xn = sem("s_xn")
        s_pA = sem("s_pA")
        s_pB = sem("s_pB")
        s_hT = sem("s_hT")
        s_rq = sem("s_rq")
        s_rk = sem("s_rk")
        s_q = sem("s_q")
        s_k = sem("s_k")
        s_v = sem("s_v")
        s_vst = sem("s_vst")
        s_vr = sem("s_vr")
        s_qb = sem("s_qb")
        s_s1 = sem("s_s1")
        s_red = sem("s_red")
        s_nm = sem("s_nm")
        s_tm = sem("s_tm")
        s_tmcp = sem("s_tmcp")
        s_m = [sem("s_m0"), sem("s_m1")]
        s_s2 = sem("s_s2")
        s_exp = sem("s_exp")
        s_aff = sem("s_aff")
        s_pv = sem("s_pv")
        s_ot = sem("s_ot")
        s_to = sem("s_to")
        s_tocp = sem("s_tocp")
        s_mk = sem("s_mk")
        s_mkcp = sem("s_mkcp")
        s_earg = sem("s_earg")
        s_e = sem("s_e")
        s_f1 = sem("s_f1")
        s_f2 = sem("s_f2")
        s_den = sem("s_den")
        s_f3 = sem("s_f3")
        s_f4 = sem("s_f4")
        s_fin = sem("s_fin")
        s_xr = [sem("s_xr0"), sem("s_xr1")]
        s_st = [sem("s_st0"), sem("s_st1")]

        s_ldx = sem("s_ldx")
        s_cs = sem("s_cs")
        s_stats2 = sem("s_stats2")
        s_aggr2 = sem("s_aggr2")
        s_rstd2 = sem("s_rstd2")
        s_n2 = sem("s_n2")
        s_m2 = sem("s_m2")
        s_h2 = sem("s_h2")
        s_id = sem("s_id")
        s_dup = sem("s_dup")
        s_h2t = sem("s_h2t")
        s_h2c = sem("s_h2c")
        s_lg = sem("s_lg")
        s_lgc = sem("s_lgc")
        s_mx = sem("s_mx")
        s_ix = sem("s_ix")
        s_ein = sem("s_ein")
        s_ixf = sem("s_ixf")
        s_oh = sem("s_oh")
        s_ch = sem("s_ch")
        s_pre = sem("s_pre")
        s_pos = sem("s_pos")
        s_prod = sem("s_prod")
        s_rowf = sem("s_rowf")
        s_row = sem("s_row")
        s_eg = sem("s_eg")
        s_gsum = sem("s_gsum")
        s_ginv = sem("s_ginv")
        s_gate = sem("s_gate")
        s_sc = sem("s_sc")
        s_tab = sem("s_tab")
        s_padc = sem("s_padc")
        s_pad = sem("s_pad")
        s_xs = [sem(f"s_xs{u}") for u in range(SU)]
        s_w = sem("s_w")
        s_xt = sem("s_xt")
        s_xtc = sem("s_xtc")
        s_hid = sem("s_hid")
        s_gelu = sem("s_gelu")
        s_y = sem("s_y")
        s_ysum = sem("s_ysum")
        s_dest = sem("s_dest")
        s_yout = sem("s_yout")
        s_ysc = sem("s_ysc")
        s_fl = [sem("s_fl0"), sem("s_fl1")]
        s_fa = sem("s_fa")
        s_fb = sem("s_fb")
        s_fc = sem("s_fc")
        s_fs = [sem("s_fs0"), sem("s_fs1")]

        NLD = 8

        def hid_bank(r, c):
            bank = (pS1, pS2)[r][c // 2]
            return bank[:, (c % 2) * TR:(c % 2 + 1) * TR]

        def apart(eng, sem, count):
            if not isinstance(count, int):
                count = eng.to_reg(count)
                eng.wait_ge(s_ld, 16 * NLD)
            after(eng, sem, count)

        block = ctx.enter_context(nc.Block())

        x_tok = x.rearrange("b (k p) e -> b p k e", p=P)
        out_tok = out.rearrange("b (k p) e -> b p k e", p=P)
        x_mid_tok = x_mid.rearrange("b (k p) e -> b p k e", p=P)

        def rows_of(ap, i, n=1):
            return ap[bass.ds(i, n)]

        @block.sync
        def _(sp):
            for n, w in enumerate((wq, wk, wv)):
                sp.dma_start(w_nat[:, n, :], w).then_inc(s_ld, 16)
            for n, b in enumerate((bq, bk)):
                sp.dma_start(bias_row[0:1, n, :], b.rearrange("(o e) -> o e", o=1)).then_inc(s_ld, 16)
            sp.dma_start(bv_all[:, :], bv.rearrange("(o e) -> o e", o=1).to_broadcast([P, E])).then_inc(s_ld, 16)
            sp.wait_ge(s_pool0, 1)
            sp.dma_start(c_in[0:NB, :], cond).then_inc(s_ld, 16)
            sp.dma_start(wmod_sb[:, :, :], wmod.rearrange("k (m e) -> k m e", m=6)).then_inc(s_ld, 16)

            def load_x_at(t, par):
                apart(sp, s_xn, NT * (t - 1))
                sp.dma_start(x_in[:, par, :, :].rearrange("p (b k) e -> p b k e", b=CB),
                             rows_of(x_tok, CB * t, CB).rearrange("b p k e -> p b k e")).then_inc(s_x[par], 16)

            load_x_at(0, 0)
            load_x_at(1, 1)
            sp.wait_ge(s_pool0, 2)
            sp.wait_ge(s_dve0, DVE_BIAS)
            sp.dma_start(bias_lhs[0:12, :, :, :].rearrange("r n c m -> r n (c m)"),
                         bias_rep.rearrange("o (r n) m -> o r n m", n=2)).then_inc(s_biasl, 16)
            sp.wait_ge(s_biasl, 16)
            sp.dma_start(experts[:, :, 0:HID], w1.rearrange("x p n -> p x n")).then_inc(s_ldx, 16)
            for e in range(NE):
                sp.dma_start(experts[:, e, HID + HC:2 * HID + HC].rearrange("p (c d) -> p c d", c=HC),
                             w2[e].rearrange("(c p) d -> p c d", p=P)).then_inc(s_ldx, 16)
            sp.dma_start(experts[:, :, 2 * HID + HC:EXP],
                         b2.rearrange("(o x) d -> o x d", o=1).broadcast_to([P, NE, E])).then_inc(s_ldx, 16)
            sp.dma_start(b1_rows[:, :], b1.rearrange("x (c p) -> (x c) p", p=P)).then_inc(s_ldx, 16)
            sp.dma_start(wg_rows[:, :], w_gate).then_inc(s_ldx, 16)
            sp.wait_ge(s_dve0, DVE_MOD)
            sp.dma_start(mod_rows, mod_sb[:, :, :]).then_inc(s_mod, 16)
            sp.wait_ge(s_mod, 16)

            def store_v(u):
                apart(sp, s_v, u + 1)
                sp.dma_start(rows_of(v_rows, u).rearrange("o (a p) e -> p (o a) e", p=P),
                             v_tok[:, :, :]).then_inc(s_vst, 16)

            def load_v(u, par):
                apart(sp, s_pv, CG * (u - 1))
                apart(sp, s_mk, CB * (u - 1))
                apart(sp, s_vst, 16 * (u + 1))
                heads = rows_of(v_rows, u).rearrange("o t e -> (o t e)").rearrange(
                    "(h k p d) -> k p h d", k=NBLK, p=P, d=D)
                for k in range(NBLK):
                    sp.dma_start(v_slot[:, par, k, :, :, 0:D].rearrange("p g h d -> p (g h) d"),
                                 heads[k]).then_inc(s_vr, 16)

            def spread_q(u, par):
                apart(sp, s_q, CQ * (u + 1))
                apart(sp, s_s2, CG * HG * (u - 1))
                for h in range(HG):
                    rows = slice(SLOT * h, SLOT * h + SLOT)
                    sp.dma_start(q_diag[rows, par, :, h, :].bitcast(F32),
                                 q_pack[rows, :, :].bitcast(F32)).then_inc(s_qb, 16)

            store_v(0)
            load_v(0, 0)
            sp.wait_ge(s_pool0, 3)
            spread_q(0, 0)

            def slot(it, g):
                G, T, s = BODY * it + g, 2 * it + g // CG, g % CG
                par = (g // CG) % 2
                if s == 2 and live(T + 2, CHUNKS):
                    load_x_at(T + 2, par)
                if live(G - 1, GROUPS):
                    apart(sp, s_tmcp, G)
                    gp = (g - 1) % BODY
                    for h in range(HG):
                        row = SLOT * h + SHIFT
                        sp.dma_start(
                            q_diag[row:row + 1, gp // CG, gp % CG, h, :].bitcast(F32).rearrange("o (k i) -> o k i", k=NBLK),
                            nshiftT[NBLK * h:NBLK * h + NBLK, (g - 1) % 2, :].bitcast(F32)).then_inc(s_m[(g - 1) % 2], 16)
                if s == 1 and live(T + 1, CHUNKS) and live(T, CHUNKS):
                    store_v(T + 1)
                if s == 4 and live(T + 1, CHUNKS) and live(T, CHUNKS):
                    load_v(T + 1, 1 - par)
                if s == 5 and live(T + 1, CHUNKS) and live(T, CHUNKS):
                    spread_q(T + 1, 1 - par)
                if g % GB == 3 and live(GB * it + g // GB - 1, NB):
                    B = GB * it + g // GB - 1
                    apart(sp, s_h2, B)
                    sp.dma_start(cs_all[:, :, :], rows_of(mod_rows, B)[:, 3:5, :].broadcast_to([P, 2, E])).then_inc(s_cs, 16)
                if g % GB == 1:
                    B = GB * it + g // GB
                    if live(B, NB):
                        apart(sp, s_fin, B - 1)
                        sp.dma_start(x_res[:, B_par(g), :, :],
                                     rows_of(x_tok, B).rearrange("b p k e -> p (b k) e")).then_inc(s_xr[B_par(g)], 16)
                        sp.dma_start(ga_all[:, B_par(g), :],
                                     rows_of(mod_rows, B)[:, 2, :].to_broadcast([P, E])).then_inc(s_xr[B_par(g)], 16)
                    if live(B - 2, NB):
                        apart(sp, s_fin, B - 1)
                        sp.dma_start(rows_of(x_mid_tok, B - 2).rearrange("b p k e -> p (b k) e"),
                                     x_new[:, B_par(g), :, :]).then_inc(s_st[B_par(g)], 16)

            def B_par(g):
                return (g // GB) % 2

            over_groups(sp, slot)
            for b in range(2):
                sp.wait_ge(s_st[b], 16 * NB // 2)

            sp.wait_ge(s_tab, TAB_STEPS)
            sp.wait_ge(s_pad, 16 * NE * NBLK)
            sp.wait_ge(s_sc, 16 * NB * NBLK * TOPK)

            def tile_load(it, u):
                st = SU * it + u
                if not live(st, STEPS):
                    return
                row = sp.value_load(table[0:1, 0, bass.ds(st, 1)], min_val=0, max_val=NE * REGION - TR)
                apart(sp, s_yout, NBLK * (st - SU + 1))
                sp.dma_start(xs[:, u, :, :],
                             x_expert[bass.ds(row, TR)].rearrange("(a p) w -> p a w", p=P)).then_inc(s_xs[u], 16)

            over_steps(sp, tile_load)
            sp.wait_ge(s_ysc, 16 * NBLK * STEPS)

            def last_load(t, r, n):
                apart(sp, s_fs[r], 16 * n)
                for k in range(TOPK):
                    sp.dma_start(fin_y[:, r, k, :, :],
                                 y_token[k * TOK:(k + 1) * TOK].rearrange("(t a p) e -> t p a e", a=NT, p=P)[
                                     bass.ds(t, 1)].rearrange("t p a e -> p (t a) e")).then_inc(s_fl[r], 16)
                sp.dma_start(fin_x[:, r, :, :].rearrange("p (b k) e -> p b k e", b=CB),
                             rows_of(x_mid_tok, CB * t, CB).rearrange("b p k e -> p b k e")).then_inc(s_fl[r], 16)
                sp.dma_start(fin_gb[:, r, :, :], rows_of(mod_rows, CB * t, CB)[:, 5, :].rearrange(
                    "(o b) e -> o b e", o=1).broadcast_to([P, CB, E])).then_inc(s_fl[r], 16)

            def last_store(t, r):
                apart(sp, s_fc, t + 1)
                sp.dma_start(rows_of(out_tok, CB * t, CB).rearrange("b p k e -> p b k e"),
                             fin_x[:, r, :, :].rearrange("p (b k) e -> p b k e", b=CB)).then_inc(s_fs[r], 16)

            last_load(0, 0, 0)
            with sp.Fori(0, CHUNKS // 2 - 1) as it:
                last_load(2 * it + 1, 1, it)
                last_store(2 * it, 0)
                last_load(2 * it + 2, 0, it + 1)
                last_store(2 * it + 1, 1)
            last_load(CHUNKS - 1, 1, CHUNKS // 2 - 1)
            last_store(CHUNKS - 2, 0)
            last_store(CHUNKS - 1, 1)
            for r in range(2):
                sp.wait_ge(s_fs[r], 16 * CHUNKS // 2)

        @block.gpsimd
        def _(pool):
            pool.memset(c_in[:, :], 0.0).then_inc(s_pool0, 1)
            pool.memset(bias_lhs[:, :, :, :], 0.0).then_inc(s_pool0, 1)
            pool.memset(q_diag[:, :, :, :, :].bitcast(F32).rearrange("p a g h i -> p (a g h i)"), 0.0).then_inc(s_pool0, 1)
            pool.memset(ident[:, :], 0.0).then_inc(s_pool0, 1)
            pool.memset(tri[:, :, :], 1.0).then_inc(s_pool0, 1)
            pool.memset(neg[:, :, :], 0.0).then_inc(s_pool0, 1)
            pool.memset(nfloor[:, :], 0.0).then_inc(s_pool0, 1)
            pool.memset(v_slot[:, :, :, :, :, :].rearrange("p a k g h d -> p (a k g h d)"), 0.0).then_inc(s_pool0, 1)
            pool.iota(row_id[:, :], pattern=[[0, 1]], base=0, channel_multiplier=1).then_inc(s_pool0, 1)
            pool.wait_ge(s_pool0, 9)
            pool.memset(v_slot[:, :, :, :, :, D:D + 1].rearrange("p a k g h d -> p (a k g h) d"), 1.0).then_inc(s_pool0, 1)
            pool.affine_select(out=ident[:, :], in_=ident[:, :], compare_op=ALU.not_equal, fill=1.0, base=0,
                               pattern=[[-1, P]], channel_multiplier=1).then_inc(s_pool0, 1)
            pool.affine_select(out=tri[:, 0, :], in_=tri[:, 0, :], compare_op=ALU.is_ge, fill=0.0, base=0,
                               pattern=[[-1, P]], channel_multiplier=1).then_inc(s_pool0, 1)
            pool.affine_select(out=tri[:, 1, :], in_=tri[:, 1, :], compare_op=ALU.is_ge, fill=0.0, base=-1,
                               pattern=[[1, P]], channel_multiplier=-1).then_inc(s_pool0, 1)
            pool.affine_select(out=neg[:, 0, :], in_=neg[:, 0, :], compare_op=ALU.is_gt, fill=MASKED, base=0,
                               pattern=[[-1, P]], channel_multiplier=1).then_inc(s_pool0, 1)
            pool.affine_select(out=neg[:, 1, :], in_=neg[:, 1, :], compare_op=ALU.is_ge, fill=MASKED, base=0,
                               pattern=[[1, P]], channel_multiplier=-1).then_inc(s_pool0, 1)
            pool.affine_select(out=nfloor[:, 1:2], in_=nfloor[:, 1:2], compare_op=ALU.not_equal, fill=-MASKED, base=0,
                               pattern=[[0, 1]], channel_multiplier=1).then_inc(s_pool0, 1)
            pool.wait_ge(s_pool0, 16)
            pool.tensor_copy(identb[:, :], ident[:, :]).then_inc(s_pool0, 1)
            pool.tensor_copy(before_b[:, :], tri[:, 1, :]).then_inc(s_pool0, 1)
            pool.memset(ones_b[:, :], 1.0).then_inc(s_pool0, 1)
            pool.memset(ones_row[:, :], 1.0).then_inc(s_pool0, 1)
            pool.memset(pad_rows[:, :, :], 0.0).then_inc(s_pool0, 1)
            pool.iota(expert_idi[:, :], pattern=[[1, NE]], base=0, channel_multiplier=0).then_inc(s_pool0, 1)
            pool.iota(pad_idi[:, :], pattern=[[P, NBLK]], base=0, channel_multiplier=1).then_inc(s_pool0, 1)
            pool.iota(step_idi[:, :], pattern=[[1, STEPS]], base=0, channel_multiplier=0).then_inc(s_pool0, 1)
            pool.wait_ge(s_pool0, 24)
            pool.tensor_copy(pad_id[:, :], pad_idi[:, :]).then_inc(s_pool0, 1)
            pool.tensor_copy(expert_id[:, :], expert_idi[:, :]).then_inc(s_pool0, 1)
            pool.tensor_copy(step_id[:, :], step_idi[:, :]).then_inc(s_pool0, 1)
            pool.wait_ge(s_pool0, 27)
            for k in range(TOPK):
                pool.tensor_scalar(token_id[:, k, :], pad_id[:, :], float(k * TOK), None, ALU.add).then_inc(s_pool0, 1)
            pool.tensor_scalar(pad_rows[:, :, E], pad_id[:, :], float(TOPK * TOK), None, ALU.add).then_inc(s_pool0, 1)
            pool.tensor_scalar(next_row[:, :], expert_id[:, :], float(REGION), None, ALU.mult).then_inc(s_pool0, 1)

            def normalise(t, par):
                apart(pool, s_rstd, RSTD_STEPS * (t + 1))
                apart(pool, s_pA, (CQ + 1) * (t - 1) + 1)
                for a in range(NT):
                    pool.tensor_scalar(xn[:, a, :], x_in[:, par, a, :], mean_var[:, a, 0:1], rstd[:, a:a + 1],
                                       ALU.subtract, ALU.mult).then_inc(s_xn, 1)

            normalise(0, 0)
            normalise(1, 1)

            def slot(it, g):
                G, T, s = BODY * it + g, 2 * it + g // CG, g % CG
                par = (g // CG) % 2
                if live(G - 2, GROUPS):
                    apart(pool, s_exp, HG * (G - 1))
                    pr = probs[:, g % 2, :, :]
                    pool.affine_select(out=pr[:, :, P:2 * P], in_=pr[:, :, P:2 * P], compare_op=ALU.is_ge, fill=0.0,
                                       base=0, pattern=[[0, HG], [-1, P]], channel_multiplier=1).then_inc(s_aff, 1)
                    pool.affine_select(out=pr[:, :, 2 * P:3 * P], in_=pr[:, :, 2 * P:3 * P], compare_op=ALU.is_ge,
                                       fill=0.0, base=-1, pattern=[[0, HG], [1, P]],
                                       channel_multiplier=-1).then_inc(s_aff, 1)
                if s == 6 and live(T + 2, CHUNKS):
                    normalise(T + 2, par)
                if g % GB == 2 and live(GB * it + g // GB - 2, NB):
                    B, b = GB * it + g // GB - 2, (g // GB) % 2
                    apart(pool, s_rstd2, RSTD_STEPS * (B + 1))
                    for k in range(NBLK):
                        pool.tensor_scalar(h2f[:, k, :], x_new[:, b, k, :], mean_var2[:, k, 0:1], rstd2[:, k:k + 1],
                                           ALU.subtract, ALU.mult).then_inc(s_n2, 1)
                    apart(pool, s_n2, NBLK * (B + 1))
                    apart(pool, s_cs, 16 * (B + 1))
                    pool.tensor_tensor(h2f[:, :, :], h2f[:, :, :], cs_all[:, 1, :].unsqueeze(1).broadcast_to([P, NBLK, E]),
                                       ALU.mult).then_inc(s_m2, 1)
                    apart(pool, s_m2, B + 1)
                    apart(pool, s_sc, 16 * NBLK * TOPK * B)
                    pool.tensor_tensor(h2_rows[:, 0, :, 0:E], h2f[:, :, :],
                                       cs_all[:, 0, :].unsqueeze(1).broadcast_to([P, NBLK, E]), ALU.add).then_inc(s_h2, 1)
                    apart(pool, s_id, 2 * B)
                    pool.tensor_copy(h2_rows[:, :, :, E], token_id[:, :, :]).then_inc(s_id, 1)
                    apart(pool, s_id, 2 * B + 1)
                    pool.tensor_scalar(token_id[:, :, :], token_id[:, :, :], float(S), None, ALU.add).then_inc(s_id, 1)
                if g % GB == 1 and live(GB * it + g // GB - 3, NB):
                    B = GB * it + g // GB - 3
                    apart(pool, s_row, B + 1)
                    apart(pool, s_gate, B + 1)
                    apart(pool, s_dup, B + 1)
                    for k in range(NBLK):
                        for e in range(TOPK):
                            pool.indirect_dma_start(x_expert[:, :], bass.IndirectOffsetOnAxis(ap=row_i[:, k, e:e + 1], axis=0),
                                                    h2_rows[:, e, k, :], None).then_inc(s_sc, 16)
                if g % GB == 3 and live(GB * it + g // GB - 1, NB):
                    B = GB * it + g // GB - 1
                    b = (g // GB - 1) % 2
                    apart(pool, s_mkcp, B + 1)
                    apart(pool, s_e, B + 1)
                    for k in range(NBLK):
                        e_k = e_shift[:, b, :].rearrange("p (n k) -> p k n", k=NBLK)[:, k, :]
                        pool.tensor_tensor(o_tmp[:, k, :, :], o_mask[:, b, k, :, :],
                                           e_k.unsqueeze(2).broadcast_to([P, H, NV]), ALU.mult).then_inc(s_f1, 1)
                    apart(pool, s_f1, NBLK * (B + 1))
                    apart(pool, s_tocp, GB * (B + 1))
                    rows = o_rows[:, b, :, :, :].rearrange("p k h v -> p (k h v)")
                    pool.tensor_tensor(rows, rows, o_tmp[:, :, :, :].rearrange("p k h v -> p (k h v)"),
                                       ALU.add).then_inc(s_f2, 1)
                if g % GB == 0 and live(GB * it + g // GB - 2, NB):
                    B = GB * it + g // GB - 2
                    b = (g // GB) % 2
                    apart(pool, s_den, B + 1)
                    rd = rden[:, b, :, :].rearrange("p k h -> p (k h)")
                    apart(pool, s_fin, B)
                    pool.tensor_tensor(o_att[:, :, :].rearrange("p k (h d) -> p (k h) d", d=D),
                                       o_rows[:, b, :, :, 0:D].rearrange("p k h d -> p (k h) d"),
                                       rd.unsqueeze(2).broadcast_to([P, NBLK * H, D]), ALU.mult).then_inc(s_f3, 1)
                    apart(pool, s_f3, B + 1)
                    apart(pool, s_xr[b], 32 * (2 * it + (g // GB - 2) // 2 + 1))
                    pool.tensor_tensor(o_att[:, :, :], o_att[:, :, :],
                                       ga_all[:, b, :].unsqueeze(1).broadcast_to([P, NBLK, E]), ALU.mult).then_inc(s_f4, 1)
                    apart(pool, s_f4, B + 1)
                    apart(pool, s_st[b], 16 * (2 * it + (g // GB - 2) // 2))
                    pool.tensor_tensor(x_new[:, b, :, :], o_att[:, :, :], x_res[:, b, :, :], ALU.add).then_inc(s_fin, 1)

            over_groups(pool, slot)

            pool.wait_ge(s_padc, 2)
            for e in range(NE):
                for k in range(NBLK):
                    pool.indirect_dma_start(x_expert[:, :], bass.IndirectOffsetOnAxis(ap=pad_i[:, e, k:k + 1], axis=0),
                                            pad_rows[:, k, :], None).then_inc(s_pad, 16)

            def scatter_y(it, u):
                st = SU * it + u - 1
                if not live(st, STEPS):
                    return
                apart(pool, s_yout, NBLK * (st + 1))
                apart(pool, s_dest, st + 1)
                apart(pool, s_ysc, 16 * NBLK * st)
                for k in range(NBLK):
                    pool.indirect_dma_start(y_token[:, :], bass.IndirectOffsetOnAxis(ap=dest[:, (u - 1) % SU, k:k + 1], axis=0),
                                            y_out[:, (u - 1) % 2, k, :], None).then_inc(s_ysc, 16)

            over_steps(pool, scatter_y)

            def last_gate(t, r):
                apart(pool, s_fa, t + 1)
                y = fin_y[:, r, 0, :, :].rearrange("p (b k) e -> p b k e", b=CB)
                pool.tensor_tensor(y, y, fin_gb[:, r, :, :].unsqueeze(2).broadcast_to([P, CB, NBLK, E]),
                                   ALU.mult).then_inc(s_fb, 1)

            with pool.Fori(0, CHUNKS // 2) as it:
                last_gate(2 * it, 0)
                last_gate(2 * it + 1, 1)

        @block.vector
        def _(dve):
            dve0 = [0]

            def step(ins):
                dve0[0] += 1
                ins.then_inc(s_dve0, 1)
                dve.wait_ge(s_dve0, dve0[0])

            dve.wait_ge(s_ld, 16 * NLD)
            step(dve.memset(bias_rep, 0.0))
            step(dve.tensor_scalar(bias_row[:, 0, :], bias_row[:, 0, :], float(D) ** -0.5, None, ALU.mult))
            step(dve.tensor_copy(bias_part[:, 0, :, :], bias_row[:, :, :]))
            step(dve.tensor_tensor(bias_rest[:, :, :], bias_row[:, :, :], bias_part[:, 0, :, :], ALU.subtract))
            step(dve.tensor_copy(bias_part[:, 1, :, :], bias_rest[:, :, :]))
            step(dve.tensor_tensor(bias_rest[:, :, :], bias_rest[:, :, :], bias_part[:, 1, :, :], ALU.subtract))
            step(dve.tensor_copy(bias_part[:, 2, :, :], bias_rest[:, :, :]))
            for a in range(3):
                for c in range(4):
                    for n in range(2):
                        for part in range(3):
                            for cq in range(CQ):
                                src = bias_part[:, a, n, (4 * cq + c) * D:(4 * cq + c + 1) * D]
                                dst = bias_rep[:, (a * 4 + c) * 2 + n, cq * P:(cq + 1) * P].rearrange("o (h m) -> o h m", h=HG)
                                last = dve.tensor_copy(dst[:, :, part * D:(part + 1) * D],
                                                       src.unsqueeze(1).broadcast_to([1, HG, D]))
            step(last)
            step(dve.memset(bias_rep.rearrange("o (r n) m -> o r n m", n=2)[:, 0:4, 1, :].rearrange(
                "o c (g m) -> o c g m", m=SLOT)[:, :, :, SHIFT:SHIFT + 1], 1.0))
            assert dve0[0] == DVE_BIAS
            dve.wait_ge(s_pool0, 9)
            step(dve.tensor_scalar(row_bits[:, :], row_id[:, :], 24, None, ALU.bitwise_and))
            step(dve.tensor_scalar(low_mask[:, 0:1], row_bits[:, :], 16.0, -1.0, ALU.is_equal, ALU.mult))
            step(dve.tensor_scalar(low_mask[:, 1:2], row_bits[:, :], 8.0, -1.0, ALU.is_equal, ALU.mult))
            step(dve.tensor_scalar(row_bits[:, :], row_id[:, :], 3, None, ALU.bitwise_and))
            step(dve.tensor_copy(quad[:, :], row_bits[:, :]))
            for c in range(4):
                step(dve.tensor_scalar(bias_ind[:, c, :], quad[:, 0:1].broadcast_to([P, P]), float(c), None, ALU.is_equal))
            dve.wait_ge(s_act0, 1)
            step(dve.tensor_scalar(c_exp[:, :], c_exp[:, :], 1.0, None, ALU.add))
            step(dve.reciprocal(c_exp[:, :], c_exp[:, :]))
            step(dve.tensor_tensor(c_in[:, :], c_in[:, :], c_exp[:, :], ALU.mult))
            assert dve0[0] == DVE_SILU
            dve.wait_ge(s_pe0, 1)
            for n in range(2):
                view = pP[0][:, n * P:(n + 1) * P].rearrange("p (c d) -> p c d", d=D)
                scale = float(D) ** -0.5 if n == 0 else 1.0
                step(dve.memset(w_slot[:, n, :, SHIFT:SLOT], 0.0))
                for part in range(3):
                    step(dve.tensor_scalar(w_slot[:, n, :, part * D:(part + 1) * D], view, scale, None, ALU.mult))
            step(dve.tensor_copy(wvT[:, :], pP[0][:, 2 * P:3 * P]))
            step(dve.tensor_copy(siluT[:, :], pP[0][:, 3 * P:3 * P + NB]))
            assert dve0[0] == DVE_WEIGHTS
            dve.wait_ge(s_pe0, 2)
            for half in range(2):
                step(dve.tensor_copy(mod_sb[:, 3 * half:3 * half + 3, :].rearrange("b m e -> b (m e)"),
                                     pP[half][0:NB, 0:3 * E]))
            for half in range(2):
                scale_m, gate_m = 3 * half + 1, 3 * half + 2
                step(dve.tensor_scalar(mod_sb[:, scale_m, :], mod_sb[:, scale_m, :], 1.0, None, ALU.add))
                step(dve.tensor_scalar(gate_sign[:, half, :], mod_sb[:, gate_m, :], 0.0, 2.0, ALU.is_ge, ALU.mult))
                step(dve.tensor_scalar(gate_sign[:, half, :], gate_sign[:, half, :], -1.0, None, ALU.add))
                step(dve.tensor_tensor(mod_sb[:, gate_m, :], mod_sb[:, gate_m, :], gate_sign[:, half, :], ALU.mult))
                step(dve.tensor_scalar(mod_sb[:, gate_m, :], mod_sb[:, gate_m, :], 0.25, None, ALU.max))
                step(dve.tensor_tensor(mod_sb[:, gate_m, :], mod_sb[:, gate_m, :], gate_sign[:, half, :], ALU.mult))
            for half in range(2):
                step(dve.tensor_copy(shiftT[:, half, :], pB[:, (2 * half) * NB:(2 * half + 1) * NB]))
                step(dve.tensor_scalar(scaleT[:, half, :], pB[:, (2 * half + 1) * NB:(2 * half + 2) * NB], 1.0, None, ALU.add))
            dve.wait_ge(s_pe0, 3)
            step(dve.tensor_copy(experts[:, :, HID:HID + HC], pP[0][:, 0:NE * HC].rearrange("p (x c) -> p x c", c=HC)))
            step(dve.tensor_copy(wgT[:, :], pP[0][:, NE * HC:NE * HC + NE]))
            assert dve0[0] == DVE_MOD

            def layer_stats(t, par, n):
                dve.wait_ge(s_x[par], 16 * (n + 1))
                after(dve, s_xn, NT * t)
                for a in range(NT):
                    dve.bn_stats(stats[:, a, :], x_in[:, par, a, :]).then_inc(s_stats, 1)
                apart(dve, s_stats, NT * (t + 1))
                for a in range(NT):
                    dve.bn_aggr(mean_var[:, a, :], stats[:, a, :]).then_inc(s_aggr, 1)
                dve.wait_ge(s_aggr, NT * (t + 1))
                rsqrt(dve, s_rstd, RSTD_STEPS * t, rstd[:, :], mean_var[:, :, 1], half_var[:, :], r_tmp[:, :])

            def values(u):
                dve.wait_ge(s_pB, (CQ + 1) * u + 1)
                after(dve, s_vst, 16 * u)
                dve.tensor_tensor(v_tok[:, :, :], pP[1][:, :].rearrange("p (a e) -> p a e", a=NT),
                                  bv_all[:, :].unsqueeze(1).broadcast_to([P, NT, E]), ALU.add).then_inc(s_v, 1)

            def pack(u, n, i, par):
                if n == 0:
                    dve.wait_ge(s_rq, CQ * u + i + 1)
                    if i == 0:
                        after(dve, s_qb, 16 * HG * u)
                    dst = q_pack[:, :, :]
                else:
                    dve.wait_ge(s_rk, CQ * u + i + 1)
                    if i == 0:
                        after(dve, s_s2, CG * HG * (u - 1))
                    dst = k_pack[:, par, :, :]
                dst = dst.rearrange("p g i -> p (g i)").rearrange("p (n c) -> p c n", c=C)[:, 4 * i:4 * i + 4, :]
                dve.scalar_tensor_tensor(out=dst, in0=rounded[:, n, :, :].bitcast(F32), scalar=low_mask[:, n:n + 1],
                                         in1=pP[n][:, :].rearrange("p (c n) -> p c n", c=4),
                                         op0=ALU.mult, op1=ALU.add).then_inc(s_q if n == 0 else s_k, 1)

            def batch_stats(B, b):
                dve.wait_ge(s_fin, B + 1)
                after(dve, s_n2, NBLK * B)
                for k in range(NBLK):
                    dve.bn_stats(stats2[:, k, :], x_new[:, b, k, :]).then_inc(s_stats2, 1)
                apart(dve, s_stats2, NBLK * (B + 1))
                for k in range(NBLK):
                    dve.bn_aggr(mean_var2[:, k, :], stats2[:, k, :]).then_inc(s_aggr2, 1)
                dve.wait_ge(s_aggr2, NBLK * (B + 1))
                rsqrt(dve, s_rstd2, RSTD_STEPS * B, rstd2[:, :], mean_var2[:, :, 1], half_var2[:, :], r_tmp2[:, :])

            def choose(B):
                dve.wait_ge(s_lg, B + 1)
                dve.tensor_copy(logits[:, :, :].rearrange("p k x -> p (k x)"), pP[1][:, S:S + NBLK * NE]).then_inc(s_lgc, 1)
                apart(dve, s_lgc, B + 1)
                for k in range(NBLK):
                    dve.max(top[:, k, :], logits[:, k, :]).then_inc(s_mx, 1)
                apart(dve, s_mx, NBLK * (B + 1))
                for k in range(NBLK):
                    dve.max_index(top_at[:, k, :], top[:, k, :], logits[:, k, :]).then_inc(s_ix, 1)
                dve.tensor_tensor(top_arg[:, :, :], top[:, :, :], top[:, :, 0:1].broadcast_to([P, NBLK, NE]),
                                  ALU.subtract).then_inc(s_ein, 1)
                dve.wait_ge(s_ix, NBLK * (B + 1))
                dve.tensor_copy(top_atf[:, :, :], top_at[:, :, 0:TOPK]).then_inc(s_ixf, 1)
                dve.wait_ge(s_ixf, B + 1)
                for k in range(NBLK):
                    dve.tensor_tensor(chosen[:, k, :, :], expert_id[:, :].unsqueeze(1).broadcast_to([P, TOPK, NE]),
                                      top_atf[:, k, :].unsqueeze(2).broadcast_to([P, TOPK, NE]), ALU.is_equal).then_inc(s_oh, 1)
                dve.wait_ge(s_oh, NBLK * (B + 1))
                dve.tensor_tensor(chosen_b[:, :, :], chosen[:, :, 0, :], chosen[:, :, 1, :], ALU.add).then_inc(s_ch, 1)

            def place_rows(B):
                dve.wait_ge(s_pre, B + 1)
                dve.tensor_tensor(place[:, :, :], pP[1][:, 0:NBLK * NE].rearrange("p (k x) -> p k x", k=NBLK),
                                  next_row[:, :].unsqueeze(1).broadcast_to([P, NBLK, NE]), ALU.add).then_inc(s_pos, 1)
                dve.wait_ge(s_pos, 2 * B + 1)
                dve.tensor_tensor(next_row[:, :], pP[1][:, NBLK * NE:(NBLK + 1) * NE], next_row[:, :], ALU.add).then_inc(s_pos, 1)
                for k in range(NBLK):
                    dve.tensor_tensor(place_of[:, k, :, :], chosen[:, k, :, :],
                                      place[:, k, :].unsqueeze(1).broadcast_to([P, TOPK, NE]), ALU.mult).then_inc(s_prod, 1)
                dve.wait_ge(s_prod, NBLK * (B + 1))
                dve.tensor_reduce(row_f[:, :, :].rearrange("p k e -> p (k e)"),
                                  place_of[:, :, :, :].rearrange("p k e x -> p (k e) x"), AX_X, ALU.add).then_inc(s_rowf, 1)
                dve.wait_ge(s_rowf, B + 1)
                after(dve, s_sc, 16 * NBLK * TOPK * B)
                dve.tensor_copy(row_i[:, :, :], row_f[:, :, :]).then_inc(s_row, 1)

            def gates(B):
                dve.wait_ge(s_eg, B + 1)
                dve.tensor_reduce(gate_sum[:, :], top_exp[:, :, :], AX_X, ALU.add).then_inc(s_gsum, 1)
                dve.wait_ge(s_gsum, B + 1)
                dve.reciprocal(gate_inv[:, :], gate_sum[:, :]).then_inc(s_ginv, 1)
                dve.wait_ge(s_ginv, B + 1)
                dve.tensor_tensor(h2_rows[:, :, :, E + 1].rearrange("p e k -> p k e"), top_exp[:, :, 0:TOPK],
                                  gate_inv[:, :].unsqueeze(2).broadcast_to([P, NBLK, TOPK]), ALU.mult).then_inc(s_gate, 1)

            dve.wait_ge(s_pool0, 31)
            layer_stats(0, 0, 0)
            values(0)
            for i in range(CQ):
                pack(0, 0, i, 0)
                pack(0, 1, i, 0)
            layer_stats(1, 1, 0)

            def slot(it, g):
                G, T, s = BODY * it + g, 2 * it + g // CG, g % CG
                par = (g // CG) % 2
                prep = live(T + 1, CHUNKS) and live(T, CHUNKS)

                def maxima(h):
                    dve.wait_ge(s_s1, HG * G + h + 1)
                    dve.tensor_reduce(row_max[:, g % 2, h, :], pS1[h % 2][:, :].rearrange("p (k j) -> p k j", k=NBLK),
                                      AX_X, ALU.max).then_inc(s_red, 1)

                if live(G, GROUPS):
                    maxima(0)
                if g % GB == 0 and live(GB * it + g // GB - 3, NB):
                    place_rows(GB * it + g // GB - 3)
                if live(G, GROUPS):
                    maxima(1)
                if prep and 1 <= s <= CQ:
                    pack(T + 1, 0, s - 1, 1 - par)
                if live(G, GROUPS):
                    maxima(2)
                    maxima(3)
                    dve.wait_ge(s_red, HG * G + HG)
                    dve.scalar_tensor_tensor(out=nshift[:, (g // GB) % 4, g % GB, :, :], in0=row_max[:, g % 2, :, :],
                                             scalar=-1.0, in1=nfloor[:, :].unsqueeze(1).broadcast_to([P, HG, NBLK]),
                                             op0=ALU.mult, op1=ALU.min).then_inc(s_nm, 1)
                if g % GB == 3 and live(GB * it + g // GB - 2, NB):
                    choose(GB * it + g // GB - 2)
                if g % GB == 0 and live(GB * it + g // GB - 3, NB):
                    gates(GB * it + g // GB - 3)
                if prep and s == 0:
                    values(T + 1)
                if prep and 1 <= s <= CQ:
                    pack(T + 1, 1, s - 1, 1 - par)
                if g % GB == 1 and live(GB * it + g // GB - 2, NB):
                    batch_stats(GB * it + g // GB - 2, (g // GB) % 2)
                if s == 5 and live(T + 2, CHUNKS):
                    layer_stats(T + 2, par, it + 1)
                if g % GB == 0:
                    B = GB * it + g // GB - 1
                    if live(B, NB):
                        dve.wait_ge(s_nm, GB * (B + 1))
                        after(dve, s_f1, NBLK * (B - 1))
                        dve.tensor_scalar(e_arg[:, (g // GB - 1) % 2, :],
                                          nshift[:, (g // GB - 1) % 4, :, :, :].bitcast(F32).rearrange("p g h k -> p (g h k)"),
                                          0.0, None, ALU.min).then_inc(s_earg, 1)
                    if live(B - 1, NB):
                        dve.wait_ge(s_f2, B)
                        b = (g // GB) % 2
                        dve.reciprocal(rden[:, b, :, :].rearrange("p k h -> p (k h)"),
                                       o_rows[:, b, :, :, D].rearrange("p k h -> p (k h)")).then_inc(s_den, 1)

            over_groups(dve, slot)

            dve.wait_ge(s_pos, 2 * NB)
            dve.tensor_tensor(pad_f[:, :, :], next_row[:, :].unsqueeze(2).broadcast_to([P, NE, NBLK]),
                              pad_id[:, :].unsqueeze(1).broadcast_to([P, NE, NBLK]), ALU.add).then_inc(s_padc, 1)
            dve.wait_ge(s_padc, 1)
            dve.tensor_copy(pad_i[:, :, :], pad_f[:, :, :]).then_inc(s_padc, 1)
            tab = [0]

            def entry(ins):
                tab[0] += 1
                ins.then_inc(s_tab, 1)
                dve.wait_ge(s_tab, tab[0])

            entry(dve.scalar_tensor_tensor(out=count_f[:, :], in0=expert_id[0:1, :], scalar=-float(REGION),
                                           in1=next_row[0:1, :], op0=ALU.mult, op1=ALU.add))
            entry(dve.tensor_scalar(tiles_i[:, :], count_f[:, :], float(TR - 1), None, ALU.add))
            entry(dve.tensor_scalar(tiles_i[:, :], tiles_i[:, :], TR.bit_length() - 1, None, ALU.logical_shift_right))
            entry(dve.tensor_copy(tiles[:, :], tiles_i[:, :]))
            entry(dve.tensor_tensor_scan(tiles_sum[:, :], ones_row[:, :], tiles[:, :], 0.0, ALU.mult, ALU.add))
            steps_of = step_id[:, :].unsqueeze(2).broadcast_to([1, STEPS, NE - 1])
            entry(dve.tensor_tensor(past[:, :, :], steps_of, tiles_sum[:, 0:NE - 1].unsqueeze(1).broadcast_to(
                [1, STEPS, NE - 1]), ALU.is_ge))
            entry(dve.tensor_tensor(past_n[:, :, :], past[:, :, :], tiles[:, 0:NE - 1].unsqueeze(1).broadcast_to(
                [1, STEPS, NE - 1]), ALU.mult))
            entry(dve.tensor_reduce(step_expert[:, :], past[:, :, :], AX_X, ALU.add))
            entry(dve.tensor_reduce(step_base[:, :], past_n[:, :, :], AX_X, ALU.add))
            entry(dve.tensor_tensor(step_row[:, :], step_id[:, :], step_base[:, :], ALU.subtract))
            entry(dve.tensor_scalar(last_tile[:, :], tiles[:, NE - 1:NE], -1.0, 0.0, ALU.add, ALU.max))
            entry(dve.tensor_scalar(step_lim[:, :], step_expert[:, :], float(NE - 1), float(STEPS), ALU.is_lt, ALU.mult))
            entry(dve.tensor_scalar(step_lim[:, :], step_lim[:, :], last_tile[:, 0:1], None, ALU.add))
            entry(dve.tensor_tensor(step_row[:, :], step_row[:, :], step_lim[:, :], ALU.min))
            entry(dve.tensor_scalar(step_row[:, :], step_row[:, :], float(TR), None, ALU.mult))
            entry(dve.scalar_tensor_tensor(out=step_row[:, :], in0=step_expert[:, :], scalar=float(REGION),
                                           in1=step_row[:, :], op0=ALU.mult, op1=ALU.add))
            entry(dve.tensor_copy(table[:, 0, :], step_row[:, :]))
            entry(dve.tensor_copy(table[:, 1, :], step_expert[:, :]))
            assert tab[0] == TAB_STEPS
            dve.wait_ge(s_pv, GROUPS)
            dve.wait_ge(s_mk, NB)
            dve.wait_ge(s_ldx, 16 * (NE + 4))

            def weights(st, r):
                e = dve.value_load(table[0:1, 1, bass.ds(st, 1)], min_val=0, max_val=NE - 1)
                after(dve, s_y, st - SU + 1)
                after(dve, s_ysum, st - SU + 1)
                dve.tensor_copy(w_ring[:, r, :], experts[:, bass.ds(e, 1), :].rearrange("p o n -> p (o n)")).then_inc(s_w, 1)

            def turned(st, r, x):
                dve.wait_ge(s_xt, st + 1)
                dve.tensor_copy(xsT[:, r, :], pB[:, 0:TR]).then_inc(s_xtc, 1)
                after(dve, s_ysc, 16 * NBLK * (st - SU + 1))
                dve.tensor_copy(dest[:, x, :], xs[:, x, :, E]).then_inc(s_dest, 1)

            weights(0, 0)
            turned(0, 0, 0)

            def expert_step(it, u):
                st = SU * it + u
                if live(st + 1, STEPS):
                    weights(st + 1, (u + 1) % SU)
                    turned(st + 1, (u + 1) % 2, (u + 1) % SU)
                if live(st - 1, STEPS):
                    r = (u - 1) % 2
                    dve.wait_ge(s_y, st)
                    after(dve, s_yout, NBLK * (st - 2))
                    dve.tensor_tensor(y_sum[:, r, :, :], pO[:, 0:NBLK * E].rearrange("p (k e) -> p k e", k=NBLK),
                                      w_ring[:, (u - 1) % SU, 2 * HID + HC:EXP].unsqueeze(1).broadcast_to([P, NBLK, E]),
                                      ALU.add).then_inc(s_ysum, 1)

            over_steps(dve, expert_step)

            def last_sum(t, r, n):
                dve.wait_ge(s_fl[r], 64 * (n + 1))
                dve.tensor_tensor(fin_y[:, r, 0, :, :], fin_y[:, r, 0, :, :], fin_y[:, r, 1, :, :], ALU.add).then_inc(s_fa, 1)

            def last_add(t, r):
                dve.wait_ge(s_fb, t + 1)
                dve.tensor_tensor(fin_x[:, r, :, :], fin_x[:, r, :, :], fin_y[:, r, 0, :, :], ALU.add).then_inc(s_fc, 1)

            with dve.Fori(0, CHUNKS // 2) as it:
                for r in range(2):
                    last_sum(2 * it + r, r, it)
                    last_add(2 * it + r, r)

        @block.scalar
        def _(act):
            act.wait_ge(s_ld, 16 * NLD)
            act.activation(c_exp[:, :], c_in[:, :], ACT.Exp, scale=-1.0).then_inc(s_act0, 1)

            def modulate(u):
                act.wait_ge(s_pA, (CQ + 1) * u + 1)
                after(act, s_pB, (CQ + 1) * u)
                for b in range(CB):
                    act.activation(hT[:, b * S:(b + 1) * S], pP[0][:, b * S:(b + 1) * S], ACT.Identity,
                                   scale=scaleT[:, 0, bass.ds(CB * u + b, 1)],
                                   bias=shiftT[:, 0, bass.ds(CB * u + b, 1)]).then_inc(s_hT, 1)

            def round_piece(u, n, i):
                act.wait_ge(s_pB if n else s_pA, (CQ + 1) * u + 2 + i)
                act.activation(rounded[:, n, :, :].rearrange("p c n -> p (c n)"), pP[n][:, :],
                               ACT.Copy).then_inc(s_rk if n else s_rq, 1)

            act.wait_ge(s_dve0, DVE_MOD)
            modulate(0)
            for i in range(CQ):
                round_piece(0, 0, i)
                round_piece(0, 1, i)

            def slot(it, g):
                G, T, s = BODY * it + g, 2 * it + g // CG, g % CG
                prep = live(T + 1, CHUNKS) and live(T, CHUNKS)
                batch = GB * it + (g - 4) // GB
                b4 = ((g - 4) // GB) % 2

                def exponentials(h):
                    act.wait_ge(s_s2, HG * (G - 2) + h + 1)
                    if h == 0:
                        after(act, s_pv, G - 3)
                    act.activation(probs[:, g % 2, h, :], pS2[h % 2][:, :], ACT.Exp).then_inc(s_exp, 1)

                if live(G - 4, GROUPS):
                    act.wait_ge(s_to, G - 3)
                    if g % GB == 0:
                        after(act, s_fin, batch - 1)
                    act.copy(o_rows[:, b4, :, HG * (g % GB):HG * (g % GB) + HG, :],
                             pB[:, 0:NBLK * P].rearrange("p (k h m) -> p k h m", k=NBLK, h=HG)[:, :, :, 0:NV]).then_inc(s_tocp, 1)
                    if g % GB == 3:
                        act.wait_ge(s_mk, batch + 1)
                        after(act, s_f1, NBLK * (batch - 1))
                        act.copy(o_mask[:, b4, :, :, :].rearrange("p k h v -> p (k h v)"),
                                 pB[:, 0:NBLK * H * NV]).then_inc(s_mkcp, 1)
                if live(G - 2, GROUPS):
                    exponentials(0)
                if g % GB == 3 and live(GB * it + g // GB - 2, NB):
                    act.wait_ge(s_h2t, GB * it + g // GB - 1)
                    act.copy(h2T[:, :], pP[1][:, 0:S]).then_inc(s_h2c, 1)
                if live(G - 1, GROUPS):
                    act.wait_ge(s_tm, G)
                    after(act, s_m[(g - 1) % 2], 16 * HG * (BODY // 2 * it + (g - 1) // 2))
                    act.copy(nshiftT[:, (g - 1) % 2, :], pB[0:HG * NBLK, 0:P]).then_inc(s_tmcp, 1)
                if live(G - 2, GROUPS):
                    exponentials(1)
                if prep and s == 0:
                    modulate(T + 1)
                if prep and 1 <= s <= CQ:
                    round_piece(T + 1, 0, s - 1)
                if live(G - 2, GROUPS):
                    exponentials(2)
                if live(G - 3, GROUPS):
                    act.wait_ge(s_pv, G - 2)
                    after(act, s_to, G - 4)
                    act.copy(oT[:, (g - 3) % 2, :], pO[:, 0:S]).then_inc(s_ot, 1)
                if live(G - 2, GROUPS):
                    exponentials(3)
                if prep and 1 <= s <= CQ:
                    round_piece(T + 1, 1, s - 1)
                if g % GB == 3 and live(GB * it + g // GB - 2, NB):
                    B = GB * it + g // GB - 2
                    act.copy(h2_rows[:, 1, :, 0:E], h2_rows[:, 0, :, 0:E]).then_inc(s_dup, 1)
                if g % GB == 0 and live(GB * it + g // GB - 3, NB):
                    B = GB * it + g // GB - 3
                    act.wait_ge(s_ein, B + 1)
                    act.activation(top_exp[:, :, :], top_arg[:, :, :], ACT.Exp).then_inc(s_eg, 1)
                if g % GB == 1 and live(GB * it + g // GB - 1, NB):
                    B = GB * it + g // GB - 1
                    act.wait_ge(s_earg, B + 1)
                    b = (g // GB - 1) % 2
                    act.activation(e_shift[:, b, :], e_arg[:, b, :], ACT.Exp).then_inc(s_e, 1)

            over_groups(act, slot)

            def expert_step(it, u):
                st = SU * it + u
                r = u % 2
                if live(st, STEPS):
                    for c in range(HC):
                        act.wait_ge(s_hid, HC * st + (c // 2 + 1) * 2)
                        if c == 0:
                            after(act, s_y, st - 1)
                        act.activation(hidT[:, r, c, :], hid_bank(r, c), ACT.Gelu,
                                       bias=w_ring[:, u, HID + c:HID + c + 1]).then_inc(s_gelu, 1)
                if live(st - 1, STEPS):
                    q = (u - 1) % 2
                    act.wait_ge(s_ysum, st)
                    after(act, s_ysc, 16 * NBLK * (st - 2))
                    for k in range(NBLK):
                        act.activation(y_out[:, q, k, :], y_sum[:, q, k, :], ACT.Copy,
                                       scale=xs[:, (u - 1) % SU, k, E + 1:E + 2]).then_inc(s_yout, 1)

            over_steps(act, expert_step)

        @block.tensor
        def _(pe):
            pe.wait_ge(s_pool0, 17)
            pe.wait_ge(s_dve0, DVE_SILU)
            for n in range(3):
                pe.transpose(pP[0][:, n * P:(n + 1) * P], w_nat[:, n, :], ident[:, :])
            pe.transpose(pP[0][:, 3 * P:4 * P], c_in[:, :], ident[:, :]).then_inc(s_pe0, 1)
            pe.wait_ge(s_dve0, DVE_WEIGHTS)
            for half in range(2):
                pe.matmul(pP[half][0:NB, 0:3 * E], siluT[:, :], wmod_sb[:, 3 * half:3 * half + 3, :].rearrange("k m e -> k (m e)"),
                          start=True, stop=True)
            for half in range(2):
                for m in range(2):
                    last = pe.matmul(pB[:, (2 * half + m) * NB:(2 * half + m + 1) * NB], wmod_sb[:, 3 * half + m, :],
                                     siluT[:, :], start=True, stop=True)
            last.then_inc(s_pe0, 1)
            pe.wait_ge(s_dve0, DVE_MOD - 2)
            pe.wait_ge(s_ldx, 16 * (NE + 4))
            pe.transpose(pP[0][:, 0:NE * HC], b1_rows[:, :], ident[0:NE * HC, 0:NE * HC])
            pe.transpose(pP[0][:, NE * HC:NE * HC + NE], wg_rows[:, :], ident[0:NE, 0:NE]).then_inc(s_pe0, 1)
            pe.wait_ge(s_dve0, DVE_MOD)

            def tokens(u):
                pe.wait_ge(s_xn, NT * (u + 1))
                after(pe, s_q, CQ * u)
                for a in range(NT):
                    last = pe.transpose(pP[0][:, a * P:(a + 1) * P], xn[:, a, :], ident[:, :])
                last.then_inc(s_pA, 1)

            def values(u):
                pe.wait_ge(s_hT, CB * (u + 1))
                after(pe, s_k, CQ * u)
                for a in range(NT):
                    last = pe.matmul(pP[1][:, a * P:(a + 1) * P], hT[:, a * P:(a + 1) * P], wvT[:, :], start=True, stop=True)
                last.then_inc(s_pB, 1)

            def project(u, n, i):
                if n == 0:
                    pe.wait_ge(s_hT, CB * (u + 1))
                    after(pe, s_q, CQ * u + i)
                else:
                    pe.wait_ge(s_v, u + 1)
                    after(pe, s_k, CQ * u + i)
                pe.matmul(pP[n][:, :], bias_lhs[:, n, i, :], bias_ind[:, :, :].rearrange("p c n -> p (c n)"),
                          start=True, stop=False, skip_group_check=True)
                heads = hT[:, :].rearrange("p (g h r) -> p h g r", h=HG, r=R)
                for c in range(4):
                    for h in range(HG):
                        last = pe.matmul(pP[n][SLOT * h:SLOT * h + SLOT, c * P:(c + 1) * P].rearrange("p (g r) -> p g r", r=R),
                                         w_slot[:, n, 4 * i + c, :], heads[:, h], start=False, stop=(c == 3),
                                         skip_group_check=True)
                last.then_inc(s_pB if n else s_pA, 1)

            tokens(0)
            values(0)
            for i in range(CQ):
                project(0, 0, i)
                project(0, 1, i)

            def slot(it, g):
                G, T, s = BODY * it + g, 2 * it + g // CG, g % CG
                par = (g // CG) % 2
                prep = live(T + 1, CHUNKS) and live(T, CHUNKS)

                def scores(h):
                    if s == 0 and h == 0:
                        pe.wait_ge(s_qb, 16 * HG * (T + 1))
                        pe.wait_ge(s_k, CQ * (T + 1))
                    after(pe, s_red, HG * G + h - 1)
                    for k in range(NBLK):
                        pe.matmul(pS1[h % 2][:, k * S:(k + 1) * S], q_diag[:, par, s, h, k * P:(k + 1) * P],
                                  k_pack[:, par, s, :], start=True, stop=False, skip_group_check=True)
                        o = k * S + (1 - k) * P
                        last = pe.matmul(pS1[h % 2][:, o:o + P], identb[:, :], neg[:, k, :], start=False, stop=True,
                                         skip_group_check=True)
                    last.then_inc(s_s1, 1)

                def shifted_scores(h):
                    g2 = (g - 2) % BODY
                    if h == 0:
                        pe.wait_ge(s_m[g % 2], 16 * HG * (BODY // 2 * it + (g - 2) // 2 + 1))
                    after(pe, s_exp, HG * (G - 2) + h - 1)
                    for k in range(NBLK):
                        last = pe.matmul(pS2[h % 2][:, k * S:(k + 1) * S], k_pack[:, g2 // CG, g2 % CG, k * P:(k + 1) * P],
                                         q_diag[:, g2 // CG, g2 % CG, h, :], start=True, stop=True)
                    last.then_inc(s_s2, 1)

                if live(G - 4, GROUPS):
                    pe.wait_ge(s_ot, G - 3)
                    after(pe, s_tmcp, min(G - 1, GROUPS) if isinstance(G, int) else G - 1)
                    for k in range(NBLK):
                        last = pe.transpose(pB[:, k * P:(k + 1) * P], oT[:, (g - 4) % 2, k * P:(k + 1) * P], ident[:, :])
                    last.then_inc(s_to, 1)
                if g % GB == 3 and live(GB * it + g // GB - 1, NB):
                    g4 = (g - 7) % BODY
                    pe.wait_ge(s_tocp, G - 3)
                    for k in range(NBLK):
                        heads = v_slot[:, g4 // CG, 1 - k, g4 % CG:g4 % CG + GB, :, 0:NV].rearrange("p g h v -> p (g h) v")
                        last = pe.matmul(pB[:, k * H * NV:(k + 1) * H * NV].rearrange("p (h v) -> p h v", v=NV),
                                         tri[:, k, :], heads, start=True, stop=True)
                    last.then_inc(s_mk, 1)
                packed = CQ * (T + 1) + max(0, min(CQ, s - 1))
                packed = min(packed, CQ * CHUNKS) if isinstance(packed, int) else packed
                if g % GB == 3 and live(GB * it + g // GB - 2, NB):
                    pe.wait_ge(s_h2, GB * it + g // GB - 1)
                    pe.wait_ge(s_k, packed)
                    for k in range(NBLK):
                        last = pe.transpose(pP[1][:, k * P:(k + 1) * P], h2_rows[:, 0, k, 0:E], ident[:, :])
                    last.then_inc(s_h2t, 1)
                if g % GB == 0 and live(GB * it + g // GB - 3, NB):
                    pe.wait_ge(s_ch, GB * it + g // GB - 2)
                    pe.wait_ge(s_k, packed)
                    first, second = chosen_b[:, 0, :], chosen_b[:, 1, :]
                    pe.matmul(pP[1][:, 0:NE], before_b[:, :], first, start=True, stop=True)
                    pe.matmul(pP[1][:, NE:2 * NE], before_b[:, :], second, start=True, stop=False)
                    pe.matmul(pP[1][:, NE:2 * NE], ones_b[:, :], first, start=False, stop=True)
                    pe.matmul(pP[1][:, 2 * NE:3 * NE], ones_b[:, :], first, start=True, stop=False)
                    pe.matmul(pP[1][:, 2 * NE:3 * NE], ones_b[:, :], second, start=False, stop=True).then_inc(s_pre, 1)
                if live(G, GROUPS):
                    scores(0)
                if live(G - 2, GROUPS):
                    shifted_scores(0)
                if live(G - 1, GROUPS):
                    pe.wait_ge(s_nm, G)
                    after(pe, s_tocp, G - 3)
                    if g % GB == 3:
                        after(pe, s_mkcp, GB * it + g // GB)
                    pe.transpose(pB[0:HG * NBLK, 0:P],
                                 nshift[:, ((g - 1) // GB) % 4, (g - 1) % GB, :, :].bitcast(F32).rearrange("p h k -> p (h k)"),
                                 ident[:, :]).then_inc(s_tm, 1)
                if live(G, GROUPS):
                    scores(1)
                if live(G - 2, GROUPS):
                    shifted_scores(1)
                if g % GB == 3 and live(GB * it + g // GB - 2, NB):
                    pe.wait_ge(s_h2c, GB * it + g // GB - 1)
                    for k in range(NBLK):
                        last = pe.matmul(pP[1][:, S + k * NE:S + (k + 1) * NE], h2T[:, k * P:(k + 1) * P], wgT[:, :],
                                         start=True, stop=True)
                    last.then_inc(s_lg, 1)
                if prep and s == 0:
                    tokens(T + 1)
                if prep and 1 <= s <= CQ:
                    project(T + 1, 0, s - 1)
                if live(G, GROUPS):
                    scores(2)
                if live(G - 2, GROUPS):
                    shifted_scores(2)
                if live(G - 3, GROUPS):
                    g3 = (g - 3) % BODY
                    pe.wait_ge(s_aff, 2 * (G - 2))
                    after(pe, s_ot, G - 3)
                    if g3 % CG == 0:
                        pe.wait_ge(s_vr, 32 * (2 * it + (g - 3) // CG + 1))
                    for k in range(NBLK):
                        for h in range(HG):
                            last = pe.matmul(pO[SLOT * h:SLOT * h + SLOT, 0:S], v_slot[:, g3 // CG, k, g3 % CG, h, :],
                                             probs[:, (g - 3) % 2, h, k * S:(k + 1) * S], start=(k == 0), stop=(k == 1))
                    last.then_inc(s_pv, 1)
                if live(G, GROUPS):
                    scores(3)
                if live(G - 2, GROUPS):
                    shifted_scores(3)
                if g % GB == 3:
                    after(pe, s_lgc, min(GB * it + g // GB - 1, NB) if isinstance(it, int) else GB * it + g // GB - 1)
                if g % GB == 0:
                    after(pe, s_pos, min(2 * (GB * it + g // GB - 2), 2 * NB) if isinstance(it, int) else
                          2 * (GB * it + g // GB - 2))
                if prep and s == 0:
                    values(T + 1)
                if prep and 1 <= s <= CQ:
                    project(T + 1, 1, s - 1)

            over_groups(pe, slot)

            def turn(st, r, n):
                pe.wait_ge(s_xs[r], 16 * (n + 1))
                after(pe, s_xtc, st)
                for k in range(NBLK):
                    last = pe.transpose(pB[:, k * P:(k + 1) * P], xs[:, r, k, 0:E], ident[:, :])
                last.then_inc(s_xt, 1)

            turn(0, 0, 0)

            def expert_step(it, u):
                st = SU * it + u
                r = u % 2

                def hidden(c):
                    if c == 0:
                        pe.wait_ge(s_w, st + 1)
                        pe.wait_ge(s_xtc, st + 1)
                        after(pe, s_gelu, HC * (st - 1))
                    pe.matmul(hid_bank(r, c), w_ring[:, u, c * P:(c + 1) * P], xsT[:, r, :],
                              start=True, stop=True).then_inc(s_hid, 1)

                if live(st, STEPS):
                    hidden(0)
                    hidden(1)
                if live(st + 1, STEPS):
                    turn(st + 1, (u + 1) % SU, it + (u + 1) // SU)
                if live(st, STEPS):
                    hidden(2)
                    hidden(3)
                if live(st - 1, STEPS):
                    q = (u - 1) % 2
                    pe.wait_ge(s_gelu, HC * st)
                    after(pe, s_ysum, st - 1)
                    for k in range(NBLK):
                        for c in range(HC):
                            w = w_ring[:, (u - 1) % SU, HID + HC + c * E:HID + HC + (c + 1) * E]
                            last = pe.matmul(pO[:, k * E:(k + 1) * E], hidT[:, q, c, k * P:(k + 1) * P], w,
                                             start=(c == 0), stop=(c == HC - 1))
                    last.then_inc(s_y, 1)

            over_steps(pe, expert_step)


_INS = ["L0_attn_x", "L0_attn_Wq", "L0_attn_bq", "L0_attn_Wk", "L0_attn_bk", "L0_attn_Wv", "L0_attn_bv",
        "L0_ffn_w_gate", "L0_ffn_W1", "L0_ffn_b1", "L0_ffn_W2", "L0_ffn_b2", "L0_c", "L0_wmod"]
_OUTS = [((NB, S, E), "float32")]


def kernel(**inputs):
    import numpy as _np
    import concourse.bacc as _bacc
    from concourse import mybir as _mybir
    from concourse.bass_utils import run_bass_kernel_spmd as _run

    nc = _bacc.Bacc("TRN2", target_bir_lowering=False, num_devices=1)
    arrays, args = {}, []
    for name in _INS:
        a = _np.ascontiguousarray(inputs[name])
        arrays[f"in_{name}_dram"] = a
        args.append(nc.dram_tensor(f"in_{name}_dram", a.shape, _mybir.dt.from_np(a.dtype), kind="ExternalInput").ap())
    for i, (shape, dtype) in enumerate(_OUTS):
        dt = _mybir.dt.from_np(_np.dtype(dtype))
        args.append(nc.dram_tensor(f"out_{i}_dram", shape, dt, kind="ExternalOutput").ap())
    build(nc, *args)
    r = _run(nc, [arrays], core_ids=[0])
    return r.results[0]["out_0_dram"]
```

```python
from contextlib import ExitStack

import concourse.bass as bass
from concourse import mybir

P = 128
F32 = mybir.dt.float32
F32R = mybir.dt.float32r
BF16 = mybir.dt.bfloat16
I32 = mybir.dt.int32
ALU = mybir.AluOpType
ACT = mybir.ActivationFunctionType
AX_X = mybir.AxisListType.X

NB, S, E = 32, 256, 128
H, D = 16, 8
TOK = NB * S
WINDOW = 128
NBLK = S // WINDOW
HG = 4
GB = H // HG
CB = 2
CG = CB * GB
CT = CB * S
NT = CT // P
CHUNKS = NB // CB
GROUPS = CHUNKS * CG
R = S // H
C = S // R
CQ = C // 4
BODY = 2 * CG
BODIES = GROUPS // BODY
LAG = 15
SLOT = 32
SHIFT = 3 * D
NV = D + 1
EPS = 1e-5
MASKED = -1.0e30
U32 = mybir.dt.uint32
NE, TOPK = 8, 2
HID = 512
HC = HID // P
EXP = 2 * HID + HC + E
ROW = E + 2
TR = 256
REGION = TOK
STEPS = -(-(TOPK * TOK + NE * (TR - 1)) // (4 * TR)) * 4
SU = 4
TAB_STEPS = 20
POOL_SETUP = 31
FIN = 4
DVE_BIAS, DVE_SILU, DVE_WEIGHTS, DVE_MOD = 9, 21, 31, 51


def after(eng, sem, count):
    if not isinstance(count, int) or count > 0:
        eng.wait_ge(sem, count)


def live(i, n):
    return not isinstance(i, int) or 0 <= i < n


def over_groups(eng, slot):
    for g in range(BODY):
        slot(0, g)
    with eng.Fori(1, BODIES - 1) as it:
        for g in range(BODY):
            slot(it, g)
    for g in range(BODY):
        slot(BODIES - 1, g)
    for g in range(LAG):
        slot(BODIES, g)


NEWTON = 3
RSTD_STEPS = 3 + 3 * NEWTON


def rsqrt_guess(dve, sem, done, out, var, half):
    dve.tensor_scalar(half, var, EPS, None, ALU.add).then_inc(sem, 1)
    dve.wait_ge(sem, done + 1)
    dve.tensor_scalar(out.bitcast(I32), half.bitcast(I32), 1, None, ALU.logical_shift_right).then_inc(sem, 1)
    dve.wait_ge(sem, done + 2)
    dve.tensor_scalar(out.bitcast(I32), out.bitcast(I32), -1.0, float(0x5F3759DF - 2 ** 31), ALU.mult, ALU.add).then_inc(sem, 1)


def rsqrt_newton(dve, sem, done, k, out, half, tmp):
    done = done + 3 + 3 * k
    dve.wait_ge(sem, done)
    dve.tensor_tensor(tmp, out, out, ALU.mult).then_inc(sem, 1)
    dve.wait_ge(sem, done + 1)
    dve.scalar_tensor_tensor(out=tmp, in0=tmp, scalar=0.5, in1=half, op0=ALU.mult, op1=ALU.mult).then_inc(sem, 1)
    dve.wait_ge(sem, done + 2)
    dve.scalar_tensor_tensor(out=out, in0=tmp, scalar=-1.5, in1=out, op0=ALU.add, op1=ALU.mult).then_inc(sem, 1)


def over_steps(eng, step):
    bodies = STEPS // SU
    for u in range(SU):
        step(0, u)
    with eng.Fori(1, bodies - 1) as it:
        for u in range(SU):
            step(it, u)
    for u in range(SU):
        step(bodies - 1, u)
    step(bodies, 0)


def build(nc, x, wq, bq, wk, bk, wv, bv, w_gate, w1, b1, w2, b2, cond, wmod, out):
    with ExitStack() as ctx:
        def sb(name, shape, dt=F32):
            return ctx.enter_context(nc.sbuf_tensor(name, shape, dt))

        def passing(scope, name, shape, dt=F32):
            return scope.enter_context(nc.sbuf_tensor(name, shape, dt))

        def psum(name):
            return ctx.enter_context(nc.psum_tensor(name, [P, 512], F32))

        def sem(name):
            return ctx.enter_context(nc.semaphore(name))

        def dram(name, shape):
            return nc.dram_tensor(name, shape, F32, kind="Internal").ap()

        mod_rows = dram("mod_rows", [NB, 6, E])
        v_rows = dram("v_rows", [CHUNKS, CT, E])
        x_mid = dram("x_mid", [NB, S, E])

        x_expert = dram("x_expert", [NE * REGION, ROW])
        y_token = dram("y_token", [TOPK * TOK + TR, E])

        pS1 = [psum("pS1a"), psum("pS1b")]
        pS2 = [psum("pS2a"), psum("pS2b")]
        pO = psum("pO")
        pP = [psum("pPa"), psum("pPb")]
        pB = psum("pB")

        ident = sb("ident", [P, P])
        identb = sb("identb", [P, P], BF16)
        neg = sb("neg", [P, NBLK, P], BF16)
        tri = sb("tri", [P, NBLK, P])
        nfloor = sb("nfloor", [P, NBLK])
        row_id = sb("row_id", [P, 1], I32)
        row_bits = sb("row_bits", [P, 1], I32)
        low_mask = sb("low_mask", [P, 2])
        quad = sb("quad", [P, 1])
        bias_ind = sb("bias_ind", [P, 4, P], BF16)

        w_slot = sb("w_slot", [P, 2, C, SLOT])
        wvT = sb("wvT", [P, E])
        experts = sb("experts", [P, NE, EXP])
        bias_rep = experts[0:1, :, :].rearrange("o x n -> o (x n)")[:, 0:24 * 256].bitcast(BF16).rearrange(
            "o (r m) -> o r m", m=512)
        bias_lhs = sb("bias_lhs", [P, 2, CQ, P], BF16)
        bv_all = sb("bv_all", [P, E])
        scaleT = sb("scaleT", [P, 2, NB])
        shiftT = sb("shiftT", [P, 2, NB])

        x_in = sb("x_in", [P, 2, NT, E])
        stats = sb("stats", [P, NT, 6])
        mean_var = sb("mean_var", [P, NT, 2])
        rstd = sb("rstd", [P, NT])
        half_var = sb("half_var", [P, NT])
        r_tmp = sb("r_tmp", [P, NT])
        mean_off = sb("mean_off", [P, NT])
        xn = sb("xn", [P, NT, E])
        hT = sb("hT", [P, CT])
        rounded = sb("rounded", [P, 2, 4, P], F32R)
        v_tok = sb("v_tok", [P, NT, E])
        row_max = sb("row_max", [P, 2, HG, NBLK])
        nshift = sb("nshift", [P, 4, GB, HG, NBLK], F32R)
        nshiftT = sb("nshiftT", [HG * NBLK, 2, P], F32R)
        with ExitStack() as setup:
            w_nat = passing(setup, "w_nat", [P, 3, E])
            bias_row = passing(setup, "bias_row", [1, 2, E])
            bias_rest = passing(setup, "bias_rest", [1, 2, E])
            bias_part = passing(setup, "bias_part", [1, 3, 2, E], BF16)
            c_in = passing(setup, "c_in", [P, E])
            c_exp = passing(setup, "c_exp", [P, E])
            siluT = passing(setup, "siluT", [P, NB])
            wmod_sb = passing(setup, "wmod_sb", [P, 6, E])
            mod_sb = passing(setup, "mod_sb", [NB, 6, E])
            gate_sign = passing(setup, "gate_sign", [NB, 2, E])
            b1_rows = passing(setup, "b1_rows", [NE * HC, P])
            wg_rows = passing(setup, "wg_rows", [NE, E])
        probs = sb("probs", [P, 2, HG, NBLK * S])
        oT = sb("oT", [P, 2, S])
        o_rows = sb("o_rows", [P, 2, NBLK, H, NV])
        o_mask = sb("o_mask", [P, 2, NBLK, H, NV])
        o_tmp = sb("o_tmp", [P, NBLK, H, NV])
        e_arg = sb("e_arg", [P, 2, H * NBLK])
        e_shift = sb("e_shift", [P, 2, H * NBLK])
        rden = sb("rden", [P, 2, NBLK, H])
        x_res = sb("x_res", [P, 2, NBLK, E])
        ga_all = sb("ga_all", [P, 2, E])
        o_att = sb("o_att", [P, NBLK, E])
        x_new = sb("x_new", [P, 2, NBLK, E])

        cs_all = sb("cs_all", [P, 2, E])
        stats2 = sb("stats2", [P, NBLK, 6])
        mean_var2 = sb("mean_var2", [P, NBLK, 2])
        rstd2 = sb("rstd2", [P, NBLK])
        half_var2 = sb("half_var2", [P, NBLK])
        r_tmp2 = sb("r_tmp2", [P, NBLK])
        mean_off2 = sb("mean_off2", [P, NBLK])
        h2f = sb("h2f", [P, NBLK, E])
        h2_rows = sb("h2_rows", [P, 2, TOPK, NBLK, ROW])
        token_id = sb("token_id", [P, TOPK, NBLK])
        h2T = sb("h2T", [P, S])
        wgT = sb("wgT", [P, NE])
        logits = sb("logits", [P, NBLK, NE])
        top = sb("top", [P, NBLK, NE])
        top_at = sb("top_at", [P, NBLK, NE], U32)
        top_atf = sb("top_atf", [P, NBLK, TOPK])
        top_arg = sb("top_arg", [P, NBLK, NE])
        top_exp = sb("top_exp", [P, NBLK, NE])
        chosen = sb("chosen", [P, NBLK, TOPK, NE])
        chosen_b = sb("chosen_b", [P, NBLK, NE], BF16)
        expert_id = sb("expert_id", [P, NE])
        expert_idi = sb("expert_idi", [P, NE], I32)
        next_row = sb("next_row", [P, NE])
        place = sb("place", [P, NBLK, NE])
        place_of = sb("place_of", [P, NBLK, TOPK, NE])
        row_f = sb("row_f", [P, NBLK, TOPK])
        row_i = sb("row_i", [P, 2, NBLK, TOPK], I32)
        gate_sum = sb("gate_sum", [P, NBLK])
        gate_inv = sb("gate_inv", [P, NBLK])
        before_b = sb("before_b", [P, P], BF16)
        ones_b = sb("ones_b", [P, P], BF16)
        pad_rows = sb("pad_rows", [P, NBLK, ROW])
        pad_idi = sb("pad_idi", [P, NBLK], I32)
        pad_id = sb("pad_id", [P, NBLK])
        ones_row = sb("ones_row", [1, NE])
        step_idi = sb("step_idi", [1, STEPS], I32)
        step_id = sb("step_id", [1, STEPS])

        with ExitStack() as attention:
            q_pack = passing(attention, "q_pack", [P, CG, S], F32R)
            k_pack = passing(attention, "k_pack", [P, 2, CG, S], F32R)
            v_slot = passing(attention, "v_slot", [P, 2, NBLK, CG, HG, SLOT])
            q_diag = passing(attention, "q_diag", [P, 2, CG, HG, S], F32R)
        count_f = sb("count_f", [1, NE])
        tiles_i = sb("tiles_i", [1, NE], I32)
        tiles = sb("tiles", [1, NE])
        tiles_sum = sb("tiles_sum", [1, NE])
        past = sb("past", [1, STEPS, NE - 1])
        past_n = sb("past_n", [1, STEPS, NE - 1])
        step_expert = sb("step_expert", [1, STEPS])
        step_base = sb("step_base", [1, STEPS])
        step_lim = sb("step_lim", [1, STEPS])
        last_row = sb("last_row", [1, NE])
        last_more = sb("last_more", [1, NE - 1])
        past_row = sb("past_row", [1, STEPS, NE - 1])
        step_row = sb("step_row", [1, STEPS])
        table = sb("table", [1, 2, STEPS], I32)
        w_ring = sb("w_ring", [P, SU, EXP])
        xs = sb("xs", [P, SU, NBLK, ROW])
        hidT = sb("hidT", [P, 2, HC, TR])
        xsT = sb("xsT", [P, 2, TR])
        dest = sb("dest", [P, SU, NBLK], I32)
        y_sum = sb("y_sum", [P, 2, NBLK, E])
        y_out = sb("y_out", [P, 2, NBLK, E])
        fin_y = sb("fin_y", [P, FIN, TOPK, NT, E])
        fin_x = sb("fin_x", [P, CHUNKS, NT, E])
        fin_gb = sb("fin_gb", [P, FIN, CB, E])

        s_ld = sem("s_ld")
        s_pool0 = sem("s_pool0")
        s_dve0 = sem("s_dve0")
        s_act0 = sem("s_act0")
        s_pe0 = sem("s_pe0")
        s_biasl = sem("s_biasl")
        s_mod = sem("s_mod")
        s_x = [sem("s_x0"), sem("s_x1")]
        s_stats = sem("s_stats")
        s_aggr = sem("s_aggr")
        s_rstd = sem("s_rstd")
        s_off = sem("s_off")
        s_xn = sem("s_xn")
        s_pA = sem("s_pA")
        s_pB = sem("s_pB")
        s_hT = sem("s_hT")
        s_rq = sem("s_rq")
        s_rk = sem("s_rk")
        s_q = sem("s_q")
        s_k = sem("s_k")
        s_v = sem("s_v")
        s_vst = sem("s_vst")
        s_vr = sem("s_vr")
        s_qb = sem("s_qb")
        s_s1 = sem("s_s1")
        s_red = sem("s_red")
        s_nm = sem("s_nm")
        s_tm = sem("s_tm")
        s_tmcp = sem("s_tmcp")
        s_m = [sem("s_m0"), sem("s_m1")]
        s_s2 = sem("s_s2")
        s_exp = sem("s_exp")
        s_aff = sem("s_aff")
        s_pv = sem("s_pv")
        s_ot = sem("s_ot")
        s_to = sem("s_to")
        s_tocp = sem("s_tocp")
        s_mk = sem("s_mk")
        s_mkcp = sem("s_mkcp")
        s_earg = sem("s_earg")
        s_e = sem("s_e")
        s_f1 = sem("s_f1")
        s_f2 = sem("s_f2")
        s_den = sem("s_den")
        s_f3 = sem("s_f3")
        s_f4 = sem("s_f4")
        s_fin = sem("s_fin")
        s_xr = [sem("s_xr0"), sem("s_xr1")]
        s_st = [sem("s_st0"), sem("s_st1")]

        s_ldx = sem("s_ldx")
        s_cs = sem("s_cs")
        s_stats2 = sem("s_stats2")
        s_aggr2 = sem("s_aggr2")
        s_rstd2 = sem("s_rstd2")
        s_off2 = sem("s_off2")
        s_n2 = sem("s_n2")
        s_m2 = sem("s_m2")
        s_h2 = sem("s_h2")
        s_id = sem("s_id")
        s_dup = sem("s_dup")
        s_h2t = sem("s_h2t")
        s_h2c = sem("s_h2c")
        s_lg = sem("s_lg")
        s_lgc = sem("s_lgc")
        s_mx = sem("s_mx")
        s_ix = sem("s_ix")
        s_ein = sem("s_ein")
        s_ixf = sem("s_ixf")
        s_oh = sem("s_oh")
        s_ch = sem("s_ch")
        s_pre = sem("s_pre")
        s_pos = sem("s_pos")
        s_prod = sem("s_prod")
        s_rowf = sem("s_rowf")
        s_row = sem("s_row")
        s_eg = sem("s_eg")
        s_gsum = sem("s_gsum")
        s_ginv = sem("s_ginv")
        s_gate = sem("s_gate")
        s_sc = sem("s_sc")
        s_tab = sem("s_tab")
        s_pad = sem("s_pad")
        s_xs = [sem(f"s_xs{u}") for u in range(SU)]
        s_w = sem("s_w")
        s_xt = sem("s_xt")
        s_xtc = sem("s_xtc")
        s_hid = sem("s_hid")
        s_gelu = sem("s_gelu")
        s_y = sem("s_y")
        s_ysum = sem("s_ysum")
        s_dest = sem("s_dest")
        s_yout = sem("s_yout")
        s_ysc = sem("s_ysc")
        s_fx = sem("s_fx")
        s_fl = [sem(f"s_fl{r}") for r in range(FIN)]
        s_fa = sem("s_fa")
        s_fb = sem("s_fb")
        s_fc = sem("s_fc")
        s_fs = sem("s_fs")

        NLD = 8

        def hid_bank(r, c):
            bank = (pS1, pS2)[r][c // 2]
            return bank[:, (c % 2) * TR:(c % 2 + 1) * TR]

        def apart(eng, sem, count):
            if not isinstance(count, int):
                count = eng.to_reg(count)
                eng.wait_ge(s_ld, 16 * NLD)
            after(eng, sem, count)

        block = ctx.enter_context(nc.Block())

        x_tok = x.rearrange("b (k p) e -> b p k e", p=P)
        out_tok = out.rearrange("b (k p) e -> b p k e", p=P)
        x_mid_tok = x_mid.rearrange("b (k p) e -> b p k e", p=P)

        def rows_of(ap, i, n=1):
            return ap[bass.ds(i, n)]

        @block.sync
        def _(sp):
            for n, w in enumerate((wq, wk, wv)):
                sp.dma_start(w_nat[:, n, :], w).then_inc(s_ld, 16)
            for n, b in enumerate((bq, bk)):
                sp.dma_start(bias_row[0:1, n, :], b.rearrange("(o e) -> o e", o=1)).then_inc(s_ld, 16)
            sp.dma_start(bv_all[:, :], bv.rearrange("(o e) -> o e", o=1).to_broadcast([P, E])).then_inc(s_ld, 16)
            sp.wait_ge(s_pool0, 1)
            sp.dma_start(c_in[0:NB, :], cond).then_inc(s_ld, 16)
            sp.dma_start(wmod_sb[:, :, :], wmod.rearrange("k (m e) -> k m e", m=6)).then_inc(s_ld, 16)

            def load_x_at(t, par):
                apart(sp, s_xn, NT * (t - 1))
                sp.dma_start(x_in[:, par, :, :].rearrange("p (b k) e -> p b k e", b=CB),
                             rows_of(x_tok, CB * t, CB).rearrange("b p k e -> p b k e")).then_inc(s_x[par], 16)

            load_x_at(0, 0)
            load_x_at(1, 1)
            sp.wait_ge(s_pool0, 2)
            sp.wait_ge(s_dve0, DVE_BIAS)
            sp.dma_start(bias_lhs[0:12, :, :, :].rearrange("r n c m -> r n (c m)"),
                         bias_rep.rearrange("o (r n) m -> o r n m", n=2)).then_inc(s_biasl, 16)
            sp.wait_ge(s_biasl, 16)
            sp.dma_start(experts[:, :, 0:HID], w1.rearrange("x p n -> p x n")).then_inc(s_ldx, 16)
            for e in range(NE):
                sp.dma_start(experts[:, e, HID + HC:2 * HID + HC].rearrange("p (c d) -> p c d", c=HC),
                             w2[e].rearrange("(c p) d -> p c d", p=P)).then_inc(s_ldx, 16)
            sp.dma_start(experts[:, :, 2 * HID + HC:EXP],
                         b2.rearrange("(o x) d -> o x d", o=1).broadcast_to([P, NE, E])).then_inc(s_ldx, 16)
            sp.dma_start(b1_rows[:, :], b1.rearrange("x (c p) -> (x c) p", p=P)).then_inc(s_ldx, 16)
            sp.dma_start(wg_rows[:, :], w_gate).then_inc(s_ldx, 16)
            sp.wait_ge(s_dve0, DVE_MOD)
            sp.dma_start(mod_rows, mod_sb[:, :, :]).then_inc(s_mod, 16)
            sp.wait_ge(s_mod, 16)

            def store_v(u):
                apart(sp, s_v, u + 1)
                sp.dma_start(rows_of(v_rows, u).rearrange("o (a p) e -> p (o a) e", p=P),
                             v_tok[:, :, :]).then_inc(s_vst, 16)

            def load_v(u, par):
                apart(sp, s_pv, CG * (u - 1))
                apart(sp, s_mk, CB * (u - 1))
                apart(sp, s_vst, 16 * (u + 1))
                heads = rows_of(v_rows, u).rearrange("o t e -> (o t e)").rearrange(
                    "(h k p d) -> k p h d", k=NBLK, p=P, d=D)
                for k in range(NBLK):
                    sp.dma_start(v_slot[:, par, k, :, :, 0:D].rearrange("p g h d -> p (g h) d"),
                                 heads[k]).then_inc(s_vr, 16)

            def spread_q(u, par):
                apart(sp, s_q, CQ * (u + 1))
                apart(sp, s_s2, CG * HG * (u - 1))
                for h in range(HG):
                    rows = slice(SLOT * h, SLOT * h + SLOT)
                    sp.dma_start(q_diag[rows, par, :, h, :].bitcast(F32),
                                 q_pack[rows, :, :].bitcast(F32)).then_inc(s_qb, 16)

            store_v(0)
            load_v(0, 0)
            sp.wait_ge(s_pool0, 3)
            spread_q(0, 0)
            sp.wait_ge(s_pool0, POOL_SETUP)
            for e in range(NE):
                sp.dma_start(x_expert[e * REGION:e * REGION + TR].rearrange("(a p) w -> p a w", p=P),
                             pad_rows[:, :, :]).then_inc(s_pad, 16)

            def slot(it, g):
                G, T, s = BODY * it + g, 2 * it + g // CG, g % CG
                par = (g // CG) % 2
                if s == 2 and live(T + 2, CHUNKS):
                    load_x_at(T + 2, par)
                if live(G - 1, GROUPS):
                    apart(sp, s_tmcp, G)
                    gp = (g - 1) % BODY
                    for h in range(HG):
                        row = SLOT * h + SHIFT
                        sp.dma_start(
                            q_diag[row:row + 1, gp // CG, gp % CG, h, :].bitcast(F32).rearrange("o (k i) -> o k i", k=NBLK),
                            nshiftT[NBLK * h:NBLK * h + NBLK, (g - 1) % 2, :].bitcast(F32)).then_inc(s_m[(g - 1) % 2], 16)
                if s == 1 and live(T + 1, CHUNKS) and live(T, CHUNKS):
                    store_v(T + 1)
                if s == 4 and live(T + 1, CHUNKS) and live(T, CHUNKS):
                    load_v(T + 1, 1 - par)
                if s == 5 and live(T + 1, CHUNKS) and live(T, CHUNKS):
                    spread_q(T + 1, 1 - par)
                if g % GB == 2 and live(GB * it + g // GB - 2, NB):
                    B = GB * it + g // GB - 2
                    apart(sp, s_h2, B)
                    sp.dma_start(cs_all[:, :, :], rows_of(mod_rows, B)[:, 3:5, :].broadcast_to([P, 2, E])).then_inc(s_cs, 16)
                if g % GB == 1:
                    B = GB * it + g // GB
                    if live(B, NB):
                        apart(sp, s_fin, B - 1)
                        sp.dma_start(x_res[:, B_par(g), :, :],
                                     rows_of(x_tok, B).rearrange("b p k e -> p (b k) e")).then_inc(s_xr[B_par(g)], 16)
                        sp.dma_start(ga_all[:, B_par(g), :],
                                     rows_of(mod_rows, B)[:, 2, :].to_broadcast([P, E])).then_inc(s_xr[B_par(g)], 16)
                    if live(B - 2, NB):
                        apart(sp, s_fin, B - 1)
                        sp.dma_start(rows_of(x_mid_tok, B - 2).rearrange("b p k e -> p (b k) e"),
                                     x_new[:, B_par(g), :, :]).then_inc(s_st[B_par(g)], 16)

            def B_par(g):
                return (g // GB) % 2

            over_groups(sp, slot)
            for b in range(2):
                sp.wait_ge(s_st[b], 16 * NB // 2)

            sp.wait_ge(s_tab, TAB_STEPS)
            sp.wait_ge(s_sc, 16 * NB * NBLK * TOPK)

            def last_load(t, r):
                for k in range(TOPK):
                    sp.dma_start(fin_y[:, r, k, :, :],
                                 y_token[k * TOK:(k + 1) * TOK].rearrange("(t a p) e -> t p a e", a=NT, p=P)[
                                     bass.ds(t, 1)].rearrange("t p a e -> p (t a) e")).then_inc(s_fl[r], 16)
                sp.dma_start(fin_gb[:, r, :, :], rows_of(mod_rows, CB * t, CB)[:, 5, :].rearrange(
                    "(o b) e -> o b e", o=1).broadcast_to([P, CB, E])).then_inc(s_fl[r], 16)

            def last_store(t):
                apart(sp, s_fc, t + 1)
                sp.dma_start(rows_of(out_tok, CB * t, CB).rearrange("b p k e -> p b k e"),
                             fin_x[:, bass.ds(t, 1), :, :].rearrange("p o (b k) e -> p (o b) k e", b=CB)).then_inc(s_fs, 16)

            def tile_load(it, u):
                st = SU * it + u
                if not live(st, STEPS):
                    return
                row = sp.value_load(table[0:1, 0, bass.ds(st, 1)], min_val=0, max_val=NE * REGION - TR)
                apart(sp, s_yout, NBLK * (st - SU + 1))
                sp.dma_start(xs[:, u, :, :],
                             x_expert[bass.ds(row, TR)].rearrange("(a p) w -> p a w", p=P)).then_inc(s_xs[u], 16)

            for u in range(SU):
                tile_load(0, u)
            for t in range(CHUNKS):
                sp.dma_start(fin_x[:, t, :, :].rearrange("p (b k) e -> p b k e", b=CB),
                             x_mid_tok[CB * t:CB * t + CB].rearrange("b p k e -> p b k e")).then_inc(s_fx, 16)
            with sp.Fori(1, STEPS // SU) as it:
                for u in range(SU):
                    tile_load(it, u)
            sp.wait_ge(s_ysc, 16 * NBLK * STEPS)

            for r in range(FIN):
                last_load(r, r)
            with sp.Fori(0, CHUNKS // FIN - 1) as it:
                for r in range(FIN):
                    last_store(FIN * it + r)
                    last_load(FIN * it + FIN + r, r)
            for r in range(FIN):
                last_store(CHUNKS - FIN + r)
            sp.wait_ge(s_fs, 16 * CHUNKS)

        @block.gpsimd
        def _(pool):
            pool.memset(c_in[:, :], 0.0).then_inc(s_pool0, 1)
            pool.memset(bias_lhs[:, :, :, :], 0.0).then_inc(s_pool0, 1)
            pool.memset(q_diag[:, :, :, :, :].bitcast(F32).rearrange("p a g h i -> p (a g h i)"), 0.0).then_inc(s_pool0, 1)
            pool.memset(ident[:, :], 0.0).then_inc(s_pool0, 1)
            pool.memset(tri[:, :, :], 1.0).then_inc(s_pool0, 1)
            pool.memset(neg[:, :, :], 0.0).then_inc(s_pool0, 1)
            pool.memset(nfloor[:, :], 0.0).then_inc(s_pool0, 1)
            pool.memset(v_slot[:, :, :, :, :, :].rearrange("p a k g h d -> p (a k g h d)"), 0.0).then_inc(s_pool0, 1)
            pool.iota(row_id[:, :], pattern=[[0, 1]], base=0, channel_multiplier=1).then_inc(s_pool0, 1)
            pool.wait_ge(s_pool0, 9)
            pool.memset(v_slot[:, :, :, :, :, D:D + 1].rearrange("p a k g h d -> p (a k g h) d"), 1.0).then_inc(s_pool0, 1)
            pool.affine_select(out=ident[:, :], in_=ident[:, :], compare_op=ALU.not_equal, fill=1.0, base=0,
                               pattern=[[-1, P]], channel_multiplier=1).then_inc(s_pool0, 1)
            pool.affine_select(out=tri[:, 0, :], in_=tri[:, 0, :], compare_op=ALU.is_ge, fill=0.0, base=0,
                               pattern=[[-1, P]], channel_multiplier=1).then_inc(s_pool0, 1)
            pool.affine_select(out=tri[:, 1, :], in_=tri[:, 1, :], compare_op=ALU.is_ge, fill=0.0, base=-1,
                               pattern=[[1, P]], channel_multiplier=-1).then_inc(s_pool0, 1)
            pool.affine_select(out=neg[:, 0, :], in_=neg[:, 0, :], compare_op=ALU.is_gt, fill=MASKED, base=0,
                               pattern=[[-1, P]], channel_multiplier=1).then_inc(s_pool0, 1)
            pool.affine_select(out=neg[:, 1, :], in_=neg[:, 1, :], compare_op=ALU.is_ge, fill=MASKED, base=0,
                               pattern=[[1, P]], channel_multiplier=-1).then_inc(s_pool0, 1)
            pool.affine_select(out=nfloor[:, 1:2], in_=nfloor[:, 1:2], compare_op=ALU.not_equal, fill=-MASKED, base=0,
                               pattern=[[0, 1]], channel_multiplier=1).then_inc(s_pool0, 1)
            pool.wait_ge(s_pool0, 16)
            pool.tensor_copy(identb[:, :], ident[:, :]).then_inc(s_pool0, 1)
            pool.tensor_copy(before_b[:, :], tri[:, 1, :]).then_inc(s_pool0, 1)
            pool.memset(ones_b[:, :], 1.0).then_inc(s_pool0, 1)
            pool.memset(ones_row[:, :], 1.0).then_inc(s_pool0, 1)
            pool.memset(pad_rows[:, :, :], 0.0).then_inc(s_pool0, 1)
            pool.iota(expert_idi[:, :], pattern=[[1, NE]], base=0, channel_multiplier=0).then_inc(s_pool0, 1)
            pool.iota(pad_idi[:, :], pattern=[[P, NBLK]], base=0, channel_multiplier=1).then_inc(s_pool0, 1)
            pool.iota(step_idi[:, :], pattern=[[1, STEPS]], base=0, channel_multiplier=0).then_inc(s_pool0, 1)
            pool.wait_ge(s_pool0, 24)
            pool.tensor_copy(pad_id[:, :], pad_idi[:, :]).then_inc(s_pool0, 1)
            pool.tensor_copy(expert_id[:, :], expert_idi[:, :]).then_inc(s_pool0, 1)
            pool.tensor_copy(step_id[:, :], step_idi[:, :]).then_inc(s_pool0, 1)
            pool.wait_ge(s_pool0, 27)
            for k in range(TOPK):
                pool.tensor_scalar(token_id[:, k, :], pad_id[:, :], float(k * TOK), None, ALU.add).then_inc(s_pool0, 1)
            pool.tensor_scalar(pad_rows[:, :, E], pad_id[:, :], float(TOPK * TOK), None, ALU.add).then_inc(s_pool0, 1)
            pool.tensor_scalar(next_row[:, :], expert_id[:, :], float(REGION), None, ALU.mult).then_inc(s_pool0, 1)

            def slot(it, g):
                G, T, s = BODY * it + g, 2 * it + g // CG, g % CG
                par = (g // CG) % 2
                if live(G - 2, GROUPS):
                    apart(pool, s_exp, HG * (G - 1))
                    pr = probs[:, g % 2, :, :]
                    pool.affine_select(out=pr[:, :, P:2 * P], in_=pr[:, :, P:2 * P], compare_op=ALU.is_ge, fill=0.0,
                                       base=0, pattern=[[0, HG], [-1, P]], channel_multiplier=1).then_inc(s_aff, 1)
                    pool.affine_select(out=pr[:, :, 2 * P:3 * P], in_=pr[:, :, 2 * P:3 * P], compare_op=ALU.is_ge,
                                       fill=0.0, base=-1, pattern=[[0, HG], [1, P]],
                                       channel_multiplier=-1).then_inc(s_aff, 1)
                if g % GB in (1, 2) and live(GB * it + g // GB - 4, NB):
                    B, b = GB * it + g // GB - 4, (g // GB) % 2
                    if isinstance(G, int) and B == 0 and g % GB == 1:
                        pool.wait_ge(s_pad, 16 * NE)
                    if g % GB == 1:
                        apart(pool, s_row, B + 1)
                        apart(pool, s_gate, B + 1)
                        apart(pool, s_dup, B + 1)
                    k = g % GB - 1
                    for e in range(TOPK):
                        pool.indirect_dma_start(x_expert[:, :], bass.IndirectOffsetOnAxis(ap=row_i[:, b, k, e:e + 1], axis=0),
                                                h2_rows[:, b, e, k, :], None).then_inc(s_sc, 16)
                if g % GB == 3 and live(GB * it + g // GB - 1, NB):
                    B = GB * it + g // GB - 1
                    b = (g // GB - 1) % 2
                    apart(pool, s_mkcp, B + 1)
                    apart(pool, s_e, B + 1)
                    for k in range(NBLK):
                        e_k = e_shift[:, b, :].rearrange("p (n k) -> p k n", k=NBLK)[:, k, :]
                        pool.tensor_tensor(o_tmp[:, k, :, :], o_mask[:, b, k, :, :],
                                           e_k.unsqueeze(2).broadcast_to([P, H, NV]), ALU.mult).then_inc(s_f1, 1)
                    apart(pool, s_f1, NBLK * (B + 1))
                    apart(pool, s_tocp, GB * (B + 1))
                    rows = o_rows[:, b, :, :, :].rearrange("p k h v -> p (k h v)")
                    pool.tensor_tensor(rows, rows, o_tmp[:, :, :, :].rearrange("p k h v -> p (k h v)"),
                                       ALU.add).then_inc(s_f2, 1)
                if g % GB == 3 and live(GB * it + g // GB - 2, NB):
                    B, b = GB * it + g // GB - 2, (g // GB) % 2
                    apart(pool, s_n2, NBLK * (B + 1))
                    apart(pool, s_cs, 16 * (B + 1))
                    pool.tensor_tensor(h2f[:, :, :], h2f[:, :, :], cs_all[:, 1, :].unsqueeze(1).broadcast_to([P, NBLK, E]),
                                       ALU.mult).then_inc(s_m2, 1)
                    apart(pool, s_m2, B + 1)
                    apart(pool, s_sc, 16 * NBLK * TOPK * (B - 1))
                    pool.tensor_tensor(h2_rows[:, b, 0, :, 0:E], h2f[:, :, :],
                                       cs_all[:, 0, :].unsqueeze(1).broadcast_to([P, NBLK, E]), ALU.add).then_inc(s_h2, 1)
                    apart(pool, s_id, 2 * B)
                    pool.tensor_copy(h2_rows[:, b, :, :, E], token_id[:, :, :]).then_inc(s_id, 1)
                    apart(pool, s_id, 2 * B + 1)
                    pool.tensor_scalar(token_id[:, :, :], token_id[:, :, :], float(S), None, ALU.add).then_inc(s_id, 1)
                if g % GB == 0 and live(GB * it + g // GB - 2, NB):
                    B = GB * it + g // GB - 2
                    b = (g // GB) % 2
                    apart(pool, s_den, B + 1)
                    rd = rden[:, b, :, :].rearrange("p k h -> p (k h)")
                    apart(pool, s_fin, B)
                    pool.tensor_tensor(o_att[:, :, :].rearrange("p k (h d) -> p (k h) d", d=D),
                                       o_rows[:, b, :, :, 0:D].rearrange("p k h d -> p (k h) d"),
                                       rd.unsqueeze(2).broadcast_to([P, NBLK * H, D]), ALU.mult).then_inc(s_f3, 1)
                    apart(pool, s_f3, B + 1)
                    apart(pool, s_xr[b], 32 * (2 * it + (g // GB - 2) // 2 + 1))
                    pool.tensor_tensor(o_att[:, :, :], o_att[:, :, :],
                                       ga_all[:, b, :].unsqueeze(1).broadcast_to([P, NBLK, E]), ALU.mult).then_inc(s_f4, 1)
                    apart(pool, s_f4, B + 1)
                    apart(pool, s_st[b], 16 * (2 * it + (g // GB - 2) // 2))
                    pool.tensor_tensor(x_new[:, b, :, :], o_att[:, :, :], x_res[:, b, :, :], ALU.add).then_inc(s_fin, 1)

            over_groups(pool, slot)

            def scatter_y(it, u):
                st = SU * it + u - 1
                if not live(st, STEPS):
                    return
                apart(pool, s_yout, NBLK * (st + 1))
                apart(pool, s_dest, st + 1)
                apart(pool, s_ysc, 16 * NBLK * st)
                for k in range(NBLK):
                    pool.indirect_dma_start(y_token[:, :], bass.IndirectOffsetOnAxis(ap=dest[:, (u - 1) % SU, k:k + 1], axis=0),
                                            y_out[:, (u - 1) % 2, k, :], None).then_inc(s_ysc, 16)

            over_steps(pool, scatter_y)

        @block.vector
        def _(dve):
            dve0 = [0]

            def step(ins):
                dve0[0] += 1
                ins.then_inc(s_dve0, 1)
                dve.wait_ge(s_dve0, dve0[0])

            dve.wait_ge(s_ld, 16 * NLD)
            step(dve.memset(bias_rep, 0.0))
            step(dve.tensor_scalar(bias_row[:, 0, :], bias_row[:, 0, :], float(D) ** -0.5, None, ALU.mult))
            step(dve.tensor_copy(bias_part[:, 0, :, :], bias_row[:, :, :]))
            step(dve.tensor_tensor(bias_rest[:, :, :], bias_row[:, :, :], bias_part[:, 0, :, :], ALU.subtract))
            step(dve.tensor_copy(bias_part[:, 1, :, :], bias_rest[:, :, :]))
            step(dve.tensor_tensor(bias_rest[:, :, :], bias_rest[:, :, :], bias_part[:, 1, :, :], ALU.subtract))
            step(dve.tensor_copy(bias_part[:, 2, :, :], bias_rest[:, :, :]))
            for a in range(3):
                for c in range(4):
                    for n in range(2):
                        for part in range(3):
                            for cq in range(CQ):
                                src = bias_part[:, a, n, (4 * cq + c) * D:(4 * cq + c + 1) * D]
                                dst = bias_rep[:, (a * 4 + c) * 2 + n, cq * P:(cq + 1) * P].rearrange("o (h m) -> o h m", h=HG)
                                last = dve.tensor_copy(dst[:, :, part * D:(part + 1) * D],
                                                       src.unsqueeze(1).broadcast_to([1, HG, D]))
            step(last)
            step(dve.memset(bias_rep.rearrange("o (r n) m -> o r n m", n=2)[:, 0:4, 1, :].rearrange(
                "o c (g m) -> o c g m", m=SLOT)[:, :, :, SHIFT:SHIFT + 1], 1.0))
            assert dve0[0] == DVE_BIAS
            dve.wait_ge(s_pool0, 9)
            step(dve.tensor_scalar(row_bits[:, :], row_id[:, :], 24, None, ALU.bitwise_and))
            step(dve.tensor_scalar(low_mask[:, 0:1], row_bits[:, :], 16.0, -1.0, ALU.is_equal, ALU.mult))
            step(dve.tensor_scalar(low_mask[:, 1:2], row_bits[:, :], 8.0, -1.0, ALU.is_equal, ALU.mult))
            step(dve.tensor_scalar(row_bits[:, :], row_id[:, :], 3, None, ALU.bitwise_and))
            step(dve.tensor_copy(quad[:, :], row_bits[:, :]))
            for c in range(4):
                step(dve.tensor_scalar(bias_ind[:, c, :], quad[:, 0:1].broadcast_to([P, P]), float(c), None, ALU.is_equal))
            dve.wait_ge(s_act0, 1)
            step(dve.tensor_scalar(c_exp[:, :], c_exp[:, :], 1.0, None, ALU.add))
            step(dve.reciprocal(c_exp[:, :], c_exp[:, :]))
            step(dve.tensor_tensor(c_in[:, :], c_in[:, :], c_exp[:, :], ALU.mult))
            assert dve0[0] == DVE_SILU
            dve.wait_ge(s_pe0, 1)
            for n in range(2):
                view = pP[0][:, n * P:(n + 1) * P].rearrange("p (c d) -> p c d", d=D)
                scale = float(D) ** -0.5 if n == 0 else 1.0
                step(dve.memset(w_slot[:, n, :, SHIFT:SLOT], 0.0))
                for part in range(3):
                    step(dve.tensor_scalar(w_slot[:, n, :, part * D:(part + 1) * D], view, scale, None, ALU.mult))
            step(dve.tensor_copy(wvT[:, :], pP[0][:, 2 * P:3 * P]))
            step(dve.tensor_copy(siluT[:, :], pP[0][:, 3 * P:3 * P + NB]))
            assert dve0[0] == DVE_WEIGHTS
            dve.wait_ge(s_pe0, 2)
            for half in range(2):
                step(dve.tensor_copy(mod_sb[:, 3 * half:3 * half + 3, :].rearrange("b m e -> b (m e)"),
                                     pP[half][0:NB, 0:3 * E]))
            for half in range(2):
                scale_m, gate_m = 3 * half + 1, 3 * half + 2
                step(dve.tensor_scalar(mod_sb[:, scale_m, :], mod_sb[:, scale_m, :], 1.0, None, ALU.add))
                step(dve.tensor_scalar(gate_sign[:, half, :], mod_sb[:, gate_m, :], 0.0, 2.0, ALU.is_ge, ALU.mult))
                step(dve.tensor_scalar(gate_sign[:, half, :], gate_sign[:, half, :], -1.0, None, ALU.add))
                step(dve.tensor_tensor(mod_sb[:, gate_m, :], mod_sb[:, gate_m, :], gate_sign[:, half, :], ALU.mult))
                step(dve.tensor_scalar(mod_sb[:, gate_m, :], mod_sb[:, gate_m, :], 0.25, None, ALU.max))
                step(dve.tensor_tensor(mod_sb[:, gate_m, :], mod_sb[:, gate_m, :], gate_sign[:, half, :], ALU.mult))
            for half in range(2):
                step(dve.tensor_copy(shiftT[:, half, :], pB[:, (2 * half) * NB:(2 * half + 1) * NB]))
                step(dve.tensor_scalar(scaleT[:, half, :], pB[:, (2 * half + 1) * NB:(2 * half + 2) * NB], 1.0, None, ALU.add))
            dve.wait_ge(s_pe0, 3)
            step(dve.tensor_copy(experts[:, :, HID:HID + HC], pP[0][:, 0:NE * HC].rearrange("p (x c) -> p x c", c=HC)))
            step(dve.tensor_copy(wgT[:, :], pP[0][:, NE * HC:NE * HC + NE]))
            assert dve0[0] == DVE_MOD

            def layer_stats(t, par, n):
                dve.wait_ge(s_x[par], 16 * (n + 1))
                after(dve, s_aggr, NT * t)
                for a in range(NT):
                    dve.bn_stats(stats[:, a, :], x_in[:, par, a, :]).then_inc(s_stats, 1)

            def layer_mean(t):
                apart(dve, s_stats, NT * (t + 1))
                apart(dve, s_off, t)
                for a in range(NT):
                    dve.bn_aggr(mean_var[:, a, :], stats[:, a, :]).then_inc(s_aggr, 1)

            def layer_guess(t):
                dve.wait_ge(s_aggr, NT * (t + 1))
                after(dve, s_xn, NT * t)
                rsqrt_guess(dve, s_rstd, RSTD_STEPS * t, rstd[:, :], mean_var[:, :, 1], half_var[:, :])

            def layer_newton(t, k):
                rsqrt_newton(dve, s_rstd, RSTD_STEPS * t, k, rstd[:, :], half_var[:, :], r_tmp[:, :])

            def layer_offset(t):
                dve.wait_ge(s_rstd, RSTD_STEPS * (t + 1))
                dve.scalar_tensor_tensor(out=mean_off[:, :], in0=mean_var[:, :, 0], scalar=-1.0, in1=rstd[:, :],
                                         op0=ALU.mult, op1=ALU.mult).then_inc(s_off, 1)

            def layer_terms(t, par, n):
                layer_stats(t, par, n)
                layer_mean(t)
                layer_guess(t)
                for k in range(NEWTON):
                    layer_newton(t, k)
                layer_offset(t)

            def values(u):
                dve.wait_ge(s_pB, (CQ + 1) * u + 1)
                after(dve, s_vst, 16 * u)
                dve.tensor_tensor(v_tok[:, :, :], pP[1][:, :].rearrange("p (a e) -> p a e", a=NT),
                                  bv_all[:, :].unsqueeze(1).broadcast_to([P, NT, E]), ALU.add).then_inc(s_v, 1)

            def pack(u, n, i, par):
                if n == 0:
                    dve.wait_ge(s_rq, CQ * u + i + 1)
                    if i == 0:
                        after(dve, s_qb, 16 * HG * u)
                    dst = q_pack[:, :, :]
                else:
                    dve.wait_ge(s_rk, CQ * u + i + 1)
                    if i == 0:
                        after(dve, s_s2, CG * HG * (u - 1))
                    dst = k_pack[:, par, :, :]
                dst = dst.rearrange("p g i -> p (g i)").rearrange("p (n c) -> p c n", c=C)[:, 4 * i:4 * i + 4, :]
                dve.scalar_tensor_tensor(out=dst, in0=rounded[:, n, :, :].bitcast(F32), scalar=low_mask[:, n:n + 1],
                                         in1=pP[n][:, :].rearrange("p (c n) -> p c n", c=4),
                                         op0=ALU.mult, op1=ALU.add).then_inc(s_q if n == 0 else s_k, 1)

            def batch_stats(B, b):
                dve.wait_ge(s_fin, B + 1)
                after(dve, s_aggr2, NBLK * B)
                for k in range(NBLK):
                    dve.bn_stats(stats2[:, k, :], x_new[:, b, k, :]).then_inc(s_stats2, 1)

            def batch_mean(B):
                apart(dve, s_stats2, NBLK * (B + 1))
                apart(dve, s_off2, B)
                for k in range(NBLK):
                    dve.bn_aggr(mean_var2[:, k, :], stats2[:, k, :]).then_inc(s_aggr2, 1)

            def batch_guess(B):
                dve.wait_ge(s_aggr2, NBLK * (B + 1))
                after(dve, s_n2, NBLK * B)
                rsqrt_guess(dve, s_rstd2, RSTD_STEPS * B, rstd2[:, :], mean_var2[:, :, 1], half_var2[:, :])

            def batch_newton(B, k):
                rsqrt_newton(dve, s_rstd2, RSTD_STEPS * B, k, rstd2[:, :], half_var2[:, :], r_tmp2[:, :])

            def batch_offset(B):
                dve.wait_ge(s_rstd2, RSTD_STEPS * (B + 1))
                dve.scalar_tensor_tensor(out=mean_off2[:, :], in0=mean_var2[:, :, 0], scalar=-1.0, in1=rstd2[:, :],
                                         op0=ALU.mult, op1=ALU.mult).then_inc(s_off2, 1)

            def take_logits(B):
                dve.wait_ge(s_lg, B + 1)
                dve.tensor_copy(logits[:, :, :].rearrange("p k x -> p (k x)"), pO[:, S:S + NBLK * NE]).then_inc(s_lgc, 1)

            def largest(B):
                apart(dve, s_lgc, B + 1)
                for k in range(NBLK):
                    dve.max(top[:, k, :], logits[:, k, :]).then_inc(s_mx, 1)

            def largest_at(B):
                apart(dve, s_mx, NBLK * (B + 1))
                for k in range(NBLK):
                    dve.max_index(top_at[:, k, :], top[:, k, :], logits[:, k, :]).then_inc(s_ix, 1)
                after(dve, s_eg, B)
                dve.tensor_tensor(top_arg[:, :, :], top[:, :, :], top[:, :, 0:1].broadcast_to([P, NBLK, NE]),
                                  ALU.subtract).then_inc(s_ein, 1)
                dve.wait_ge(s_ix, NBLK * (B + 1))
                dve.tensor_copy(top_atf[:, :, :], top_at[:, :, 0:TOPK]).then_inc(s_ixf, 1)

            def mark_chosen(B):
                dve.wait_ge(s_ixf, B + 1)
                for k in range(NBLK):
                    dve.tensor_tensor(chosen[:, k, :, :], expert_id[:, :].unsqueeze(1).broadcast_to([P, TOPK, NE]),
                                      top_atf[:, k, :].unsqueeze(2).broadcast_to([P, TOPK, NE]), ALU.is_equal).then_inc(s_oh, 1)
                dve.wait_ge(s_oh, NBLK * (B + 1))
                dve.tensor_tensor(chosen_b[:, :, :], chosen[:, :, 0, :], chosen[:, :, 1, :], ALU.add).then_inc(s_ch, 1)

            def places(B):
                dve.wait_ge(s_pre, B + 1)
                dve.tensor_tensor(place[:, :, :], pO[:, S:S + NBLK * NE].rearrange("p (k x) -> p k x", k=NBLK),
                                  next_row[:, :].unsqueeze(1).broadcast_to([P, NBLK, NE]), ALU.add).then_inc(s_pos, 1)
                dve.wait_ge(s_pos, 2 * B + 1)
                dve.tensor_tensor(next_row[:, :], pO[:, S + NBLK * NE:S + (NBLK + 1) * NE], next_row[:, :],
                                  ALU.add).then_inc(s_pos, 1)

            def chosen_places(B):
                for k in range(NBLK):
                    dve.tensor_tensor(place_of[:, k, :, :], chosen[:, k, :, :],
                                      place[:, k, :].unsqueeze(1).broadcast_to([P, TOPK, NE]), ALU.mult).then_inc(s_prod, 1)

            def rows_f(B):
                dve.wait_ge(s_prod, NBLK * (B + 1))
                dve.tensor_reduce(row_f[:, :, :].rearrange("p k e -> p (k e)"),
                                  place_of[:, :, :, :].rearrange("p k e x -> p (k e) x"), AX_X, ALU.add).then_inc(s_rowf, 1)

            def rows_i(B, b):
                dve.wait_ge(s_rowf, B + 1)
                dve.tensor_copy(row_i[:, b, :, :], row_f[:, :, :]).then_inc(s_row, 1)

            def gate_sums(B):
                dve.wait_ge(s_eg, B + 1)
                dve.tensor_reduce(gate_sum[:, :], top_exp[:, :, :], AX_X, ALU.add).then_inc(s_gsum, 1)

            def gate_inverse(B):
                dve.wait_ge(s_gsum, B + 1)
                dve.reciprocal(gate_inv[:, :], gate_sum[:, :]).then_inc(s_ginv, 1)

            def gates(B, b):
                dve.wait_ge(s_ginv, B + 1)
                dve.tensor_tensor(h2_rows[:, b, :, :, E + 1].rearrange("p e k -> p k e"), top_exp[:, :, 0:TOPK],
                                  gate_inv[:, :].unsqueeze(2).broadcast_to([P, NBLK, TOPK]), ALU.mult).then_inc(s_gate, 1)

            dve.wait_ge(s_pool0, POOL_SETUP)
            layer_terms(0, 0, 0)
            values(0)
            for i in range(CQ):
                pack(0, 0, i, 0)
                pack(0, 1, i, 0)
            layer_terms(1, 1, 0)

            def slot(it, g):
                G, T, s = BODY * it + g, 2 * it + g // CG, g % CG
                par = (g // CG) % 2
                prep = live(T + 1, CHUNKS) and live(T, CHUNKS)

                def maxima(h):
                    dve.wait_ge(s_s1, HG * G + h + 1)
                    dve.tensor_reduce(row_max[:, g % 2, h, :], pS1[h % 2][:, :].rearrange("p (k j) -> p k j", k=NBLK),
                                      AX_X, ALU.max).then_inc(s_red, 1)

                B, j = GB * it + g // GB, g % GB
                b = (g // GB) % 2

                if live(G, GROUPS):
                    maxima(0)
                if j == 2 and live(B - 3, NB):
                    take_logits(B - 3)
                    largest(B - 3)
                if j == 3 and live(B - 3, NB):
                    places(B - 3)
                if j == 0 and live(B - 4, NB):
                    rows_i(B - 4, b)
                    gates(B - 4, b)
                if j == 3 and live(B - 2, NB):
                    batch_newton(B - 2, 1)
                if s == 5 and live(T + 2, CHUNKS):
                    layer_mean(T + 2)
                if s == 6 and live(T + 2, CHUNKS):
                    layer_offset(T + 2)
                if live(G, GROUPS):
                    maxima(1)
                if prep and 2 <= s <= CQ + 1:
                    pack(T + 1, 1, s - 2, 1 - par)
                if j == 0 and live(B - 1, NB):
                    dve.wait_ge(s_nm, GB * B)
                    after(dve, s_f1, NBLK * (B - 2))
                    dve.tensor_scalar(e_arg[:, (g // GB - 1) % 2, :],
                                      nshift[:, (g // GB - 1) % 4, :, :, :].bitcast(F32).rearrange("p g h k -> p (g h k)"),
                                      0.0, None, ALU.min).then_inc(s_earg, 1)
                if j == 2 and live(B - 3, NB):
                    largest_at(B - 3)
                if j == 3 and live(B - 3, NB):
                    chosen_places(B - 3)
                    gate_sums(B - 3)
                if j == 3 and live(B - 2, NB):
                    batch_newton(B - 2, 2)
                if s == 5 and live(T + 2, CHUNKS):
                    layer_guess(T + 2)
                if live(G, GROUPS):
                    maxima(2)
                if j == 2 and live(B - 3, NB):
                    mark_chosen(B - 3)
                if j == 2 and live(B - 2, NB):
                    batch_guess(B - 2)
                if j == 3 and live(B - 2, NB):
                    batch_offset(B - 2)
                if j == 3 and live(B - 3, NB):
                    rows_f(B - 3)
                    gate_inverse(B - 3)
                if j == 1 and live(B - 2, NB):
                    batch_stats(B - 2, b)
                if s == 5 and live(T + 2, CHUNKS):
                    layer_newton(T + 2, 0)
                if j == 0 and live(B - 2, NB):
                    dve.wait_ge(s_f2, B - 1)
                    dve.reciprocal(rden[:, b, :, :].rearrange("p k h -> p (k h)"),
                                   o_rows[:, b, :, :, D].rearrange("p k h -> p (k h)")).then_inc(s_den, 1)
                if live(G, GROUPS):
                    maxima(3)
                    dve.wait_ge(s_red, HG * G + HG)
                    dve.scalar_tensor_tensor(out=nshift[:, (g // GB) % 4, g % GB, :, :], in0=row_max[:, g % 2, :, :],
                                             scalar=-1.0, in1=nfloor[:, :].unsqueeze(1).broadcast_to([P, HG, NBLK]),
                                             op0=ALU.mult, op1=ALU.min).then_inc(s_nm, 1)
                if prep and 1 <= s <= CQ:
                    pack(T + 1, 0, s - 1, 1 - par)
                if prep and s == 0:
                    values(T + 1)
                if j == 1 and live(B - 2, NB):
                    batch_mean(B - 2)
                if j == 2 and live(B - 2, NB):
                    batch_newton(B - 2, 0)
                if s == 4 and live(T + 2, CHUNKS):
                    layer_stats(T + 2, par, it + 1)
                if s == 5 and live(T + 2, CHUNKS):
                    layer_newton(T + 2, 1)
                    layer_newton(T + 2, 2)

            over_groups(dve, slot)

            dve.wait_ge(s_pos, 2 * NB)
            tab = [0]

            def entry(ins):
                tab[0] += 1
                ins.then_inc(s_tab, 1)
                dve.wait_ge(s_tab, tab[0])

            entry(dve.scalar_tensor_tensor(out=count_f[:, :], in0=expert_id[0:1, :], scalar=-float(REGION),
                                           in1=next_row[0:1, :], op0=ALU.mult, op1=ALU.add))
            entry(dve.tensor_scalar(tiles_i[:, :], count_f[:, :], float(TR - 1), None, ALU.add))
            entry(dve.tensor_scalar(tiles_i[:, :], tiles_i[:, :], TR.bit_length() - 1, None, ALU.logical_shift_right))
            entry(dve.tensor_copy(tiles[:, :], tiles_i[:, :]))
            entry(dve.tensor_tensor_scan(tiles_sum[:, :], ones_row[:, :], tiles[:, :], 0.0, ALU.mult, ALU.add))
            steps_of = step_id[:, :].unsqueeze(2).broadcast_to([1, STEPS, NE - 1])
            entry(dve.tensor_tensor(past[:, :, :], steps_of, tiles_sum[:, 0:NE - 1].unsqueeze(1).broadcast_to(
                [1, STEPS, NE - 1]), ALU.is_ge))
            entry(dve.tensor_tensor(past_n[:, :, :], past[:, :, :], tiles[:, 0:NE - 1].unsqueeze(1).broadcast_to(
                [1, STEPS, NE - 1]), ALU.mult))
            entry(dve.tensor_reduce(step_expert[:, :], past[:, :, :], AX_X, ALU.add))
            entry(dve.tensor_reduce(step_base[:, :], past_n[:, :, :], AX_X, ALU.add))
            entry(dve.tensor_tensor(step_row[:, :], step_id[:, :], step_base[:, :], ALU.subtract))
            entry(dve.tensor_scalar(step_row[:, :], step_row[:, :], float(TR), None, ALU.mult))
            entry(dve.tensor_scalar(last_row[:, :], count_f[:, :], -float(TR), 0.0, ALU.add, ALU.max))
            entry(dve.tensor_tensor(last_more[:, :], last_row[:, 1:NE], last_row[:, 0:NE - 1], ALU.subtract))
            entry(dve.tensor_tensor(past_row[:, :, :], past[:, :, :], last_more[:, :].unsqueeze(1).broadcast_to(
                [1, STEPS, NE - 1]), ALU.mult))
            entry(dve.tensor_reduce(step_lim[:, :], past_row[:, :, :], AX_X, ALU.add))
            entry(dve.tensor_scalar(step_lim[:, :], step_lim[:, :], last_row[:, 0:1], None, ALU.add))
            entry(dve.tensor_tensor(step_row[:, :], step_row[:, :], step_lim[:, :], ALU.min))
            entry(dve.scalar_tensor_tensor(out=step_row[:, :], in0=step_expert[:, :], scalar=float(REGION),
                                           in1=step_row[:, :], op0=ALU.mult, op1=ALU.add))
            entry(dve.tensor_copy(table[:, 0, :], step_row[:, :]))
            entry(dve.tensor_copy(table[:, 1, :], step_expert[:, :]))
            assert tab[0] == TAB_STEPS
            dve.wait_ge(s_pv, GROUPS)
            dve.wait_ge(s_mk, NB)
            dve.wait_ge(s_ldx, 16 * (NE + 4))

            def weights(st, r):
                e = dve.value_load(table[0:1, 1, bass.ds(st, 1)], min_val=0, max_val=NE - 1)
                after(dve, s_y, st - SU + 1)
                after(dve, s_ysum, st - SU + 1)
                dve.tensor_copy(w_ring[:, r, :], experts[:, bass.ds(e, 1), :].rearrange("p o n -> p (o n)")).then_inc(s_w, 1)

            def turned(st, r, x):
                dve.wait_ge(s_xt, st + 1)
                dve.tensor_copy(xsT[:, r, :], pB[:, 0:TR]).then_inc(s_xtc, 1)
                after(dve, s_ysc, 16 * NBLK * (st - SU + 1))
                dve.tensor_copy(dest[:, x, :], xs[:, x, :, E]).then_inc(s_dest, 1)

            weights(0, 0)
            turned(0, 0, 0)

            def expert_step(it, u):
                st = SU * it + u
                if live(st + 1, STEPS):
                    weights(st + 1, (u + 1) % SU)
                    turned(st + 1, (u + 1) % 2, (u + 1) % SU)
                if live(st - 1, STEPS):
                    r = (u - 1) % 2
                    dve.wait_ge(s_y, st)
                    after(dve, s_yout, NBLK * (st - 2))
                    dve.tensor_tensor(y_sum[:, r, :, :], pO[:, 0:NBLK * E].rearrange("p (k e) -> p k e", k=NBLK),
                                      w_ring[:, (u - 1) % SU, 2 * HID + HC:EXP].unsqueeze(1).broadcast_to([P, NBLK, E]),
                                      ALU.add).then_inc(s_ysum, 1)

            over_steps(dve, expert_step)

            dve.wait_ge(s_fx, 16 * CHUNKS)

            def last_sum(t, r, n):
                dve.wait_ge(s_fl[r], 16 * (TOPK + 1) * (n + 1))
                y = fin_y[:, r, 0, :, :]
                dve.tensor_tensor(y, y, fin_y[:, r, 1, :, :], ALU.add).then_inc(s_fa, 1)
                dve.wait_ge(s_fa, t + 1)
                y_b = y.rearrange("p (b k) e -> p b k e", b=CB)
                dve.tensor_tensor(y_b, y_b, fin_gb[:, r, :, :].unsqueeze(2).broadcast_to([P, CB, NBLK, E]),
                                  ALU.mult).then_inc(s_fb, 1)
                dve.wait_ge(s_fb, t + 1)
                x_t = fin_x[:, bass.ds(t, 1), :, :].rearrange("p o a e -> p (o a) e")
                dve.tensor_tensor(x_t, x_t, y, ALU.add).then_inc(s_fc, 1)

            with dve.Fori(0, CHUNKS // FIN) as it:
                for r in range(FIN):
                    last_sum(FIN * it + r, r, it)

        @block.scalar
        def _(act):
            act.wait_ge(s_ld, 16 * NLD)
            act.activation(c_exp[:, :], c_in[:, :], ACT.Exp, scale=-1.0).then_inc(s_act0, 1)

            def modulate(u):
                act.wait_ge(s_pA, (CQ + 1) * u + 1)
                after(act, s_pB, (CQ + 1) * u)
                for b in range(CB):
                    act.activation(hT[:, b * S:(b + 1) * S], pP[0][:, b * S:(b + 1) * S], ACT.Identity,
                                   scale=scaleT[:, 0, bass.ds(CB * u + b, 1)],
                                   bias=shiftT[:, 0, bass.ds(CB * u + b, 1)]).then_inc(s_hT, 1)

            def round_piece(u, n, i):
                act.wait_ge(s_pB if n else s_pA, (CQ + 1) * u + 2 + i)
                act.activation(rounded[:, n, :, :].rearrange("p c n -> p (c n)"), pP[n][:, :],
                               ACT.Copy).then_inc(s_rk if n else s_rq, 1)

            def normalise(t, par):
                act.wait_ge(s_off, t + 1)
                after(act, s_pA, (CQ + 1) * (t - 1) + 1)
                for a in range(NT):
                    act.activation(xn[:, a, :], x_in[:, par, a, :], ACT.Identity, scale=rstd[:, a:a + 1],
                                   bias=mean_off[:, a:a + 1]).then_inc(s_xn, 1)

            normalise(0, 0)
            act.wait_ge(s_dve0, DVE_MOD)
            modulate(0)
            for i in range(CQ):
                round_piece(0, 0, i)
                round_piece(0, 1, i)
            normalise(1, 1)

            def slot(it, g):
                G, T, s = BODY * it + g, 2 * it + g // CG, g % CG
                par = (g // CG) % 2
                B, j = GB * it + g // GB, g % GB
                b = (g // GB) % 2
                prep = live(T + 1, CHUNKS) and live(T, CHUNKS)
                batch = GB * it + (g - 4) // GB
                b4 = ((g - 4) // GB) % 2

                def exponentials(h):
                    act.wait_ge(s_s2, HG * (G - 2) + h + 1)
                    if h == 0:
                        after(act, s_pv, G - 3)
                    act.activation(probs[:, g % 2, h, :], pS2[h % 2][:, :], ACT.Exp).then_inc(s_exp, 1)

                if live(G - 1, GROUPS):
                    act.wait_ge(s_tm, G)
                    after(act, s_m[(g - 1) % 2], 16 * HG * (BODY // 2 * it + (g - 1) // 2))
                    act.copy(nshiftT[:, (g - 1) % 2, :], pB[0:HG * NBLK, 0:P]).then_inc(s_tmcp, 1)
                if live(G - 2, GROUPS):
                    exponentials(0)
                if live(G - 4, GROUPS):
                    act.wait_ge(s_to, G - 3)
                    if g % GB == 0:
                        after(act, s_fin, batch - 1)
                    act.copy(o_rows[:, b4, :, HG * (g % GB):HG * (g % GB) + HG, :],
                             pB[:, 0:NBLK * P].rearrange("p (k h m) -> p k h m", k=NBLK, h=HG)[:, :, :, 0:NV]).then_inc(s_tocp, 1)
                if j == 1 and live(B - 3, NB):
                    act.wait_ge(s_h2t, B - 2)
                    act.copy(h2T[:, :], pO[:, S:2 * S]).then_inc(s_h2c, 1)
                if prep and 2 <= s <= CQ + 1:
                    round_piece(T + 1, 1, s - 2)
                if live(G - 2, GROUPS):
                    exponentials(1)
                if prep and s == 0:
                    modulate(T + 1)
                if prep and 1 <= s <= CQ:
                    round_piece(T + 1, 0, s - 1)
                if live(G - 2, GROUPS):
                    exponentials(2)
                if live(G - 4, GROUPS) and j == 3:
                    act.wait_ge(s_mk, batch + 1)
                    after(act, s_f1, NBLK * (batch - 1))
                    act.copy(o_mask[:, b4, :, :, :].rearrange("p k h v -> p (k h v)"),
                             pB[:, 0:NBLK * H * NV]).then_inc(s_mkcp, 1)
                if live(G - 2, GROUPS):
                    exponentials(3)
                if live(G - 3, GROUPS):
                    act.wait_ge(s_pv, G - 2)
                    after(act, s_to, G - 4)
                    act.copy(oT[:, (g - 3) % 2, :], pO[:, 0:S]).then_inc(s_ot, 1)
                if j == 3 and live(B - 2, NB):
                    act.wait_ge(s_off2, B - 1)
                    after(act, s_h2, B - 2)
                    for k in range(NBLK):
                        act.activation(h2f[:, k, :], x_new[:, b, k, :], ACT.Identity, scale=rstd2[:, k:k + 1],
                                       bias=mean_off2[:, k:k + 1]).then_inc(s_n2, 1)
                if s == 6 and live(T + 2, CHUNKS):
                    normalise(T + 2, par)
                if j == 1 and live(B - 3, NB):
                    q = (g // GB - 3) % 2
                    act.copy(h2_rows[:, q, 1, :, 0:E], h2_rows[:, q, 0, :, 0:E]).then_inc(s_dup, 1)
                if j == 2 and live(B - 3, NB):
                    act.wait_ge(s_ein, B - 2)
                    act.activation(top_exp[:, :, :], top_arg[:, :, :], ACT.Exp).then_inc(s_eg, 1)
                if j == 1 and live(B - 1, NB):
                    act.wait_ge(s_earg, B)
                    act.activation(e_shift[:, (g // GB - 1) % 2, :], e_arg[:, (g // GB - 1) % 2, :], ACT.Exp).then_inc(s_e, 1)

            over_groups(act, slot)

            def expert_step(it, u):
                st = SU * it + u
                r = u % 2
                if live(st, STEPS):
                    for c in range(HC):
                        act.wait_ge(s_hid, HC * st + (c // 2 + 1) * 2)
                        if c == 0:
                            after(act, s_y, st - 1)
                        act.activation(hidT[:, r, c, :], hid_bank(r, c), ACT.Gelu,
                                       bias=w_ring[:, u, HID + c:HID + c + 1]).then_inc(s_gelu, 1)
                if live(st - 1, STEPS):
                    q = (u - 1) % 2
                    act.wait_ge(s_ysum, st)
                    after(act, s_ysc, 16 * NBLK * (st - 2))
                    for k in range(NBLK):
                        act.activation(y_out[:, q, k, :], y_sum[:, q, k, :], ACT.Copy,
                                       scale=xs[:, (u - 1) % SU, k, E + 1:E + 2]).then_inc(s_yout, 1)

            over_steps(act, expert_step)

        @block.tensor
        def _(pe):
            pe.wait_ge(s_pool0, 17)
            pe.wait_ge(s_dve0, DVE_SILU)
            for n in range(3):
                pe.transpose(pP[0][:, n * P:(n + 1) * P], w_nat[:, n, :], ident[:, :])
            pe.transpose(pP[0][:, 3 * P:4 * P], c_in[:, :], ident[:, :]).then_inc(s_pe0, 1)
            pe.wait_ge(s_dve0, DVE_WEIGHTS)
            for half in range(2):
                pe.matmul(pP[half][0:NB, 0:3 * E], siluT[:, :], wmod_sb[:, 3 * half:3 * half + 3, :].rearrange("k m e -> k (m e)"),
                          start=True, stop=True)
            for half in range(2):
                for m in range(2):
                    last = pe.matmul(pB[:, (2 * half + m) * NB:(2 * half + m + 1) * NB], wmod_sb[:, 3 * half + m, :],
                                     siluT[:, :], start=True, stop=True)
            last.then_inc(s_pe0, 1)
            pe.wait_ge(s_dve0, DVE_MOD - 2)
            pe.wait_ge(s_ldx, 16 * (NE + 4))
            pe.transpose(pP[0][:, 0:NE * HC], b1_rows[:, :], ident[0:NE * HC, 0:NE * HC])
            pe.transpose(pP[0][:, NE * HC:NE * HC + NE], wg_rows[:, :], ident[0:NE, 0:NE]).then_inc(s_pe0, 1)
            pe.wait_ge(s_dve0, DVE_MOD)

            def tokens(u):
                pe.wait_ge(s_xn, NT * (u + 1))
                after(pe, s_q, CQ * u)
                for a in range(NT):
                    last = pe.transpose(pP[0][:, a * P:(a + 1) * P], xn[:, a, :], ident[:, :])
                last.then_inc(s_pA, 1)

            def values(u):
                pe.wait_ge(s_hT, CB * (u + 1))
                after(pe, s_k, CQ * u)
                for a in range(NT):
                    last = pe.matmul(pP[1][:, a * P:(a + 1) * P], hT[:, a * P:(a + 1) * P], wvT[:, :], start=True, stop=True)
                last.then_inc(s_pB, 1)

            def project(u, n, i):
                if n == 0:
                    pe.wait_ge(s_hT, CB * (u + 1))
                    after(pe, s_q, CQ * u + i)
                else:
                    pe.wait_ge(s_v, u + 1)
                    after(pe, s_k, CQ * u + i)
                pe.matmul(pP[n][:, :], bias_lhs[:, n, i, :], bias_ind[:, :, :].rearrange("p c n -> p (c n)"),
                          start=True, stop=False, skip_group_check=True)
                heads = hT[:, :].rearrange("p (g h r) -> p h g r", h=HG, r=R)
                for c in range(4):
                    for h in range(HG):
                        last = pe.matmul(pP[n][SLOT * h:SLOT * h + SLOT, c * P:(c + 1) * P].rearrange("p (g r) -> p g r", r=R),
                                         w_slot[:, n, 4 * i + c, :], heads[:, h], start=False, stop=(c == 3),
                                         skip_group_check=True)
                last.then_inc(s_pB if n else s_pA, 1)

            tokens(0)
            values(0)
            for i in range(CQ):
                project(0, 0, i)
                project(0, 1, i)

            def slot(it, g):
                G, T, s = BODY * it + g, 2 * it + g // CG, g % CG
                B, j = GB * it + g // GB, g % GB
                par = (g // CG) % 2
                prep = live(T + 1, CHUNKS) and live(T, CHUNKS)

                def scores(h):
                    if s == 0 and h == 0:
                        pe.wait_ge(s_qb, 16 * HG * (T + 1))
                        pe.wait_ge(s_k, CQ * (T + 1))
                    after(pe, s_red, HG * G + h - 1)
                    for k in range(NBLK):
                        pe.matmul(pS1[h % 2][:, k * S:(k + 1) * S], q_diag[:, par, s, h, k * P:(k + 1) * P],
                                  k_pack[:, par, s, :], start=True, stop=False, skip_group_check=True)
                        o = k * S + (1 - k) * P
                        last = pe.matmul(pS1[h % 2][:, o:o + P], identb[:, :], neg[:, k, :], start=False, stop=True,
                                         skip_group_check=True)
                    last.then_inc(s_s1, 1)

                def shifted_scores(h):
                    g2 = (g - 2) % BODY
                    if h == 0:
                        pe.wait_ge(s_m[g % 2], 16 * HG * (BODY // 2 * it + (g - 2) // 2 + 1))
                    after(pe, s_exp, HG * (G - 2) + h - 1)
                    for k in range(NBLK):
                        last = pe.matmul(pS2[h % 2][:, k * S:(k + 1) * S], k_pack[:, g2 // CG, g2 % CG, k * P:(k + 1) * P],
                                         q_diag[:, g2 // CG, g2 % CG, h, :], start=True, stop=True)
                    last.then_inc(s_s2, 1)

                if live(G, GROUPS):
                    scores(0)
                if live(G - 1, GROUPS):
                    pe.wait_ge(s_nm, G)
                    after(pe, s_tocp, G - 4)
                    if isinstance(G, int) and G < 5:
                        after(pe, s_tmcp, G - 1)
                    if j == 0:
                        after(pe, s_mkcp, B - 1)
                    pe.transpose(pB[0:HG * NBLK, 0:P],
                                 nshift[:, ((g - 1) // GB) % 4, (g - 1) % GB, :, :].bitcast(F32).rearrange("p h k -> p (h k)"),
                                 ident[:, :]).then_inc(s_tm, 1)
                if live(G - 2, GROUPS):
                    shifted_scores(0)
                if live(G, GROUPS):
                    scores(1)
                if live(G - 4, GROUPS):
                    pe.wait_ge(s_ot, G - 3)
                    after(pe, s_tmcp, min(G, GROUPS) if isinstance(G, int) else G)
                    if not live(G - 1, GROUPS):
                        pe.wait_ge(s_tocp, G - 4)
                        if j == 0:
                            pe.wait_ge(s_mkcp, B - 1)
                    for k in range(NBLK):
                        last = pe.transpose(pB[:, k * P:(k + 1) * P], oT[:, (g - 4) % 2, k * P:(k + 1) * P], ident[:, :])
                    last.then_inc(s_to, 1)
                after(pe, s_ot, min(G - 3, GROUPS) if isinstance(G, int) else G - 3)
                if j == 1 and live(B - 3, NB):
                    pe.wait_ge(s_h2, B - 2)
                    for k in range(NBLK):
                        last = pe.transpose(pO[:, S + k * P:S + (k + 1) * P], h2_rows[:, (g // GB - 3) % 2, 0, k, 0:E],
                                            ident[:, :])
                    last.then_inc(s_h2t, 1)
                if j == 2 and live(B - 3, NB):
                    pe.wait_ge(s_h2c, B - 2)
                    for k in range(NBLK):
                        last = pe.matmul(pO[:, S + k * NE:S + (k + 1) * NE], h2T[:, k * P:(k + 1) * P], wgT[:, :],
                                         start=True, stop=True)
                    last.then_inc(s_lg, 1)
                if j == 3 and live(B - 3, NB):
                    pe.wait_ge(s_ch, B - 2)
                    first, second = chosen_b[:, 0, :], chosen_b[:, 1, :]
                    pre = [pO[:, S + n * NE:S + (n + 1) * NE] for n in range(NBLK + 1)]
                    pe.matmul(pre[0], before_b[:, :], first, start=True, stop=True)
                    pe.matmul(pre[1], before_b[:, :], second, start=True, stop=False)
                    pe.matmul(pre[1], ones_b[:, :], first, start=False, stop=True)
                    pe.matmul(pre[2], ones_b[:, :], first, start=True, stop=False)
                    pe.matmul(pre[2], ones_b[:, :], second, start=False, stop=True).then_inc(s_pre, 1)
                if live(G - 2, GROUPS):
                    shifted_scores(1)
                if prep and s == 0:
                    tokens(T + 1)
                if prep and 1 <= s <= CQ:
                    project(T + 1, 0, s - 1)
                if live(G, GROUPS):
                    scores(2)
                if live(G - 2, GROUPS):
                    shifted_scores(2)
                if j == 3 and live(B - 1, NB):
                    g4 = (g - 7) % BODY
                    after(pe, s_tmcp, min(G, GROUPS) if isinstance(G, int) else G)
                    pe.wait_ge(s_tocp, G - 3)
                    for k in range(NBLK):
                        heads = v_slot[:, g4 // CG, 1 - k, g4 % CG:g4 % CG + GB, :, 0:NV].rearrange("p g h v -> p (g h) v")
                        last = pe.matmul(pB[:, k * H * NV:(k + 1) * H * NV].rearrange("p (h v) -> p h v", v=NV),
                                         tri[:, k, :], heads, start=True, stop=True)
                    last.then_inc(s_mk, 1)
                if live(B - 3, NB):
                    if j == 1:
                        pe.wait_ge(s_h2c, B - 2)
                    if j == 2:
                        pe.wait_ge(s_lgc, B - 2)
                    if j == 3:
                        pe.wait_ge(s_pos, 2 * (B - 2))
                if live(G - 3, GROUPS):
                    g3 = (g - 3) % BODY
                    pe.wait_ge(s_aff, 2 * (G - 2))
                    after(pe, s_ot, G - 3)
                    if g3 % CG == 0:
                        pe.wait_ge(s_vr, 32 * (2 * it + (g - 3) // CG + 1))
                    for k in range(NBLK):
                        for h in range(HG):
                            last = pe.matmul(pO[SLOT * h:SLOT * h + SLOT, 0:S], v_slot[:, g3 // CG, k, g3 % CG, h, :],
                                             probs[:, (g - 3) % 2, h, k * S:(k + 1) * S], start=(k == 0), stop=(k == 1))
                    last.then_inc(s_pv, 1)
                if live(G, GROUPS):
                    scores(3)
                if live(G - 2, GROUPS):
                    shifted_scores(3)
                if prep and s == 0:
                    values(T + 1)
                if prep and 1 <= s <= CQ:
                    project(T + 1, 1, s - 1)

            over_groups(pe, slot)

            def turn(st, r, n):
                pe.wait_ge(s_xs[r], 16 * (n + 1))
                after(pe, s_xtc, st)
                for k in range(NBLK):
                    last = pe.transpose(pB[:, k * P:(k + 1) * P], xs[:, r, k, 0:E], ident[:, :])
                last.then_inc(s_xt, 1)

            turn(0, 0, 0)

            def expert_step(it, u):
                st = SU * it + u
                r = u % 2

                def hidden(c):
                    if c == 0:
                        pe.wait_ge(s_w, st + 1)
                        pe.wait_ge(s_xtc, st + 1)
                        after(pe, s_gelu, HC * (st - 1))
                    pe.matmul(hid_bank(r, c), w_ring[:, u, c * P:(c + 1) * P], xsT[:, r, :],
                              start=True, stop=True).then_inc(s_hid, 1)

                if live(st, STEPS):
                    hidden(0)
                    hidden(1)
                if live(st + 1, STEPS):
                    turn(st + 1, (u + 1) % SU, it + (u + 1) // SU)
                if live(st, STEPS):
                    hidden(2)
                    hidden(3)
                if live(st - 1, STEPS):
                    q = (u - 1) % 2
                    pe.wait_ge(s_gelu, HC * st)
                    after(pe, s_ysum, st - 1)
                    for k in range(NBLK):
                        for c in range(HC):
                            w = w_ring[:, (u - 1) % SU, HID + HC + c * E:HID + HC + (c + 1) * E]
                            last = pe.matmul(pO[:, k * E:(k + 1) * E], hidT[:, q, c, k * P:(k + 1) * P], w,
                                             start=(c == 0), stop=(c == HC - 1))
                    last.then_inc(s_y, 1)

            over_steps(pe, expert_step)


_INS = ["L0_attn_x", "L0_attn_Wq", "L0_attn_bq", "L0_attn_Wk", "L0_attn_bk", "L0_attn_Wv", "L0_attn_bv",
        "L0_ffn_w_gate", "L0_ffn_W1", "L0_ffn_b1", "L0_ffn_W2", "L0_ffn_b2", "L0_c", "L0_wmod"]
_OUTS = [((NB, S, E), "float32")]


def kernel(**inputs):
    import numpy as _np
    import concourse.bacc as _bacc
    from concourse import mybir as _mybir
    from concourse.bass_utils import run_bass_kernel_spmd as _run

    nc = _bacc.Bacc("TRN2", target_bir_lowering=False, num_devices=1)
    arrays, args = {}, []
    for name in _INS:
        a = _np.ascontiguousarray(inputs[name])
        arrays[f"in_{name}_dram"] = a
        args.append(nc.dram_tensor(f"in_{name}_dram", a.shape, _mybir.dt.from_np(a.dtype), kind="ExternalInput").ap())
    for i, (shape, dtype) in enumerate(_OUTS):
        dt = _mybir.dt.from_np(_np.dtype(dtype))
        args.append(nc.dram_tensor(f"out_{i}_dram", shape, dt, kind="ExternalOutput").ap())
    build(nc, *args)
    r = _run(nc, [arrays], core_ids=[0])
    return r.results[0]["out_0_dram"]
```

```python
from contextlib import ExitStack

import concourse.bass as bass
from concourse import mybir

P = 128
F32 = mybir.dt.float32
F32R = mybir.dt.float32r
BF16 = mybir.dt.bfloat16
I32 = mybir.dt.int32
ALU = mybir.AluOpType
ACT = mybir.ActivationFunctionType
AX_X = mybir.AxisListType.X

NB, S, E = 32, 256, 128
H, D = 16, 8
TOK = NB * S
WINDOW = 128
NBLK = S // WINDOW
HG = 4
GB = H // HG
CB = 2
CG = CB * GB
CT = CB * S
NT = CT // P
CHUNKS = NB // CB
GROUPS = CHUNKS * CG
R = S // H
C = S // R
CQ = C // 4
BODY = 2 * CG
BODIES = GROUPS // BODY
LAG = 15
SLOT = 32
SHIFT = 3 * D
NV = D + 1
EPS = 1e-5
MASKED = -1.0e30
U32 = mybir.dt.uint32
NE, TOPK = 8, 2
HID = 512
HC = HID // P
EXP = 2 * HID + HC + E
ROW = E + 2
TR = 256
REGION = TOK
STEPS = -(-(TOPK * TOK + NE * (TR - 1)) // (4 * TR)) * 4
SU = 4
TAB_STEPS = 21
POOL_SETUP = 33
QUERY_SLOTS, KEY_SLOTS = (1, 2, 3, 4), (2, 3, 5, 6)
FIN = 4
DVE_SILU, DVE_WEIGHTS, DVE_MOD, DVE_COLUMNS, DVE_BIAS, DVE_ROWS, DVE_LATE = 3, 13, 15, 19, 48, 54, 56


def after(eng, sem, count):
    if not isinstance(count, int) or count > 0:
        eng.wait_ge(sem, count)


def live(i, n):
    return not isinstance(i, int) or 0 <= i < n


def over_groups(eng, slot):
    for g in range(BODY):
        slot(0, g)
    with eng.Fori(1, BODIES - 1) as it:
        for g in range(BODY):
            slot(it, g)
    for g in range(BODY):
        slot(BODIES - 1, g)
    for g in range(LAG):
        slot(BODIES, g)


NEWTON = 3
RSTD_STEPS = 3 + 3 * NEWTON


def rsqrt_guess(dve, sem, done, out, var, half):
    dve.tensor_scalar(half, var, EPS, None, ALU.add).then_inc(sem, 1)
    dve.wait_ge(sem, done + 1)
    dve.tensor_scalar(out.bitcast(I32), half.bitcast(I32), 1, None, ALU.logical_shift_right).then_inc(sem, 1)
    dve.wait_ge(sem, done + 2)
    dve.tensor_scalar(out.bitcast(I32), out.bitcast(I32), -1.0, float(0x5F3759DF - 2 ** 31), ALU.mult, ALU.add).then_inc(sem, 1)


def rsqrt_newton(dve, sem, done, k, out, half, tmp):
    done = done + 3 + 3 * k
    dve.wait_ge(sem, done)
    dve.tensor_tensor(tmp, out, out, ALU.mult).then_inc(sem, 1)
    dve.wait_ge(sem, done + 1)
    dve.scalar_tensor_tensor(out=tmp, in0=tmp, scalar=0.5, in1=half, op0=ALU.mult, op1=ALU.mult).then_inc(sem, 1)
    dve.wait_ge(sem, done + 2)
    dve.scalar_tensor_tensor(out=out, in0=tmp, scalar=-1.5, in1=out, op0=ALU.add, op1=ALU.mult).then_inc(sem, 1)


def over_steps(eng, step):
    bodies = STEPS // SU
    for u in range(SU):
        step(0, u)
    with eng.Fori(1, bodies - 1) as it:
        for u in range(SU):
            step(it, u)
    for u in range(SU):
        step(bodies - 1, u)
    step(bodies, 0)


def build(nc, x, wq, bq, wk, bk, wv, bv, w_gate, w1, b1, w2, b2, cond, wmod, out):
    with ExitStack() as ctx:
        def sb(name, shape, dt=F32):
            return ctx.enter_context(nc.sbuf_tensor(name, shape, dt))

        def passing(scope, name, shape, dt=F32):
            return scope.enter_context(nc.sbuf_tensor(name, shape, dt))

        def psum(name):
            return ctx.enter_context(nc.psum_tensor(name, [P, 512], F32))

        def sem(name):
            return ctx.enter_context(nc.semaphore(name))

        def dram(name, shape):
            return nc.dram_tensor(name, shape, F32, kind="Internal").ap()

        mod_rows = dram("mod_rows", [NB, 6, E])
        v_rows = dram("v_rows", [CHUNKS, CT, E])
        x_mid = dram("x_mid", [NB, S, E])

        x_expert = dram("x_expert", [NE * REGION, ROW])
        y_token = dram("y_token", [TOPK * TOK + 2 * TR, E])

        pS1 = [psum("pS1a"), psum("pS1b")]
        pS2 = [psum("pS2a"), psum("pS2b")]
        pO = psum("pO")
        pP = [psum("pPa"), psum("pPb")]
        pB = psum("pB")

        ident = sb("ident", [P, P])
        identb = sb("identb", [P, P], BF16)
        neg = sb("neg", [P, NBLK, P], BF16)
        tri = sb("tri", [P, NBLK, P])
        nfloor = sb("nfloor", [P, NBLK])
        row_id = sb("row_id", [P, 1], I32)
        row_bits = sb("row_bits", [P, 1], I32)
        low_mask = sb("low_mask", [P, 2])
        quad = sb("quad", [P, 1])
        bias_ind = sb("bias_ind", [P, 4, P], BF16)

        w_slot = sb("w_slot", [P, 2, C, SLOT])
        wvT = sb("wvT", [P, E])
        experts = sb("experts", [P, NE, EXP])
        bias_lhs = sb("bias_lhs", [P, 2, CQ, P], BF16)
        bv_all = sb("bv_all", [P, E])
        scaleT = sb("scaleT", [P, 2, NB])
        shiftT = sb("shiftT", [P, 2, NB])

        x_in = sb("x_in", [P, 2, NT, E])
        stats = sb("stats", [P, NT, 6])
        mean_var = sb("mean_var", [P, NT, 2])
        rstd = sb("rstd", [P, NT])
        half_var = sb("half_var", [P, NT])
        r_tmp = sb("r_tmp", [P, NT])
        mean_off = sb("mean_off", [P, NT])
        xn = sb("xn", [P, NT, E])
        hT = sb("hT", [P, CT])
        rounded = sb("rounded", [P, 2, 4, P], F32R)
        v_tok = sb("v_tok", [P, NT, E])
        row_max = sb("row_max", [P, 2, HG, NBLK])
        nshift = sb("nshift", [P, 4, GB, HG, NBLK], F32R)
        nshiftT = sb("nshiftT", [HG * NBLK, 2, P], F32R)
        with ExitStack() as setup:
            w_nat = passing(setup, "w_nat", [P, 3, E])
            bias_row = passing(setup, "bias_row", [3 * 4, 2, CQ, D])
            bias_rest = passing(setup, "bias_rest", [3 * 4, 2, CQ, D])
            bias_part = passing(setup, "bias_part", [3 * 4, 3, 2, CQ, D], BF16)
            bias_mine = passing(setup, "bias_mine", [3 * 4, 3, 2, CQ, D], BF16)
            part_row = passing(setup, "part_row", [P, 3])
            bias_bits = passing(setup, "bias_bits", [P, 1], I32)
            c_in = passing(setup, "c_in", [P, E])
            c_exp = passing(setup, "c_exp", [P, E])
            siluT = passing(setup, "siluT", [P, NB])
            wmod_sb = passing(setup, "wmod_sb", [P, 6, E])
            mod_sb = passing(setup, "mod_sb", [NB, 6, E])
            gate_sign = passing(setup, "gate_sign", [NB, 2, E])
            b1_rows = passing(setup, "b1_rows", [NE * HC, P])
            wg_rows = passing(setup, "wg_rows", [NE, E])
        probs = sb("probs", [P, 2, HG, NBLK * S])
        oT = sb("oT", [P, 2, S])
        o_rows = sb("o_rows", [P, 2, NBLK, H, NV])
        o_mask = sb("o_mask", [P, 2, NBLK, H, NV])
        o_tmp = sb("o_tmp", [P, NBLK, H, NV])
        e_arg = sb("e_arg", [P, 2, H * NBLK])
        e_shift = sb("e_shift", [P, 2, H * NBLK])
        rden = sb("rden", [P, 2, NBLK, H])
        x_res = sb("x_res", [P, 2, NBLK, E])
        ga_all = sb("ga_all", [P, 2, E])
        o_att = sb("o_att", [P, NBLK, E])
        x_new = sb("x_new", [P, 2, NBLK, E])

        cs_all = sb("cs_all", [P, 2, E])
        stats2 = sb("stats2", [P, NBLK, 6])
        mean_var2 = sb("mean_var2", [P, NBLK, 2])
        rstd2 = sb("rstd2", [P, NBLK])
        half_var2 = sb("half_var2", [P, NBLK])
        r_tmp2 = sb("r_tmp2", [P, NBLK])
        mean_off2 = sb("mean_off2", [P, NBLK])
        h2f = sb("h2f", [P, NBLK, E])
        h2_rows = sb("h2_rows", [P, 2, TOPK, NBLK, ROW])
        token_id = sb("token_id", [P, TOPK, NBLK])
        h2T = sb("h2T", [P, S])
        wgT = sb("wgT", [P, NE])
        logits = sb("logits", [P, NBLK, NE])
        top = sb("top", [P, NBLK, NE])
        top_at = sb("top_at", [P, NBLK, NE], U32)
        top_atf = sb("top_atf", [P, NBLK, TOPK])
        top_arg = sb("top_arg", [P, NBLK, NE])
        top_exp = sb("top_exp", [P, NBLK, NE])
        chosen = sb("chosen", [P, NBLK, TOPK, NE])
        chosen_b = sb("chosen_b", [P, NBLK, NE], BF16)
        expert_id = sb("expert_id", [P, NE])
        expert_idi = sb("expert_idi", [P, NE], I32)
        next_row = sb("next_row", [P, NE])
        place = sb("place", [P, NBLK, NE])
        place_of = sb("place_of", [P, NBLK, TOPK, NE])
        row_f = sb("row_f", [P, NBLK, TOPK])
        row_i = sb("row_i", [P, 2, NBLK, TOPK], I32)
        gate_sum = sb("gate_sum", [P, NBLK])
        gate_inv = sb("gate_inv", [P, NBLK])
        before_b = sb("before_b", [P, P], BF16)
        ones_b = sb("ones_b", [P, P], BF16)
        pad_rows = sb("pad_rows", [P, NBLK, ROW])
        pad_idi = sb("pad_idi", [P, NBLK], I32)
        pad_id = sb("pad_id", [P, NBLK])
        away = sb("away", [P, 2, NBLK])
        ones_row = sb("ones_row", [P, NE])
        step_idi = sb("step_idi", [P, STEPS], I32)
        step_id = sb("step_id", [P, STEPS])

        with ExitStack() as attention:
            q_pack = passing(attention, "q_pack", [P, CG, S], F32R)
            k_pack = passing(attention, "k_pack", [P, 2, CG, S], F32R)
            v_slot = passing(attention, "v_slot", [P, 2, NBLK, CG, HG, SLOT])
            q_diag = passing(attention, "q_diag", [P, 2, CG, HG, S], F32R)
        count_f = sb("count_f", [P, NE])
        tiles_i = sb("tiles_i", [P, NE], I32)
        tiles = sb("tiles", [P, NE])
        tiles_sum = sb("tiles_sum", [P, NE])
        past = sb("past", [P, STEPS, NE - 1])
        past_n = sb("past_n", [P, STEPS, NE - 1])
        step_expert = sb("step_expert", [P, STEPS])
        step_base = sb("step_base", [P, STEPS])
        step_lim = sb("step_lim", [P, STEPS])
        last_row = sb("last_row", [P, NE])
        last_more = sb("last_more", [P, NE - 1])
        past_row = sb("past_row", [P, STEPS, NE - 1])
        step_row = sb("step_row", [P, STEPS])
        seen = sb("seen", [P, STEPS])
        table = sb("table", [1, 2, STEPS], I32)
        w_ring = sb("w_ring", [P, SU, EXP])
        xs = sb("xs", [P, SU, NBLK, ROW])
        hidT = sb("hidT", [P, 2, HC, TR])
        xsT = sb("xsT", [P, 2, TR])
        dest = sb("dest", [P, SU, NBLK], I32)
        parts = sb("parts", [P, 2, NBLK])
        row_gate = sb("row_gate", [P, SU, NBLK])
        y_sum = sb("y_sum", [P, 2, NBLK, E])
        y_out = sb("y_out", [P, 2, NBLK, E])
        fin_y = sb("fin_y", [P, FIN, TOPK, NT, E])
        fin_x = sb("fin_x", [P, CHUNKS, NT, E])
        fin_gb = probs[:, :, :, :].rearrange("p a h n -> p (a h n)").rearrange("p (b e) -> p b e", e=E)

        s_ld = sem("s_ld")
        s_pool0 = sem("s_pool0")
        s_dve0 = sem("s_dve0")
        s_act0 = sem("s_act0")
        s_pe0 = sem("s_pe0")
        s_late = sem("s_late")
        s_bias = sem("s_bias")
        s_mod = sem("s_mod")
        s_x = [sem("s_x0"), sem("s_x1")]
        s_stats = sem("s_stats")
        s_aggr = sem("s_aggr")
        s_rstd = sem("s_rstd")
        s_off = sem("s_off")
        s_xn = sem("s_xn")
        s_pA = sem("s_pA")
        s_pB = sem("s_pB")
        s_hT = sem("s_hT")
        s_rq = sem("s_rq")
        s_rk = sem("s_rk")
        s_q = sem("s_q")
        s_k = sem("s_k")
        s_v = sem("s_v")
        s_vst = sem("s_vst")
        s_vr = sem("s_vr")
        s_qb = sem("s_qb")
        s_s1 = sem("s_s1")
        s_red = sem("s_red")
        s_nm = sem("s_nm")
        s_tm = sem("s_tm")
        s_tmcp = sem("s_tmcp")
        s_m = [sem("s_m0"), sem("s_m1")]
        s_s2 = sem("s_s2")
        s_exp = sem("s_exp")
        s_aff = sem("s_aff")
        s_pv = sem("s_pv")
        s_ot = sem("s_ot")
        s_to = sem("s_to")
        s_tocp = sem("s_tocp")
        s_mk = sem("s_mk")
        s_mkcp = sem("s_mkcp")
        s_earg = sem("s_earg")
        s_e = sem("s_e")
        s_f1 = sem("s_f1")
        s_f2 = sem("s_f2")
        s_den = sem("s_den")
        s_f3 = sem("s_f3")
        s_f4 = sem("s_f4")
        s_fin = sem("s_fin")
        s_xr = [sem("s_xr0"), sem("s_xr1")]
        s_st = [sem("s_st0"), sem("s_st1")]

        s_ldx = sem("s_ldx")
        s_cs = sem("s_cs")
        s_stats2 = sem("s_stats2")
        s_aggr2 = sem("s_aggr2")
        s_rstd2 = sem("s_rstd2")
        s_off2 = sem("s_off2")
        s_n2 = sem("s_n2")
        s_m2 = sem("s_m2")
        s_h2 = sem("s_h2")
        s_id = sem("s_id")
        s_dup = sem("s_dup")
        s_h2t = sem("s_h2t")
        s_h2c = sem("s_h2c")
        s_lg = sem("s_lg")
        s_lgc = sem("s_lgc")
        s_mx = sem("s_mx")
        s_ix = sem("s_ix")
        s_ein = sem("s_ein")
        s_ixf = sem("s_ixf")
        s_oh = sem("s_oh")
        s_ch = sem("s_ch")
        s_pre = sem("s_pre")
        s_pos = sem("s_pos")
        s_prod = sem("s_prod")
        s_rowf = sem("s_rowf")
        s_row = sem("s_row")
        s_eg = sem("s_eg")
        s_gsum = sem("s_gsum")
        s_ginv = sem("s_ginv")
        s_gate = sem("s_gate")
        s_sc = sem("s_sc")
        s_tab = sem("s_tab")
        s_pad = sem("s_pad")
        s_xs = [sem(f"s_xs{u}") for u in range(SU)]
        s_w = sem("s_w")
        s_xt = sem("s_xt")
        s_xtc = sem("s_xtc")
        s_hid = sem("s_hid")
        s_gelu = sem("s_gelu")
        s_y = sem("s_y")
        s_ysum = sem("s_ysum")
        s_dest = sem("s_dest")
        s_yout = sem("s_yout")
        s_ysc = [sem("s_ysc0"), sem("s_ysc1")]
        s_away = sem("s_away")
        s_fx = sem("s_fx")
        s_fl = [sem(f"s_fl{r}") for r in range(FIN)]
        s_fa = [sem(f"s_fa{r}") for r in range(FIN)]
        s_fb = [sem(f"s_fb{r}") for r in range(FIN)]
        s_fc = [sem(f"s_fc{r}") for r in range(FIN)]
        s_fs = sem("s_fs")

        NLD = 6

        def hid_bank(r, c):
            bank = (pS1, pS2)[r][c // 2]
            return bank[:, (c % 2) * TR:(c % 2 + 1) * TR]

        def apart(eng, sem, count):
            if not isinstance(count, int):
                count = eng.to_reg(count)
                eng.wait_ge(s_ld, 16 * NLD)
            after(eng, sem, count)

        block = ctx.enter_context(nc.Block())

        def finish(eng, n, r):
            y = fin_y[:, r, 0, :, :]
            y_b = y.rearrange("p (b k) e -> p b k e", b=CB)
            x_t = fin_x[:, bass.ds(FIN * n + r, 1), :, :].rearrange("p o a e -> p (o a) e")
            gates_t = fin_gb[:, bass.ds(CB * (FIN * n + r), CB), :].unsqueeze(2).broadcast_to([P, CB, NBLK, E])
            apart(eng, s_fl[r], 16 * TOPK * (n + 1))
            eng.tensor_tensor(y, y, fin_y[:, r, 1, :, :], ALU.add).then_inc(s_fa[r], 1)
            apart(eng, s_fa[r], n + 1)
            eng.tensor_tensor(y_b, y_b, gates_t, ALU.mult).then_inc(s_fb[r], 1)
            apart(eng, s_fb[r], n + 1)
            eng.tensor_tensor(x_t, x_t, y, ALU.add).then_inc(s_fc[r], 1)

        x_tok = x.rearrange("b (k p) e -> b p k e", p=P)
        out_tok = out.rearrange("b (k p) e -> b p k e", p=P)
        x_mid_tok = x_mid.rearrange("b (k p) e -> b p k e", p=P)

        def rows_of(ap, i, n=1):
            return ap[bass.ds(i, n)]

        @block.sync
        def _(sp):
            for n, w in enumerate((wq, wk, wv)):
                sp.dma_start(w_nat[:, n, :], w).then_inc(s_ld, 16)
            sp.dma_start(bv_all[:, :], bv.rearrange("(o e) -> o e", o=1).to_broadcast([P, E])).then_inc(s_ld, 16)
            sp.wait_ge(s_pool0, 1)
            sp.dma_start(c_in[0:NB, :], cond).then_inc(s_ld, 16)
            sp.dma_start(wmod_sb[:, :, :], wmod.rearrange("k (m e) -> k m e", m=6)).then_inc(s_ld, 16)

            def load_x_at(t, par):
                apart(sp, s_xn, NT * (t - 1))
                sp.dma_start(x_in[:, par, :, :].rearrange("p (b k) e -> p b k e", b=CB),
                             rows_of(x_tok, CB * t, CB).rearrange("b p k e -> p b k e")).then_inc(s_x[par], 16)

            load_x_at(0, 0)
            load_x_at(1, 1)
            for n, b in enumerate((bq, bk)):
                for a in range(3):
                    sp.dma_start(bias_row[4 * a:4 * a + 4, n, :, :],
                                 b.rearrange("(q c d) -> c q d", c=4, d=D)).then_inc(s_bias, 16)
            sp.dma_start(b1_rows[:, :], b1.rearrange("x (c p) -> (x c) p", p=P)).then_inc(s_late, 16)
            sp.dma_start(wg_rows[:, :], w_gate).then_inc(s_late, 16)

            def store_v(u):
                apart(sp, s_v, u + 1)
                sp.dma_start(rows_of(v_rows, u).rearrange("o (a p) e -> p (o a) e", p=P),
                             v_tok[:, :, :]).then_inc(s_vst, 16)

            def load_v(u, par):
                apart(sp, s_pv, CG * (u - 1))
                apart(sp, s_mk, CB * (u - 1))
                apart(sp, s_vst, 16 * (u + 1))
                heads = rows_of(v_rows, u).rearrange("o t e -> (o t e)").rearrange(
                    "(h k p d) -> k p h d", k=NBLK, p=P, d=D)
                for k in range(NBLK):
                    sp.dma_start(v_slot[:, par, k, :, :, 0:D].rearrange("p g h d -> p (g h) d"),
                                 heads[k]).then_inc(s_vr, 16)

            def spread_q(u, par):
                apart(sp, s_q, CQ * (u + 1))
                apart(sp, s_s2, CG * HG * (u - 1))
                for h in range(HG):
                    rows = slice(SLOT * h, SLOT * h + SLOT)
                    sp.dma_start(q_diag[rows, par, :, h, :].bitcast(F32),
                                 q_pack[rows, :, :].bitcast(F32)).then_inc(s_qb, 16)

            sp.wait_ge(s_pool0, 10)
            store_v(0)
            load_v(0, 0)
            sp.wait_ge(s_pool0, 6)
            spread_q(0, 0)
            sp.wait_ge(s_dve0, DVE_ROWS)
            sp.dma_start(mod_rows, mod_sb[:, :, :]).then_inc(s_mod, 16)
            sp.wait_ge(s_mod, 16)
            sp.wait_ge(s_pool0, POOL_SETUP)

            def late_load(e):
                sp.dma_start(x_expert[e * REGION:e * REGION + TR].rearrange("(a p) w -> p a w", p=P),
                             pad_rows[:, :, :]).then_inc(s_pad, 16)
                sp.dma_start(experts[:, e, 0:HID], w1[e]).then_inc(s_ldx, 16)
                sp.dma_start(experts[:, e, HID + HC:2 * HID + HC].rearrange("p (c d) -> p c d", c=HC),
                             w2[e].rearrange("(c p) d -> p c d", p=P)).then_inc(s_ldx, 16)
                sp.dma_start(experts[:, e, 2 * HID + HC:EXP],
                             b2[e].rearrange("(o d) -> o d", o=1).broadcast_to([P, E])).then_inc(s_ldx, 16)

            def slot(it, g):
                G, T, s = BODY * it + g, 2 * it + g // CG, g % CG
                par = (g // CG) % 2
                if s == 2 and live(T + 2, CHUNKS):
                    load_x_at(T + 2, par)
                if isinstance(it, int) and it == 0 and 6 <= g < 6 + NE:
                    late_load(g - 6)
                if live(G - 1, GROUPS):
                    apart(sp, s_tmcp, G)
                    gp = (g - 1) % BODY
                    for h in range(HG):
                        row = SLOT * h + SHIFT
                        sp.dma_start(
                            q_diag[row:row + 1, gp // CG, gp % CG, h, :].bitcast(F32).rearrange("o (k i) -> o k i", k=NBLK),
                            nshiftT[NBLK * h:NBLK * h + NBLK, (g - 1) % 2, :].bitcast(F32)).then_inc(s_m[(g - 1) % 2], 16)
                if s == 1 and live(T + 1, CHUNKS) and live(T, CHUNKS):
                    store_v(T + 1)
                if s == 4 and live(T + 1, CHUNKS) and live(T, CHUNKS):
                    load_v(T + 1, 1 - par)
                if s == QUERY_SLOTS[-1] + 1 and live(T + 1, CHUNKS) and live(T, CHUNKS):
                    spread_q(T + 1, 1 - par)
                if g % GB == 2 and live(GB * it + g // GB - 2, NB):
                    B = GB * it + g // GB - 2
                    apart(sp, s_h2, B)
                    sp.dma_start(cs_all[:, :, :], rows_of(mod_rows, B)[:, 3:5, :].broadcast_to([P, 2, E])).then_inc(s_cs, 16)
                if g % GB == 1:
                    B = GB * it + g // GB
                    if live(B, NB):
                        apart(sp, s_fin, B - 1)
                        sp.dma_start(x_res[:, B_par(g), :, :],
                                     rows_of(x_tok, B).rearrange("b p k e -> p (b k) e")).then_inc(s_xr[B_par(g)], 16)
                        sp.dma_start(ga_all[:, B_par(g), :],
                                     rows_of(mod_rows, B)[:, 2, :].to_broadcast([P, E])).then_inc(s_xr[B_par(g)], 16)
                    if live(B - 2, NB):
                        apart(sp, s_fin, B - 1)
                        sp.dma_start(rows_of(x_mid_tok, B - 2).rearrange("b p k e -> p (b k) e"),
                                     x_new[:, B_par(g), :, :]).then_inc(s_st[B_par(g)], 16)

            def B_par(g):
                return (g // GB) % 2

            over_groups(sp, slot)
            for b in range(2):
                sp.wait_ge(s_st[b], 16 * NB // 2)

            sp.wait_ge(s_tab, TAB_STEPS)
            sp.wait_ge(s_sc, 16 * NB * NBLK * TOPK)

            def last_load(t, r):
                for k in range(TOPK):
                    sp.dma_start(fin_y[:, r, k, :, :],
                                 y_token[k * TOK:(k + 1) * TOK].rearrange("(t a p) e -> t p a e", a=NT, p=P)[
                                     bass.ds(t, 1)].rearrange("t p a e -> p (t a) e")).then_inc(s_fl[r], 16)

            def last_store(t, r, n):
                apart(sp, s_fc[r], n + 1)
                sp.dma_start(rows_of(out_tok, CB * t, CB).rearrange("b p k e -> p b k e"),
                             fin_x[:, bass.ds(t, 1), :, :].rearrange("p o (b k) e -> p (o b) k e", b=CB)).then_inc(s_fs, 16)

            def tile_load(it, u):
                st = SU * it + u
                if not live(st, STEPS):
                    return
                row = sp.value_load(table[0:1, 0, bass.ds(st, 1)], min_val=0, max_val=NE * REGION - TR)
                apart(sp, s_dest, 2 * (st - SU + 1))
                sp.dma_start(xs[:, u, :, :],
                             x_expert[bass.ds(row, TR)].rearrange("(a p) w -> p a w", p=P)).then_inc(s_xs[u], 16)

            for u in range(SU):
                tile_load(0, u)
            assert STEPS // SU >= CHUNKS + 2
            for t in range(CHUNKS):
                sp.dma_start(fin_x[:, t, :, :].rearrange("p (b k) e -> p b k e", b=CB),
                             x_mid_tok[CB * t:CB * t + CB].rearrange("b p k e -> p b k e")).then_inc(s_fx, 16)
            sp.wait_ge(s_pv, GROUPS)
            with sp.Fori(1, CHUNKS + 1) as it:
                for u in range(SU):
                    tile_load(it, u)
                sp.dma_start(fin_gb[:, bass.ds(CB * it - CB, CB), :], rows_of(mod_rows, CB * it - CB, CB)[:, 5, :].rearrange(
                    "(o b) e -> o b e", o=1).broadcast_to([P, CB, E])).then_inc(s_fx, 16)
            for body in range(CHUNKS + 1, STEPS // SU):
                for u in range(SU):
                    tile_load(body, u)
            for q in range(2):
                sp.wait_ge(s_ysc[q], 16 * NBLK * STEPS // 2)

            for r in range(FIN):
                last_load(r, r)
            with sp.Fori(0, CHUNKS // FIN - 1) as it:
                for r in range(FIN):
                    last_store(FIN * it + r, r, it)
                    last_load(FIN * it + FIN + r, r)
            for r in range(FIN):
                last_store(CHUNKS - FIN + r, r, CHUNKS // FIN - 1)
            sp.wait_ge(s_fs, 16 * CHUNKS)

        @block.gpsimd
        def _(pool):
            pool.memset(c_in[:, :], 0.0).then_inc(s_pool0, 1)
            pool.memset(ident[:, :], 0.0).then_inc(s_pool0, 1)
            pool.iota(row_id[:, :], pattern=[[0, 1]], base=0, channel_multiplier=1).then_inc(s_pool0, 1)
            pool.wait_ge(s_pool0, 3)
            pool.affine_select(out=ident[:, :], in_=ident[:, :], compare_op=ALU.not_equal, fill=1.0, base=0,
                               pattern=[[-1, P]], channel_multiplier=1).then_inc(s_pool0, 1)
            pool.memset(bias_lhs[:, :, :, :], 0.0).then_inc(s_pool0, 1)
            pool.memset(q_diag[:, :, :, :, :].bitcast(F32).rearrange("p a g h i -> p (a g h i)"), 0.0).then_inc(s_pool0, 1)
            pool.memset(tri[:, :, :], 1.0).then_inc(s_pool0, 1)
            pool.memset(neg[:, :, :], 0.0).then_inc(s_pool0, 1)
            pool.memset(nfloor[:, :], 0.0).then_inc(s_pool0, 1)
            pool.memset(v_slot[:, :, :, :, :, :].rearrange("p a k g h d -> p (a k g h d)"), 0.0).then_inc(s_pool0, 1)
            pool.wait_ge(s_pool0, 10)
            pool.memset(v_slot[:, :, :, :, :, D:D + 1].rearrange("p a k g h d -> p (a k g h) d"), 1.0).then_inc(s_pool0, 1)
            pool.affine_select(out=tri[:, 0, :], in_=tri[:, 0, :], compare_op=ALU.is_ge, fill=0.0, base=0,
                               pattern=[[-1, P]], channel_multiplier=1).then_inc(s_pool0, 1)
            pool.affine_select(out=tri[:, 1, :], in_=tri[:, 1, :], compare_op=ALU.is_ge, fill=0.0, base=-1,
                               pattern=[[1, P]], channel_multiplier=-1).then_inc(s_pool0, 1)
            pool.affine_select(out=neg[:, 0, :], in_=neg[:, 0, :], compare_op=ALU.is_gt, fill=MASKED, base=0,
                               pattern=[[-1, P]], channel_multiplier=1).then_inc(s_pool0, 1)
            pool.affine_select(out=neg[:, 1, :], in_=neg[:, 1, :], compare_op=ALU.is_ge, fill=MASKED, base=0,
                               pattern=[[1, P]], channel_multiplier=-1).then_inc(s_pool0, 1)
            pool.affine_select(out=nfloor[:, 1:2], in_=nfloor[:, 1:2], compare_op=ALU.not_equal, fill=-MASKED, base=0,
                               pattern=[[0, 1]], channel_multiplier=1).then_inc(s_pool0, 1)
            pool.wait_ge(s_pool0, 16)
            pool.tensor_copy(identb[:, :], ident[:, :]).then_inc(s_pool0, 1)
            pool.tensor_copy(before_b[:, :], tri[:, 1, :]).then_inc(s_pool0, 1)
            pool.memset(ones_b[:, :], 1.0).then_inc(s_pool0, 1)
            pool.memset(ones_row[:, :], 1.0).then_inc(s_pool0, 1)
            pool.memset(pad_rows[:, :, :], 0.0).then_inc(s_pool0, 1)
            pool.iota(expert_idi[:, :], pattern=[[1, NE]], base=0, channel_multiplier=0).then_inc(s_pool0, 1)
            pool.iota(pad_idi[:, :], pattern=[[P, NBLK]], base=0, channel_multiplier=1).then_inc(s_pool0, 1)
            pool.iota(step_idi[:, :], pattern=[[1, STEPS]], base=0, channel_multiplier=0).then_inc(s_pool0, 1)
            pool.wait_ge(s_pool0, 24)
            pool.tensor_copy(pad_id[:, :], pad_idi[:, :]).then_inc(s_pool0, 1)
            pool.tensor_copy(expert_id[:, :], expert_idi[:, :]).then_inc(s_pool0, 1)
            pool.tensor_copy(step_id[:, :], step_idi[:, :]).then_inc(s_pool0, 1)
            pool.wait_ge(s_pool0, 27)
            for k in range(TOPK):
                pool.tensor_scalar(token_id[:, k, :], pad_id[:, :], float(k * TOK), None, ALU.add).then_inc(s_pool0, 1)
            pool.tensor_scalar(pad_rows[:, :, E], pad_id[:, :], float(TOPK * TOK), None, ALU.add).then_inc(s_pool0, 1)
            for q in range(2):
                pool.tensor_scalar(away[:, q, :], pad_id[:, :], float(TOPK * TOK + TR * q), None, ALU.add).then_inc(s_pool0, 1)
            pool.tensor_scalar(next_row[:, :], expert_id[:, :], float(REGION), None, ALU.mult).then_inc(s_pool0, 1)

            def slot(it, g):
                G, T, s = BODY * it + g, 2 * it + g // CG, g % CG
                par = (g // CG) % 2
                if live(G - 2, GROUPS):
                    apart(pool, s_exp, HG * (G - 1))
                    pr = probs[:, g % 2, :, :]
                    pool.affine_select(out=pr[:, :, P:2 * P], in_=pr[:, :, P:2 * P], compare_op=ALU.is_ge, fill=0.0,
                                       base=0, pattern=[[0, HG], [-1, P]], channel_multiplier=1).then_inc(s_aff, 1)
                    pool.affine_select(out=pr[:, :, 2 * P:3 * P], in_=pr[:, :, 2 * P:3 * P], compare_op=ALU.is_ge,
                                       fill=0.0, base=-1, pattern=[[0, HG], [1, P]],
                                       channel_multiplier=-1).then_inc(s_aff, 1)
                if isinstance(it, int) and it == 0 and g == BODY - 1:
                    pool.wait_ge(s_pad, 16 * NE)
                if g % GB in (1, 2) and live(GB * it + g // GB - 4, NB):
                    B, b = GB * it + g // GB - 4, (g // GB) % 2
                    if g % GB == 1:
                        apart(pool, s_row, B + 1)
                        apart(pool, s_gate, B + 1)
                        apart(pool, s_dup, B + 1)
                    k = g % GB - 1
                    for e in range(TOPK):
                        pool.indirect_dma_start(x_expert[:, :], bass.IndirectOffsetOnAxis(ap=row_i[:, b, k, e:e + 1], axis=0),
                                                h2_rows[:, b, e, k, :], None).then_inc(s_sc, 16)
                if g % GB == 3 and live(GB * it + g // GB - 1, NB):
                    B = GB * it + g // GB - 1
                    b = (g // GB - 1) % 2
                    apart(pool, s_mkcp, B + 1)
                    apart(pool, s_e, B + 1)
                    for k in range(NBLK):
                        e_k = e_shift[:, b, :].rearrange("p (n k) -> p k n", k=NBLK)[:, k, :]
                        pool.tensor_tensor(o_tmp[:, k, :, :], o_mask[:, b, k, :, :],
                                           e_k.unsqueeze(2).broadcast_to([P, H, NV]), ALU.mult).then_inc(s_f1, 1)
                    apart(pool, s_f1, NBLK * (B + 1))
                    apart(pool, s_tocp, GB * (B + 1))
                    rows = o_rows[:, b, :, :, :].rearrange("p k h v -> p (k h v)")
                    pool.tensor_tensor(rows, rows, o_tmp[:, :, :, :].rearrange("p k h v -> p (k h v)"),
                                       ALU.add).then_inc(s_f2, 1)
                if g % GB == 3 and live(GB * it + g // GB - 2, NB):
                    B, b = GB * it + g // GB - 2, (g // GB) % 2
                    apart(pool, s_n2, NBLK * (B + 1))
                    apart(pool, s_cs, 16 * (B + 1))
                    pool.tensor_tensor(h2f[:, :, :], h2f[:, :, :], cs_all[:, 1, :].unsqueeze(1).broadcast_to([P, NBLK, E]),
                                       ALU.mult).then_inc(s_m2, 1)
                    apart(pool, s_m2, B + 1)
                    apart(pool, s_sc, 16 * NBLK * TOPK * (B - 1))
                    pool.tensor_tensor(h2_rows[:, b, 0, :, 0:E], h2f[:, :, :],
                                       cs_all[:, 0, :].unsqueeze(1).broadcast_to([P, NBLK, E]), ALU.add).then_inc(s_h2, 1)
                    apart(pool, s_id, 2 * B)
                    pool.tensor_copy(h2_rows[:, b, :, :, E], token_id[:, :, :]).then_inc(s_id, 1)
                    apart(pool, s_id, 2 * B + 1)
                    pool.tensor_scalar(token_id[:, :, :], token_id[:, :, :], float(S), None, ALU.add).then_inc(s_id, 1)
                if g % GB == 0 and live(GB * it + g // GB - 2, NB):
                    B = GB * it + g // GB - 2
                    b = (g // GB) % 2
                    apart(pool, s_den, B + 1)
                    rd = rden[:, b, :, :].rearrange("p k h -> p (k h)")
                    apart(pool, s_fin, B)
                    pool.tensor_tensor(o_att[:, :, :].rearrange("p k (h d) -> p (k h) d", d=D),
                                       o_rows[:, b, :, :, 0:D].rearrange("p k h d -> p (k h) d"),
                                       rd.unsqueeze(2).broadcast_to([P, NBLK * H, D]), ALU.mult).then_inc(s_f3, 1)
                    apart(pool, s_f3, B + 1)
                    apart(pool, s_xr[b], 32 * (2 * it + (g // GB - 2) // 2 + 1))
                    pool.tensor_tensor(o_att[:, :, :], o_att[:, :, :],
                                       ga_all[:, b, :].unsqueeze(1).broadcast_to([P, NBLK, E]), ALU.mult).then_inc(s_f4, 1)
                    apart(pool, s_f4, B + 1)
                    apart(pool, s_st[b], 16 * (2 * it + (g // GB - 2) // 2))
                    pool.tensor_tensor(x_new[:, b, :, :], o_att[:, :, :], x_res[:, b, :, :], ALU.add).then_inc(s_fin, 1)

            over_groups(pool, slot)

            def scatter_y(it, u):
                st = SU * it + u - 1
                if not live(st, STEPS):
                    return
                apart(pool, s_yout, NBLK * (st + 1))
                apart(pool, s_dest, 2 * st + 2)
                apart(pool, s_ysc[(u - 1) % 2], 16 * NBLK * (SU // 2 * it + (u - 1) // 2))
                for k in range(NBLK):
                    pool.indirect_dma_start(y_token[:, :], bass.IndirectOffsetOnAxis(ap=dest[:, (u - 1) % SU, k:k + 1], axis=0),
                                            y_out[:, (u - 1) % 2, k, :], None).then_inc(
                                                s_ysc[(u - 1) % 2], 16)

            over_steps(pool, scatter_y)
            pool.wait_ge(s_fx, 16 * 2 * CHUNKS)
            with pool.Fori(0, CHUNKS // FIN) as it:
                finish(pool, it, FIN - 1)

        @block.vector
        def _(dve):
            dve0 = [0]

            def step(ins):
                dve0[0] += 1
                ins.then_inc(s_dve0, 1)
                dve.wait_ge(s_dve0, dve0[0])

            def free_step(ins):
                dve0[0] += 1
                ins.then_inc(s_dve0, 1)

            dve.wait_ge(s_ld, 16 * NLD)
            dve.wait_ge(s_act0, 1)
            step(dve.tensor_scalar(c_exp[:, :], c_exp[:, :], 1.0, None, ALU.add))
            step(dve.reciprocal(c_exp[:, :], c_exp[:, :]))
            step(dve.tensor_tensor(c_in[:, :], c_in[:, :], c_exp[:, :], ALU.mult))
            assert dve0[0] == DVE_SILU

            def layer_stats(t, par, n):
                dve.wait_ge(s_x[par], 16 * (n + 1))
                after(dve, s_aggr, NT * t)
                for a in range(NT):
                    dve.bn_stats(stats[:, a, :], x_in[:, par, a, :]).then_inc(s_stats, 1)

            def layer_mean(t):
                apart(dve, s_stats, NT * (t + 1))
                apart(dve, s_off, t)
                for a in range(NT):
                    dve.bn_aggr(mean_var[:, a, :], stats[:, a, :]).then_inc(s_aggr, 1)

            def layer_guess(t):
                dve.wait_ge(s_aggr, NT * (t + 1))
                after(dve, s_xn, NT * t)
                rsqrt_guess(dve, s_rstd, RSTD_STEPS * t, rstd[:, :], mean_var[:, :, 1], half_var[:, :])

            def layer_newton(t, k):
                rsqrt_newton(dve, s_rstd, RSTD_STEPS * t, k, rstd[:, :], half_var[:, :], r_tmp[:, :])

            def layer_offset(t):
                dve.wait_ge(s_rstd, RSTD_STEPS * (t + 1))
                dve.scalar_tensor_tensor(out=mean_off[:, :], in0=mean_var[:, :, 0], scalar=-1.0, in1=rstd[:, :],
                                         op0=ALU.mult, op1=ALU.mult).then_inc(s_off, 1)

            def layer_terms(t, par, n):
                layer_stats(t, par, n)
                layer_mean(t)
                layer_guess(t)
                for k in range(NEWTON):
                    layer_newton(t, k)
                layer_offset(t)

            def values(u):
                dve.wait_ge(s_pB, (CQ + 1) * u + 1)
                after(dve, s_vst, 16 * u)
                dve.tensor_tensor(v_tok[:, :, :], pP[1][:, :].rearrange("p (a e) -> p a e", a=NT),
                                  bv_all[:, :].unsqueeze(1).broadcast_to([P, NT, E]), ALU.add).then_inc(s_v, 1)

            def pack(u, n, i, par):
                if n == 0:
                    dve.wait_ge(s_rq, CQ * u + i + 1)
                    if i == 0:
                        after(dve, s_qb, 16 * HG * u)
                    dst = q_pack[:, :, :]
                else:
                    dve.wait_ge(s_rk, CQ * u + i + 1)
                    if i == 0:
                        after(dve, s_s2, CG * HG * (u - 1))
                    dst = k_pack[:, par, :, :]
                dst = dst.rearrange("p g i -> p (g i)").rearrange("p (n c) -> p c n", c=C)[:, 4 * i:4 * i + 4, :]
                dve.scalar_tensor_tensor(out=dst, in0=rounded[:, n, :, :].bitcast(F32), scalar=low_mask[:, n:n + 1],
                                         in1=pP[n][:, :].rearrange("p (c n) -> p c n", c=4),
                                         op0=ALU.mult, op1=ALU.add).then_inc(s_q if n == 0 else s_k, 1)

            def batch_stats(B, b):
                dve.wait_ge(s_fin, B + 1)
                after(dve, s_aggr2, NBLK * B)
                for k in range(NBLK):
                    dve.bn_stats(stats2[:, k, :], x_new[:, b, k, :]).then_inc(s_stats2, 1)

            def batch_mean(B):
                apart(dve, s_stats2, NBLK * (B + 1))
                apart(dve, s_off2, B)
                for k in range(NBLK):
                    dve.bn_aggr(mean_var2[:, k, :], stats2[:, k, :]).then_inc(s_aggr2, 1)

            def batch_guess(B):
                dve.wait_ge(s_aggr2, NBLK * (B + 1))
                after(dve, s_n2, NBLK * B)
                rsqrt_guess(dve, s_rstd2, RSTD_STEPS * B, rstd2[:, :], mean_var2[:, :, 1], half_var2[:, :])

            def batch_newton(B, k):
                rsqrt_newton(dve, s_rstd2, RSTD_STEPS * B, k, rstd2[:, :], half_var2[:, :], r_tmp2[:, :])

            def batch_offset(B):
                dve.wait_ge(s_rstd2, RSTD_STEPS * (B + 1))
                dve.scalar_tensor_tensor(out=mean_off2[:, :], in0=mean_var2[:, :, 0], scalar=-1.0, in1=rstd2[:, :],
                                         op0=ALU.mult, op1=ALU.mult).then_inc(s_off2, 1)

            def take_logits(B):
                dve.wait_ge(s_lg, B + 1)
                dve.tensor_copy(logits[:, :, :].rearrange("p k x -> p (k x)"), pO[:, S:S + NBLK * NE]).then_inc(s_lgc, 1)

            def largest(B):
                apart(dve, s_lgc, B + 1)
                for k in range(NBLK):
                    dve.max(top[:, k, :], logits[:, k, :]).then_inc(s_mx, 1)

            def largest_at(B):
                apart(dve, s_mx, NBLK * (B + 1))
                for k in range(NBLK):
                    dve.max_index(top_at[:, k, :], top[:, k, :], logits[:, k, :]).then_inc(s_ix, 1)
                after(dve, s_eg, B)
                dve.tensor_tensor(top_arg[:, :, :], top[:, :, :], top[:, :, 0:1].broadcast_to([P, NBLK, NE]),
                                  ALU.subtract).then_inc(s_ein, 1)
                dve.wait_ge(s_ix, NBLK * (B + 1))
                dve.tensor_copy(top_atf[:, :, :], top_at[:, :, 0:TOPK]).then_inc(s_ixf, 1)

            def mark_chosen(B):
                dve.wait_ge(s_ixf, B + 1)
                for k in range(NBLK):
                    dve.tensor_tensor(chosen[:, k, :, :], expert_id[:, :].unsqueeze(1).broadcast_to([P, TOPK, NE]),
                                      top_atf[:, k, :].unsqueeze(2).broadcast_to([P, TOPK, NE]), ALU.is_equal).then_inc(s_oh, 1)
                dve.wait_ge(s_oh, NBLK * (B + 1))
                dve.tensor_tensor(chosen_b[:, :, :], chosen[:, :, 0, :], chosen[:, :, 1, :], ALU.add).then_inc(s_ch, 1)

            def places(B):
                dve.wait_ge(s_pre, B + 1)
                dve.tensor_tensor(place[:, :, :], pO[:, S:S + NBLK * NE].rearrange("p (k x) -> p k x", k=NBLK),
                                  next_row[:, :].unsqueeze(1).broadcast_to([P, NBLK, NE]), ALU.add).then_inc(s_pos, 1)
                dve.wait_ge(s_pos, 2 * B + 1)
                dve.tensor_tensor(next_row[:, :], pO[:, S + NBLK * NE:S + (NBLK + 1) * NE], next_row[:, :],
                                  ALU.add).then_inc(s_pos, 1)

            def chosen_places(B):
                for k in range(NBLK):
                    dve.tensor_tensor(place_of[:, k, :, :], chosen[:, k, :, :],
                                      place[:, k, :].unsqueeze(1).broadcast_to([P, TOPK, NE]), ALU.mult).then_inc(s_prod, 1)

            def rows_f(B):
                dve.wait_ge(s_prod, NBLK * (B + 1))
                dve.tensor_reduce(row_f[:, :, :].rearrange("p k e -> p (k e)"),
                                  place_of[:, :, :, :].rearrange("p k e x -> p (k e) x"), AX_X, ALU.add).then_inc(s_rowf, 1)

            def rows_i(B, b):
                dve.wait_ge(s_rowf, B + 1)
                dve.tensor_copy(row_i[:, b, :, :], row_f[:, :, :]).then_inc(s_row, 1)

            def gate_sums(B):
                dve.wait_ge(s_eg, B + 1)
                dve.tensor_reduce(gate_sum[:, :], top_exp[:, :, :], AX_X, ALU.add).then_inc(s_gsum, 1)

            def gate_inverse(B):
                dve.wait_ge(s_gsum, B + 1)
                dve.reciprocal(gate_inv[:, :], gate_sum[:, :]).then_inc(s_ginv, 1)

            def gates(B, b):
                dve.wait_ge(s_ginv, B + 1)
                dve.tensor_tensor(h2_rows[:, b, :, :, E + 1].rearrange("p e k -> p k e"), top_exp[:, :, 0:TOPK],
                                  gate_inv[:, :].unsqueeze(2).broadcast_to([P, NBLK, TOPK]), ALU.mult).then_inc(s_gate, 1)

            layer_terms(0, 0, 0)
            dve.wait_ge(s_pe0, 1)
            free_step(dve.tensor_copy(siluT[:, :], pP[0][:, 3 * P:3 * P + NB]))
            for n in range(2):
                view = pP[0][:, n * P:(n + 1) * P].rearrange("p (c d) -> p c d", d=D)
                scale = float(D) ** -0.5 if n == 0 else 1.0
                free_step(dve.memset(w_slot[:, n, :, SHIFT:SLOT], 0.0))
                for part in range(3):
                    free_step(dve.tensor_scalar(w_slot[:, n, :, part * D:(part + 1) * D], view, scale, None, ALU.mult))
            step(dve.tensor_copy(wvT[:, :], pP[0][:, 2 * P:3 * P]))
            assert dve0[0] == DVE_WEIGHTS
            dve.wait_ge(s_pe0, 2)
            for half in range(2):
                free_step(dve.tensor_copy(mod_sb[:, 3 * half:3 * half + 3, :].rearrange("b m e -> b (m e)"),
                                          pP[half][0:NB, 0:3 * E]))
            assert dve0[0] == DVE_MOD
            for half in range(2):
                free_step(dve.tensor_copy(shiftT[:, half, :], pB[:, (2 * half) * NB:(2 * half + 1) * NB]))
                free_step(dve.tensor_scalar(scaleT[:, half, :], pB[:, (2 * half + 1) * NB:(2 * half + 2) * NB], 1.0, None, ALU.add))
            dve.wait_ge(s_dve0, DVE_COLUMNS)
            assert dve0[0] == DVE_COLUMNS
            dve.wait_ge(s_pool0, 5)
            free_step(dve.tensor_scalar(row_bits[:, :], row_id[:, :], 24, None, ALU.bitwise_and))
            step(dve.tensor_scalar(bias_bits[:, :], row_id[:, :], 12, None, ALU.bitwise_and))
            free_step(dve.tensor_scalar(low_mask[:, 0:1], row_bits[:, :], 16.0, -1.0, ALU.is_equal, ALU.mult))
            free_step(dve.tensor_scalar(low_mask[:, 1:2], row_bits[:, :], 8.0, -1.0, ALU.is_equal, ALU.mult))
            for part in range(3):
                free_step(dve.tensor_scalar(part_row[:, part:part + 1], bias_bits[:, :], float(4 * part), None, ALU.is_equal))
            dve.wait_ge(s_bias, 16 * 6)
            step(dve.tensor_scalar(bias_row[:, 0, :, :], bias_row[:, 0, :, :], float(D) ** -0.5, None, ALU.mult))
            step(dve.tensor_copy(bias_part[:, 0, :, :, :], bias_row[:, :, :, :]))
            step(dve.tensor_tensor(bias_rest[:, :, :, :], bias_row[:, :, :, :], bias_part[:, 0, :, :, :], ALU.subtract))
            step(dve.tensor_copy(bias_part[:, 1, :, :, :], bias_rest[:, :, :, :]))
            step(dve.tensor_tensor(bias_rest[:, :, :, :], bias_rest[:, :, :, :], bias_part[:, 1, :, :, :], ALU.subtract))
            step(dve.tensor_copy(bias_part[:, 2, :, :, :], bias_rest[:, :, :, :]))
            step(dve.tensor_scalar(bias_mine[:, 0, :, :, :], bias_part[:, 0, :, :, :], part_row[0:12, 0:1], None, ALU.mult))
            for part in range(1, 3):
                step(dve.scalar_tensor_tensor(out=bias_mine[:, part, :, :, :], in0=bias_part[:, part, :, :, :],
                                              scalar=part_row[0:12, part:part + 1], in1=bias_mine[:, part - 1, :, :, :],
                                              op0=ALU.mult, op1=ALU.add))
            for n in range(2):
                for part in range(3):
                    dst = bias_lhs[0:12, n, :, :].rearrange("r q (h m) -> r q h m", h=HG)[:, :, :, part * D:(part + 1) * D]
                    free_step(dve.tensor_copy(dst, bias_mine[:, 2, n, :, :].unsqueeze(2).broadcast_to([12, CQ, HG, D])))
            free_step(dve.memset(bias_lhs[0:4, 1, :, :].rearrange("r q (h m) -> r (q h) m", h=HG)[:, :, SHIFT:SHIFT + 1], 1.0))
            step(dve.tensor_scalar(row_bits[:, :], row_id[:, :], 3, None, ALU.bitwise_and))
            step(dve.tensor_copy(quad[:, :], row_bits[:, :]))
            for c in range(4):
                free_step(dve.tensor_scalar(bias_ind[:, c, :], quad[:, 0:1].broadcast_to([P, P]), float(c), None, ALU.is_equal))
            assert dve0[0] == DVE_BIAS, dve0[0]
            values(0)
            layer_terms(1, 1, 0)
            for i in range(CQ):
                pack(0, 0, i, 0)
                pack(0, 1, i, 0)
            dve.wait_ge(s_dve0, DVE_BIAS)
            rows = mod_sb[:, :, :].rearrange("b (l m) e -> b l m e", m=3)
            scales, held = rows[:, :, 1, :], rows[:, :, 2, :]
            free_step(dve.tensor_scalar(scales, scales, 1.0, None, ALU.add))
            step(dve.tensor_scalar(gate_sign[:, :, :], held, 0.0, 2.0, ALU.is_ge, ALU.mult))
            step(dve.tensor_scalar(gate_sign[:, :, :], gate_sign[:, :, :], -1.0, None, ALU.add))
            step(dve.tensor_tensor(held, held, gate_sign[:, :, :], ALU.mult))
            step(dve.tensor_scalar(held, held, 0.25, None, ALU.max))
            step(dve.tensor_tensor(held, held, gate_sign[:, :, :], ALU.mult))
            assert dve0[0] == DVE_ROWS
            dve.wait_ge(s_pe0, 3)
            step(dve.tensor_copy(experts[:, :, HID:HID + HC], pP[0][:, 0:NE * HC].rearrange("p (x c) -> p x c", c=HC)))
            step(dve.tensor_copy(wgT[:, :], pP[0][:, NE * HC:NE * HC + NE]))
            assert dve0[0] == DVE_LATE
            dve.wait_ge(s_pool0, POOL_SETUP)

            def slot(it, g):
                G, T, s = BODY * it + g, 2 * it + g // CG, g % CG
                par = (g // CG) % 2
                prep = live(T + 1, CHUNKS) and live(T, CHUNKS)

                def maxima(h):
                    dve.wait_ge(s_s1, HG * G + h + 1)
                    dve.tensor_reduce(row_max[:, g % 2, h, :], pS1[h % 2][:, :].rearrange("p (k j) -> p k j", k=NBLK),
                                      AX_X, ALU.max).then_inc(s_red, 1)

                B, j = GB * it + g // GB, g % GB
                b = (g // GB) % 2

                if live(G, GROUPS):
                    maxima(0)
                if j == 2 and live(B - 3, NB):
                    take_logits(B - 3)
                    largest(B - 3)
                if j == 3 and live(B - 3, NB):
                    places(B - 3)
                if j == 0 and live(B - 4, NB):
                    rows_i(B - 4, b)
                    gates(B - 4, b)
                if j == 3 and live(B - 2, NB):
                    batch_newton(B - 2, 1)
                if s == 5 and live(T + 2, CHUNKS):
                    layer_mean(T + 2)
                if s == 6 and live(T + 2, CHUNKS):
                    layer_offset(T + 2)
                if live(G, GROUPS):
                    maxima(1)
                if prep and s - 1 in KEY_SLOTS:
                    pack(T + 1, 1, KEY_SLOTS.index(s - 1), 1 - par)
                if j == 0 and live(B - 1, NB):
                    dve.wait_ge(s_nm, GB * B)
                    after(dve, s_f1, NBLK * (B - 2))
                    dve.tensor_scalar(e_arg[:, (g // GB - 1) % 2, :],
                                      nshift[:, (g // GB - 1) % 4, :, :, :].bitcast(F32).rearrange("p g h k -> p (g h k)"),
                                      0.0, None, ALU.min).then_inc(s_earg, 1)
                if j == 2 and live(B - 3, NB):
                    largest_at(B - 3)
                if j == 3 and live(B - 3, NB):
                    chosen_places(B - 3)
                    gate_sums(B - 3)
                if j == 3 and live(B - 2, NB):
                    batch_newton(B - 2, 2)
                if s == 5 and live(T + 2, CHUNKS):
                    layer_guess(T + 2)
                if live(G, GROUPS):
                    maxima(2)
                if j == 2 and live(B - 3, NB):
                    mark_chosen(B - 3)
                if j == 2 and live(B - 2, NB):
                    batch_guess(B - 2)
                if j == 3 and live(B - 2, NB):
                    batch_offset(B - 2)
                if j == 3 and live(B - 3, NB):
                    rows_f(B - 3)
                    gate_inverse(B - 3)
                if j == 1 and live(B - 2, NB):
                    batch_stats(B - 2, b)
                if s == 5 and live(T + 2, CHUNKS):
                    layer_newton(T + 2, 0)
                if j == 0 and live(B - 2, NB):
                    dve.wait_ge(s_f2, B - 1)
                    dve.reciprocal(rden[:, b, :, :].rearrange("p k h -> p (k h)"),
                                   o_rows[:, b, :, :, D].rearrange("p k h -> p (k h)")).then_inc(s_den, 1)
                if live(G, GROUPS):
                    maxima(3)
                    dve.wait_ge(s_red, HG * G + HG)
                    dve.scalar_tensor_tensor(out=nshift[:, (g // GB) % 4, g % GB, :, :], in0=row_max[:, g % 2, :, :],
                                             scalar=-1.0, in1=nfloor[:, :].unsqueeze(1).broadcast_to([P, HG, NBLK]),
                                             op0=ALU.mult, op1=ALU.min).then_inc(s_nm, 1)
                if prep and s in QUERY_SLOTS:
                    pack(T + 1, 0, QUERY_SLOTS.index(s), 1 - par)
                if prep and s == 0:
                    values(T + 1)
                if j == 1 and live(B - 2, NB):
                    batch_mean(B - 2)
                if j == 2 and live(B - 2, NB):
                    batch_newton(B - 2, 0)
                if s == 4 and live(T + 2, CHUNKS):
                    layer_stats(T + 2, par, it + 1)
                if s == 5 and live(T + 2, CHUNKS):
                    layer_newton(T + 2, 1)
                    layer_newton(T + 2, 2)

            over_groups(dve, slot)

            dve.wait_ge(s_pos, 2 * NB)
            tab = [0]

            def entry(ins):
                tab[0] += 1
                ins.then_inc(s_tab, 1)
                dve.wait_ge(s_tab, tab[0])

            entry(dve.scalar_tensor_tensor(out=count_f[:, :], in0=expert_id[:, :], scalar=-float(REGION),
                                           in1=next_row[:, :], op0=ALU.mult, op1=ALU.add))
            entry(dve.tensor_scalar(tiles_i[:, :], count_f[:, :], float(TR - 1), None, ALU.add))
            entry(dve.tensor_scalar(tiles_i[:, :], tiles_i[:, :], TR.bit_length() - 1, None, ALU.logical_shift_right))
            entry(dve.tensor_copy(tiles[:, :], tiles_i[:, :]))
            entry(dve.tensor_tensor_scan(tiles_sum[:, :], ones_row[:, :], tiles[:, :], 0.0, ALU.mult, ALU.add))
            steps_of = step_id[:, :].unsqueeze(2).broadcast_to([P, STEPS, NE - 1])
            entry(dve.tensor_tensor(past[:, :, :], steps_of, tiles_sum[:, 0:NE - 1].unsqueeze(1).broadcast_to(
                [P, STEPS, NE - 1]), ALU.is_ge))
            entry(dve.tensor_tensor(past_n[:, :, :], past[:, :, :], tiles[:, 0:NE - 1].unsqueeze(1).broadcast_to(
                [P, STEPS, NE - 1]), ALU.mult))
            entry(dve.tensor_reduce(step_expert[:, :], past[:, :, :], AX_X, ALU.add))
            entry(dve.tensor_reduce(step_base[:, :], past_n[:, :, :], AX_X, ALU.add))
            entry(dve.tensor_tensor(step_row[:, :], step_id[:, :], step_base[:, :], ALU.subtract))
            entry(dve.tensor_scalar(step_row[:, :], step_row[:, :], float(TR), None, ALU.mult))
            entry(dve.tensor_scalar(last_row[:, :], count_f[:, :], -float(TR), 0.0, ALU.add, ALU.max))
            entry(dve.tensor_tensor(last_more[:, :], last_row[:, 1:NE], last_row[:, 0:NE - 1], ALU.subtract))
            entry(dve.tensor_tensor(past_row[:, :, :], past[:, :, :], last_more[:, :].unsqueeze(1).broadcast_to(
                [P, STEPS, NE - 1]), ALU.mult))
            entry(dve.tensor_reduce(step_lim[:, :], past_row[:, :, :], AX_X, ALU.add))
            entry(dve.tensor_scalar(step_lim[:, :], step_lim[:, :], last_row[:, 0:1], None, ALU.add))
            entry(dve.tensor_tensor(seen[:, :], step_row[:, :], step_lim[:, :], ALU.subtract))
            entry(dve.tensor_tensor(step_row[:, :], step_row[:, :], step_lim[:, :], ALU.min))
            entry(dve.scalar_tensor_tensor(out=step_row[:, :], in0=step_expert[:, :], scalar=float(REGION),
                                           in1=step_row[:, :], op0=ALU.mult, op1=ALU.add))
            entry(dve.tensor_copy(table[:, 0, :], step_row[0:1, :]))
            entry(dve.tensor_copy(table[:, 1, :], step_expert[0:1, :]))
            assert tab[0] == TAB_STEPS
            dve.wait_ge(s_pv, GROUPS)
            dve.wait_ge(s_mk, NB)
            dve.wait_ge(s_ldx, 16 * 3 * NE)

            def weights(st, r):
                e = dve.value_load(table[0:1, 1, bass.ds(st, 1)], min_val=0, max_val=NE - 1)
                after(dve, s_y, st - SU + 1)
                after(dve, s_ysum, st - SU + 1)
                dve.tensor_copy(w_ring[:, r, :], experts[:, bass.ds(e, 1), :].rearrange("p o n -> p (o n)")).then_inc(s_w, 1)

            def turned(st, r, x, n):
                dve.wait_ge(s_xt, st + 1)
                dve.tensor_copy(xsT[:, r, :], pB[:, 0:TR]).then_inc(s_xtc, 1)
                after(dve, s_dest, 2 * st)
                dve.scalar_tensor_tensor(out=parts[:, 0, :], in0=pad_id[:, :], scalar=seen[:, bass.ds(st, 1)],
                                         in1=away[:, r, :], op0=ALU.is_lt, op1=ALU.mult).then_inc(s_away, 1)
                dve.scalar_tensor_tensor(out=parts[:, 1, :], in0=xs[:, x, :, E], scalar=float(TOPK * TOK),
                                         in1=away[:, r, :], op0=ALU.is_ge, op1=ALU.mult).then_inc(s_away, 1)
                dve.wait_ge(s_away, 3 * st + 2)
                dve.tensor_tensor(parts[:, 0, :], parts[:, 0, :], parts[:, 1, :], ALU.max).then_inc(s_away, 1)
                dve.wait_ge(s_away, 3 * st + 3)
                after(dve, s_ysc[r], 16 * NBLK * (n - 1))
                dve.tensor_tensor(dest[:, x, :], parts[:, 0, :], xs[:, x, :, E], ALU.max).then_inc(s_dest, 1)
                dve.tensor_copy(row_gate[:, x, :], xs[:, x, :, E + 1]).then_inc(s_dest, 1)

            weights(0, 0)
            weights(1, 1)
            turned(0, 0, 0, 0)

            def expert_step(it, u):
                st = SU * it + u
                if live(st + 1, STEPS):
                    turned(st + 1, (u + 1) % 2, (u + 1) % SU, SU // 2 * it + (u + 1) // 2)
                if live(st + 2, STEPS):
                    weights(st + 2, (u + 2) % SU)
                if live(st - 1, STEPS):
                    r = (u - 1) % 2
                    dve.wait_ge(s_y, st)
                    after(dve, s_yout, NBLK * (st - 2))
                    dve.tensor_tensor(y_sum[:, r, :, :], pO[:, 0:NBLK * E].rearrange("p (k e) -> p k e", k=NBLK),
                                      w_ring[:, (u - 1) % SU, 2 * HID + HC:EXP].unsqueeze(1).broadcast_to([P, NBLK, E]),
                                      ALU.add).then_inc(s_ysum, 1)

            over_steps(dve, expert_step)

            dve.wait_ge(s_fx, 16 * 2 * CHUNKS)
            with dve.Fori(0, CHUNKS // FIN) as it:
                for r in range(FIN - 1):
                    finish(dve, it, r)

        @block.scalar
        def _(act):
            act.wait_ge(s_ld, 16 * NLD)
            act.activation(c_exp[:, :], c_in[:, :], ACT.Exp, scale=-1.0).then_inc(s_act0, 1)

            def modulate(u):
                act.wait_ge(s_pA, (CQ + 1) * u + 1)
                after(act, s_pB, (CQ + 1) * u)
                for b in range(CB):
                    act.activation(hT[:, b * S:(b + 1) * S], pP[0][:, b * S:(b + 1) * S], ACT.Identity,
                                   scale=scaleT[:, 0, bass.ds(CB * u + b, 1)],
                                   bias=shiftT[:, 0, bass.ds(CB * u + b, 1)]).then_inc(s_hT, 1)

            def round_piece(u, n, i):
                act.wait_ge(s_pB if n else s_pA, (CQ + 1) * u + 2 + i)
                act.activation(rounded[:, n, :, :].rearrange("p c n -> p (c n)"), pP[n][:, :],
                               ACT.Copy).then_inc(s_rk if n else s_rq, 1)

            def normalise(t, par):
                act.wait_ge(s_off, t + 1)
                after(act, s_pA, (CQ + 1) * (t - 1) + 1)
                for a in range(NT):
                    act.activation(xn[:, a, :], x_in[:, par, a, :], ACT.Identity, scale=rstd[:, a:a + 1],
                                   bias=mean_off[:, a:a + 1]).then_inc(s_xn, 1)

            normalise(0, 0)
            act.wait_ge(s_dve0, DVE_COLUMNS)
            modulate(0)
            normalise(1, 1)
            for i in range(CQ):
                round_piece(0, 0, i)
                round_piece(0, 1, i)

            def slot(it, g):
                G, T, s = BODY * it + g, 2 * it + g // CG, g % CG
                par = (g // CG) % 2
                B, j = GB * it + g // GB, g % GB
                b = (g // GB) % 2
                prep = live(T + 1, CHUNKS) and live(T, CHUNKS)
                batch = GB * it + (g - 4) // GB
                b4 = ((g - 4) // GB) % 2

                def exponentials(h):
                    act.wait_ge(s_s2, HG * (G - 2) + h + 1)
                    if h == 0:
                        after(act, s_pv, G - 3)
                    act.activation(probs[:, g % 2, h, :], pS2[h % 2][:, :], ACT.Exp).then_inc(s_exp, 1)

                if live(G - 1, GROUPS):
                    act.wait_ge(s_tm, G)
                    after(act, s_m[(g - 1) % 2], 16 * HG * (BODY // 2 * it + (g - 1) // 2))
                    act.copy(nshiftT[:, (g - 1) % 2, :], pB[0:HG * NBLK, 0:P]).then_inc(s_tmcp, 1)
                if live(G - 2, GROUPS):
                    exponentials(0)
                if live(G - 4, GROUPS):
                    act.wait_ge(s_to, G - 3)
                    if g % GB == 0:
                        after(act, s_fin, batch - 1)
                    act.copy(o_rows[:, b4, :, HG * (g % GB):HG * (g % GB) + HG, :],
                             pB[:, 0:NBLK * P].rearrange("p (k h m) -> p k h m", k=NBLK, h=HG)[:, :, :, 0:NV]).then_inc(s_tocp, 1)
                if j == 1 and live(B - 3, NB):
                    act.wait_ge(s_h2t, B - 2)
                    act.copy(h2T[:, :], pO[:, S:2 * S]).then_inc(s_h2c, 1)
                if prep and s - 1 in KEY_SLOTS:
                    round_piece(T + 1, 1, KEY_SLOTS.index(s - 1))
                if live(G - 2, GROUPS):
                    exponentials(1)
                if live(G - 2, GROUPS):
                    exponentials(2)
                if prep and s == 0:
                    modulate(T + 1)
                if prep and s in QUERY_SLOTS:
                    round_piece(T + 1, 0, QUERY_SLOTS.index(s))
                if live(G - 4, GROUPS) and j == 3:
                    act.wait_ge(s_mk, batch + 1)
                    after(act, s_f1, NBLK * (batch - 1))
                    act.copy(o_mask[:, b4, :, :, :].rearrange("p k h v -> p (k h v)"),
                             pB[:, 0:NBLK * H * NV]).then_inc(s_mkcp, 1)
                if live(G - 2, GROUPS):
                    exponentials(3)
                if live(G - 3, GROUPS):
                    act.wait_ge(s_pv, G - 2)
                    after(act, s_to, G - 4)
                    act.copy(oT[:, (g - 3) % 2, :], pO[:, 0:S]).then_inc(s_ot, 1)
                if j == 3 and live(B - 2, NB):
                    act.wait_ge(s_off2, B - 1)
                    after(act, s_h2, B - 2)
                    for k in range(NBLK):
                        act.activation(h2f[:, k, :], x_new[:, b, k, :], ACT.Identity, scale=rstd2[:, k:k + 1],
                                       bias=mean_off2[:, k:k + 1]).then_inc(s_n2, 1)
                if s == 6 and live(T + 2, CHUNKS):
                    normalise(T + 2, par)
                if j == 1 and live(B - 3, NB):
                    q = (g // GB - 3) % 2
                    act.copy(h2_rows[:, q, 1, :, 0:E], h2_rows[:, q, 0, :, 0:E]).then_inc(s_dup, 1)
                if j == 2 and live(B - 3, NB):
                    act.wait_ge(s_ein, B - 2)
                    act.activation(top_exp[:, :, :], top_arg[:, :, :], ACT.Exp).then_inc(s_eg, 1)
                if j == 1 and live(B - 1, NB):
                    act.wait_ge(s_earg, B)
                    act.activation(e_shift[:, (g // GB - 1) % 2, :], e_arg[:, (g // GB - 1) % 2, :], ACT.Exp).then_inc(s_e, 1)

            over_groups(act, slot)

            def expert_step(it, u):
                st = SU * it + u
                r = u % 2
                if live(st, STEPS):
                    for c in range(HC):
                        act.wait_ge(s_hid, HC * st + (c // 2 + 1) * 2)
                        if c == 0:
                            after(act, s_y, st - 1)
                        act.activation(hidT[:, r, c, :], hid_bank(r, c), ACT.Gelu,
                                       bias=w_ring[:, u, HID + c:HID + c + 1]).then_inc(s_gelu, 1)
                if live(st - 1, STEPS):
                    q = (u - 1) % 2
                    act.wait_ge(s_ysum, st)
                    after(act, s_ysc[q], 16 * NBLK * (SU // 2 * it + (u - 1) // 2))
                    for k in range(NBLK):
                        act.activation(y_out[:, q, k, :], y_sum[:, q, k, :], ACT.Copy,
                                       scale=row_gate[:, (u - 1) % SU, k:k + 1]).then_inc(s_yout, 1)

            over_steps(act, expert_step)

        @block.tensor
        def _(pe):
            pe.wait_ge(s_pool0, 4)
            pe.wait_ge(s_dve0, DVE_SILU)
            for n in range(3):
                pe.transpose(pP[0][:, n * P:(n + 1) * P], w_nat[:, n, :], ident[:, :])
            pe.transpose(pP[0][:, 3 * P:4 * P], c_in[:, :], ident[:, :]).then_inc(s_pe0, 1)
            pe.wait_ge(s_dve0, DVE_WEIGHTS)
            for half in range(2):
                pe.matmul(pP[half][0:NB, 0:3 * E], siluT[:, :], wmod_sb[:, 3 * half:3 * half + 3, :].rearrange("k m e -> k (m e)"),
                          start=True, stop=True)
            for half in range(2):
                for m in range(2):
                    last = pe.matmul(pB[:, (2 * half + m) * NB:(2 * half + m + 1) * NB], wmod_sb[:, 3 * half + m, :],
                                     siluT[:, :], start=True, stop=True)
            last.then_inc(s_pe0, 1)
            pe.wait_ge(s_dve0, DVE_COLUMNS)

            def tokens(u):
                pe.wait_ge(s_xn, NT * (u + 1))
                after(pe, s_q, CQ * u)
                for a in range(NT):
                    last = pe.transpose(pP[0][:, a * P:(a + 1) * P], xn[:, a, :], ident[:, :])
                last.then_inc(s_pA, 1)

            def values(u):
                pe.wait_ge(s_hT, CB * (u + 1))
                after(pe, s_k, CQ * u)
                for a in range(NT):
                    last = pe.matmul(pP[1][:, a * P:(a + 1) * P], hT[:, a * P:(a + 1) * P], wvT[:, :], start=True, stop=True)
                last.then_inc(s_pB, 1)

            def project(u, n, i):
                if n == 0:
                    pe.wait_ge(s_hT, CB * (u + 1))
                    after(pe, s_q, CQ * u + i)
                else:
                    pe.wait_ge(s_v, u + 1)
                    after(pe, s_k, CQ * u + i)
                pe.matmul(pP[n][:, :], bias_lhs[:, n, i, :], bias_ind[:, :, :].rearrange("p c n -> p (c n)"),
                          start=True, stop=False, skip_group_check=True)
                heads = hT[:, :].rearrange("p (g h r) -> p h g r", h=HG, r=R)
                for c in range(4):
                    for h in range(HG):
                        last = pe.matmul(pP[n][SLOT * h:SLOT * h + SLOT, c * P:(c + 1) * P].rearrange("p (g r) -> p g r", r=R),
                                         w_slot[:, n, 4 * i + c, :], heads[:, h], start=False, stop=(c == 3),
                                         skip_group_check=True)
                last.then_inc(s_pB if n else s_pA, 1)

            tokens(0)
            values(0)
            pe.wait_ge(s_dve0, DVE_BIAS)
            for i in range(CQ):
                project(0, 0, i)
                project(0, 1, i)
            pe.wait_ge(s_late, 32)
            pe.wait_ge(s_q, CQ)
            pe.transpose(pP[0][:, 0:NE * HC], b1_rows[:, :], ident[0:NE * HC, 0:NE * HC])
            pe.transpose(pP[0][:, NE * HC:NE * HC + NE], wg_rows[:, :], ident[0:NE, 0:NE]).then_inc(s_pe0, 1)
            pe.wait_ge(s_dve0, DVE_LATE)
            pe.wait_ge(s_pool0, 17)

            def slot(it, g):
                G, T, s = BODY * it + g, 2 * it + g // CG, g % CG
                B, j = GB * it + g // GB, g % GB
                par = (g // CG) % 2
                prep = live(T + 1, CHUNKS) and live(T, CHUNKS)

                def scores(h):
                    if s == 0 and h == 0:
                        pe.wait_ge(s_qb, 16 * HG * (T + 1))
                        pe.wait_ge(s_k, CQ * (T + 1))
                    after(pe, s_red, HG * G + h - 1)
                    for k in range(NBLK):
                        pe.matmul(pS1[h % 2][:, k * S:(k + 1) * S], q_diag[:, par, s, h, k * P:(k + 1) * P],
                                  k_pack[:, par, s, :], start=True, stop=False, skip_group_check=True)
                    pe.matmul(pS1[h % 2][:, P:P + NBLK * P], identb[:, :], neg[:, :, :].rearrange("p k j -> p (k j)"),
                              start=False, stop=True, skip_group_check=True).then_inc(s_s1, 1)

                def shifted_scores(h):
                    g2 = (g - 2) % BODY
                    if h == 0:
                        pe.wait_ge(s_m[g % 2], 16 * HG * (BODY // 2 * it + (g - 2) // 2 + 1))
                    after(pe, s_exp, HG * (G - 2) + h - 1)
                    for k in range(NBLK):
                        last = pe.matmul(pS2[h % 2][:, k * S:(k + 1) * S], k_pack[:, g2 // CG, g2 % CG, k * P:(k + 1) * P],
                                         q_diag[:, g2 // CG, g2 % CG, h, :], start=True, stop=True)
                    last.then_inc(s_s2, 1)

                def weigh_values():
                    if live(B - 3, NB):
                        if j == 1:
                            pe.wait_ge(s_h2c, B - 2)
                        if j == 2:
                            pe.wait_ge(s_lgc, B - 2)
                        if j == 3:
                            pe.wait_ge(s_pos, 2 * (B - 2))
                    if live(G - 3, GROUPS):
                        g3 = (g - 3) % BODY
                        pe.wait_ge(s_aff, 2 * (G - 2))
                        after(pe, s_ot, G - 3)
                        if g3 % CG == 0:
                            pe.wait_ge(s_vr, 32 * (2 * it + (g - 3) // CG + 1))
                        for k in range(NBLK):
                            for h in range(HG):
                                last = pe.matmul(pO[SLOT * h:SLOT * h + SLOT, 0:S], v_slot[:, g3 // CG, k, g3 % CG, h, :],
                                                 probs[:, (g - 3) % 2, h, k * S:(k + 1) * S], start=(k == 0), stop=(k == 1))
                        last.then_inc(s_pv, 1)

                if live(G, GROUPS):
                    scores(0)
                if live(G - 1, GROUPS):
                    pe.wait_ge(s_nm, G)
                    after(pe, s_tocp, G - 4)
                    if isinstance(G, int) and G < 5:
                        after(pe, s_tmcp, G - 1)
                    if j == 0:
                        after(pe, s_mkcp, B - 1)
                    pe.transpose(pB[0:HG * NBLK, 0:P],
                                 nshift[:, ((g - 1) // GB) % 4, (g - 1) % GB, :, :].bitcast(F32).rearrange("p h k -> p (h k)"),
                                 ident[:, :]).then_inc(s_tm, 1)
                if live(G - 2, GROUPS):
                    shifted_scores(0)
                if live(G, GROUPS):
                    scores(1)
                after(pe, s_ot, min(G - 3, GROUPS) if isinstance(G, int) else G - 3)
                if j == 1 and live(B - 3, NB):
                    pe.wait_ge(s_h2, B - 2)
                    for k in range(NBLK):
                        last = pe.transpose(pO[:, S + k * P:S + (k + 1) * P], h2_rows[:, (g // GB - 3) % 2, 0, k, 0:E],
                                            ident[:, :])
                    last.then_inc(s_h2t, 1)
                if j == 2 and live(B - 3, NB):
                    pe.wait_ge(s_h2c, B - 2)
                    for k in range(NBLK):
                        last = pe.matmul(pO[:, S + k * NE:S + (k + 1) * NE], h2T[:, k * P:(k + 1) * P], wgT[:, :],
                                         start=True, stop=True)
                    last.then_inc(s_lg, 1)
                if j == 3 and live(B - 3, NB):
                    pe.wait_ge(s_ch, B - 2)
                    first, second = chosen_b[:, 0, :], chosen_b[:, 1, :]
                    pre = [pO[:, S + n * NE:S + (n + 1) * NE] for n in range(NBLK + 1)]
                    pe.matmul(pre[0], before_b[:, :], first, start=True, stop=True)
                    pe.matmul(pre[1], before_b[:, :], second, start=True, stop=False)
                    pe.matmul(pre[1], ones_b[:, :], first, start=False, stop=True)
                    pe.matmul(pre[2], ones_b[:, :], first, start=True, stop=False)
                    pe.matmul(pre[2], ones_b[:, :], second, start=False, stop=True).then_inc(s_pre, 1)
                if live(G - 2, GROUPS):
                    shifted_scores(1)
                if live(G - 4, GROUPS):
                    pe.wait_ge(s_ot, G - 3)
                    after(pe, s_tmcp, min(G, GROUPS) if isinstance(G, int) else G)
                    if not live(G - 1, GROUPS):
                        pe.wait_ge(s_tocp, G - 4)
                        if j == 0:
                            pe.wait_ge(s_mkcp, B - 1)
                    for k in range(NBLK):
                        last = pe.transpose(pB[:, k * P:(k + 1) * P], oT[:, (g - 4) % 2, k * P:(k + 1) * P], ident[:, :])
                    last.then_inc(s_to, 1)
                if live(G, GROUPS):
                    scores(2)
                if live(G - 2, GROUPS):
                    shifted_scores(2)
                if j == 3 and live(B - 1, NB):
                    g4 = (g - 7) % BODY
                    after(pe, s_tmcp, min(G, GROUPS) if isinstance(G, int) else G)
                    pe.wait_ge(s_tocp, G - 3)
                    for k in range(NBLK):
                        heads = v_slot[:, g4 // CG, 1 - k, g4 % CG:g4 % CG + GB, :, 0:NV].rearrange("p g h v -> p (g h) v")
                        last = pe.matmul(pB[:, k * H * NV:(k + 1) * H * NV].rearrange("p (h v) -> p h v", v=NV),
                                         tri[:, k, :], heads, start=True, stop=True)
                    last.then_inc(s_mk, 1)
                if prep and s == 0:
                    tokens(T + 1)
                if prep and s in QUERY_SLOTS:
                    project(T + 1, 0, QUERY_SLOTS.index(s))
                if s in KEY_SLOTS or s == 0:
                    weigh_values()
                if live(G, GROUPS):
                    scores(3)
                if live(G - 2, GROUPS):
                    shifted_scores(3)
                if prep and s == 0:
                    values(T + 1)
                if prep and s in KEY_SLOTS:
                    project(T + 1, 1, KEY_SLOTS.index(s))
                if s not in KEY_SLOTS and s != 0:
                    weigh_values()

            over_groups(pe, slot)

            def turn(st, r, n):
                pe.wait_ge(s_xs[r], 16 * (n + 1))
                after(pe, s_xtc, st)
                for k in range(NBLK):
                    last = pe.transpose(pB[:, k * P:(k + 1) * P], xs[:, r, k, 0:E], ident[:, :])
                last.then_inc(s_xt, 1)

            turn(0, 0, 0)

            def expert_step(it, u):
                st = SU * it + u
                r = u % 2

                def hidden(c):
                    if c == 0:
                        pe.wait_ge(s_w, st + 1)
                        pe.wait_ge(s_xtc, st + 1)
                        after(pe, s_gelu, HC * (st - 1))
                    pe.matmul(hid_bank(r, c), w_ring[:, u, c * P:(c + 1) * P], xsT[:, r, :],
                              start=True, stop=True).then_inc(s_hid, 1)

                if live(st, STEPS):
                    hidden(0)
                    hidden(1)
                if live(st + 1, STEPS):
                    turn(st + 1, (u + 1) % SU, it + (u + 1) // SU)
                if live(st, STEPS):
                    hidden(2)
                    hidden(3)
                if live(st - 1, STEPS):
                    q = (u - 1) % 2
                    pe.wait_ge(s_gelu, HC * st)
                    after(pe, s_ysum, st - 1)
                    for k in range(NBLK):
                        for c in range(HC):
                            w = w_ring[:, (u - 1) % SU, HID + HC + c * E:HID + HC + (c + 1) * E]
                            last = pe.matmul(pO[:, k * E:(k + 1) * E], hidT[:, q, c, k * P:(k + 1) * P], w,
                                             start=(c == 0), stop=(c == HC - 1))
                    last.then_inc(s_y, 1)

            over_steps(pe, expert_step)


_INS = ["L0_attn_x", "L0_attn_Wq", "L0_attn_bq", "L0_attn_Wk", "L0_attn_bk", "L0_attn_Wv", "L0_attn_bv",
        "L0_ffn_w_gate", "L0_ffn_W1", "L0_ffn_b1", "L0_ffn_W2", "L0_ffn_b2", "L0_c", "L0_wmod"]
_OUTS = [((NB, S, E), "float32")]


def kernel(**inputs):
    import numpy as _np
    import concourse.bacc as _bacc
    from concourse import mybir as _mybir
    from concourse.bass_utils import run_bass_kernel_spmd as _run

    nc = _bacc.Bacc("TRN2", target_bir_lowering=False, num_devices=1)
    arrays, args = {}, []
    for name in _INS:
        a = _np.ascontiguousarray(inputs[name])
        arrays[f"in_{name}_dram"] = a
        args.append(nc.dram_tensor(f"in_{name}_dram", a.shape, _mybir.dt.from_np(a.dtype), kind="ExternalInput").ap())
    for i, (shape, dtype) in enumerate(_OUTS):
        dt = _mybir.dt.from_np(_np.dtype(dtype))
        args.append(nc.dram_tensor(f"out_{i}_dram", shape, dt, kind="ExternalOutput").ap())
    build(nc, *args)
    r = _run(nc, [arrays], core_ids=[0])
    return r.results[0]["out_0_dram"]
```
